# Optimizing a Trainium2 kernel written in Bass

```python
import numpy as np
import jax
import jax.numpy as jnp

def _softmax(x, axis=-1):
    return jax.nn.softmax(x, axis=axis)

def _gelu(x):
    return jax.nn.gelu(x, approximate=True)

def _silu(x):
    return jax.nn.silu(x)

def _sigmoid(x):
    return jax.nn.sigmoid(x)

def _layernorm(x, axis=-1, eps=1e-05):
    m = jnp.mean(x, axis=axis, keepdims=True)
    v = jnp.var(x, axis=axis, keepdims=True)
    return (x - m) / jnp.sqrt(v + eps)

def _scatter_add(tgt, idx, src, axis=0):
    return tgt.at[idx].add(src)

def _segment_sum(src, seg, n):
    return jax.ops.segment_sum(src, seg, n)
kernel_name = 'mk_gnn_resnorm_d4_gnn_r32_1004f0'

def setup_inputs(seed: int=0):
    np.random.seed(seed)
    _w = jnp.asarray

    def _rec_inputs():
        import jax
        import jax.numpy as jnp
        _gk = jax.random.key(seed)
        x = -8.776e-05 + 1 * jax.random.normal(jax.random.fold_in(_gk, 1), (10000, 512), jnp.float32)
        src = jax.random.randint(jax.random.fold_in(_gk, 2), (5000,), 0, 10000, jnp.int32)
        dst = jnp.minimum((10000 * jax.random.uniform(jax.random.fold_in(_gk, 3), (5000,)) ** 2.0).astype(jnp.int32), 9999)
        _o = jnp.argsort(dst, stable=True)
        src = src[_o]
        dst = dst[_o]
        edge_weight = jax.random.uniform(jax.random.fold_in(_gk, 14), (5000,), jnp.float32, 0.0, 0.999994)
        return (x, src, dst, edge_weight)
    x, src, dst, edge_weight = _rec_inputs()

    def _L0_gnn_setup():
        import jax, jax.numpy as jnp
        import numpy as np
        N_NODES = 10000
        N_EDGES = 5000
        DIM = 512
        LN_EPS = 1e-05
        key = jax.random.key(seed)
        ks = jax.random.split(key, 6)
        scale = 1.0 / np.sqrt(DIM)
        h = jax.random.normal(ks[0], (N_NODES, DIM), dtype=jnp.float32)
        edge_index = jax.random.randint(ks[1], (2, N_EDGES), 0, N_NODES, dtype=jnp.int32)
        W_self = jax.random.normal(ks[2], (DIM, DIM), dtype=jnp.float32) * scale
        b_self = jnp.zeros((DIM,), dtype=jnp.float32)
        W_neigh = jax.random.normal(ks[3], (DIM, DIM), dtype=jnp.float32) * scale
        b_neigh = jnp.zeros((DIM,), dtype=jnp.float32)
        ln_gamma = jnp.ones((DIM,), dtype=jnp.float32)
        ln_beta = jnp.zeros((DIM,), dtype=jnp.float32)
        return {'h': h, 'edge_index': edge_index, 'W_self': W_self, 'b_self': b_self, 'W_neigh': W_neigh, 'b_neigh': b_neigh, 'ln_gamma': ln_gamma, 'ln_beta': ln_beta}
    _L0_gnn_all = _L0_gnn_setup()
    _L0_gnn_in = {k: v for k, v in _L0_gnn_all.items() if k in ('W_self', 'b_self', 'W_neigh', 'b_neigh', 'ln_gamma', 'ln_beta')}
    del _L0_gnn_all

    def _L1_gnn_setup():
        import jax, jax.numpy as jnp
        import numpy as np
        N_NODES = 50000
        DIM = 512
        N_EDGES = 5000
        key = jax.random.key(seed)
        k_x, k_e, k_ws, k_bs, k_wn, k_bn = jax.random.split(key, 6)
        scale = 1.0 / np.sqrt(DIM)
        return {'x': jax.random.normal(k_x, (N_NODES, DIM), dtype=jnp.float32), 'edge_index': jax.random.randint(k_e, (2, N_EDGES), 0, N_NODES, dtype=jnp.int64), 'self_w': jax.random.uniform(k_ws, (DIM, DIM), jnp.float32, -scale, scale), 'self_b': jax.random.uniform(k_bs, (DIM,), jnp.float32, -scale, scale), 'neigh_w': jax.random.uniform(k_wn, (DIM, DIM), jnp.float32, -scale, scale), 'neigh_b': jax.random.uniform(k_bn, (DIM,), jnp.float32, -scale, scale)}
    _L1_gnn_all = _L1_gnn_setup()
    _L1_gnn_in = {k: v for k, v in _L1_gnn_all.items() if k in ('self_w', 'self_b', 'neigh_w', 'neigh_b')}
    del _L1_gnn_all

    def _L2_gnn_setup():
        import jax, jax.numpy as jnp
        import numpy as np
        N_NODES = 625
        N_EDGES = 5000
        N_IN = 512
        N_OUT = 512
        key = jax.random.key(seed)
        k1, k2, k3, k4, k5 = jax.random.split(key, 5)
        x = jax.random.normal(k1, (N_NODES, N_IN), dtype=jnp.float32)
        vals = jax.random.uniform(k2, (N_EDGES,), dtype=jnp.float32)
        bound = 1.0 / np.sqrt(N_IN)
        weight = jax.random.uniform(k3, (N_OUT, N_IN), minval=-bound, maxval=bound, dtype=jnp.float32)
        row = jax.random.randint(k4, (N_EDGES,), 0, N_NODES, dtype=jnp.int32)
        col = jax.random.randint(k5, (N_EDGES,), 0, N_NODES, dtype=jnp.int32)
        return {'x': x, 'vals': vals, 'weight': weight, 'row': row, 'col': col}
    _L2_gnn_all = _L2_gnn_setup()
    _L2_gnn_in = {k: v for k, v in _L2_gnn_all.items() if k in ('weight',)}
    del _L2_gnn_all

    def _L3_gnn_setup():
        import jax, jax.numpy as jnp
        import numpy as np
        N = 625
        E = 250000
        B = 128
        Fin = 512
        Fqk = 512
        Fv = 512
        H = 8
        key = jax.random.key(seed)
        k1, k2, k3, k4 = jax.random.split(key, 4)
        x = jax.random.normal(k1, (N, Fin), dtype=jnp.float32)
        batch = jnp.sort(jax.random.randint(k2, (N,), 0, B)).astype(jnp.int32)
        ei = jax.random.randint(k3, (2, E), 0, N).astype(jnp.int32)
        W = jax.random.normal(k4, (Fin, 2 * Fqk + Fv), dtype=jnp.float32) / np.sqrt(Fin).astype(np.float32)
        return {'x': x, 'batch': batch, 'ei': ei, 'W': W}
    _L3_gnn_all = _L3_gnn_setup()
    _L3_gnn_in = {k: v for k, v in _L3_gnn_all.items() if k in ('W',)}
    del _L3_gnn_all
    return {'x': x, 'src': src, 'dst': dst, 'edge_weight': edge_weight, 'L0_gnn_W_self': _L0_gnn_in['W_self'], 'L0_gnn_b_self': _L0_gnn_in['b_self'], 'L0_gnn_W_neigh': _L0_gnn_in['W_neigh'], 'L0_gnn_b_neigh': _L0_gnn_in['b_neigh'], 'L0_gnn_ln_gamma': _L0_gnn_in['ln_gamma'], 'L0_gnn_ln_beta': _L0_gnn_in['ln_beta'], 'L1_gnn_self_w': _L1_gnn_in['self_w'], 'L1_gnn_self_b': _L1_gnn_in['self_b'], 'L1_gnn_neigh_w': _L1_gnn_in['neigh_w'], 'L1_gnn_neigh_b': _L1_gnn_in['neigh_b'], 'L2_gnn_weight': _L2_gnn_in['weight'], 'L3_gnn_W': _L3_gnn_in['W']}

def reference(x, src, dst, edge_weight, L0_gnn_W_self, L0_gnn_b_self, L0_gnn_W_neigh, L0_gnn_b_neigh, L0_gnn_ln_gamma, L0_gnn_ln_beta, L1_gnn_self_w, L1_gnn_self_b, L1_gnn_neigh_w, L1_gnn_neigh_b, L2_gnn_weight, L3_gnn_W):
    import jax
    import jax.numpy as jnp

    def _L0_gnn_ref(h, edge_index, W_self, b_self, W_neigh, b_neigh, ln_gamma, ln_beta):
        import jax, jax.numpy as jnp
        import numpy as np
        N_NODES = 10000
        N_EDGES = 5000
        DIM = 512
        LN_EPS = 1e-05
        n = h.shape[0]
        src = edge_index[0]
        dst = edge_index[1]
        msg = h[dst] @ W_neigh.T + b_neigh
        neigh = jax.ops.segment_sum(msg, src, num_segments=n)
        deg = jax.ops.segment_sum(jnp.ones(src.shape, h.dtype), src, num_segments=n)
        deg = jnp.maximum(deg, 1.0)
        neigh = neigh / deg[:, None]
        out = jax.nn.relu(h @ W_self.T + b_self + neigh)
        x = h + out
        mean = jnp.mean(x, axis=-1, keepdims=True)
        var = jnp.mean(jnp.square(x - mean), axis=-1, keepdims=True)
        return (x - mean) * jax.lax.rsqrt(var + LN_EPS) * ln_gamma + ln_beta

    def _L1_gnn_ref(x, edge_index, self_w, self_b, neigh_w, neigh_b):
        import jax, jax.numpy as jnp
        import numpy as np
        N_NODES = 50000
        DIM = 512
        N_EDGES = 5000
        row, col = (edge_index[0], edge_index[1])
        agg = jax.ops.segment_sum(x[col], row, num_segments=x.shape[0])
        out = jnp.dot(x, self_w.T) + self_b + jnp.dot(agg, neigh_w.T) + neigh_b
        return jax.nn.relu(out)

    def _L2_gnn_ref(x, vals, weight, row, col):
        import jax, jax.numpy as jnp
        import numpy as np
        N_NODES = 625
        N_EDGES = 5000
        N_IN = 512
        N_OUT = 512
        n = x.shape[0]
        msgs = x[col] * vals[:, None]
        agg = jax.ops.segment_sum(msgs, row, num_segments=n)
        return jnp.einsum('nd,od->no', agg, weight)

    def _L3_gnn_ref(x, batch, ei, W):
        import jax, jax.numpy as jnp
        import numpy as np
        N = 625
        E = 250000
        B = 128
        Fin = 512
        Fqk = 512
        Fv = 512
        H = 8
        src, dest = (ei[0], ei[1])
        n = x.shape[0]
        Fh = Fqk // H
        Fhv = Fv // H
        scaling = float(Fh) ** (-0.5)
        qkv = x @ W
        q, k, v = jnp.split(qkv, [Fqk, 2 * Fqk], axis=-1)
        q = (q * scaling).reshape(n, H, Fh)
        k = k.reshape(n, H, Fh)
        v = v.reshape(n, H, Fhv)
        qs = q[src]
        ks = k[dest]
        vs = v[dest]
        aw = jnp.einsum('ehf,ehf->eh', qs, ks)
        m = jax.ops.segment_max(aw, src, num_segments=n)
        e = jnp.exp(aw - m[src])
        denom = jax.ops.segment_sum(e, src, num_segments=n)
        alpha = e / denom[src]
        out = jax.ops.segment_sum(alpha[:, :, None] * vs, src, num_segments=n)
        return out.reshape(n, Fv)
    edge_index = jnp.stack([src, dst])
    batch0 = jnp.zeros((10000,), jnp.int32)
    x = _layernorm(x + _L0_gnn_ref(x, edge_index, L0_gnn_W_self, L0_gnn_b_self, L0_gnn_W_neigh, L0_gnn_b_neigh, L0_gnn_ln_gamma, L0_gnn_ln_beta), axis=-1)
    x = _layernorm(x + _L1_gnn_ref(x, edge_index, L1_gnn_self_w, L1_gnn_self_b, L1_gnn_neigh_w, L1_gnn_neigh_b), axis=-1)
    x = _layernorm(x + _L2_gnn_ref(x, edge_weight, L2_gnn_weight, src, dst), axis=-1)
    x = _layernorm(x + _L3_gnn_ref(x, batch0, edge_index, L3_gnn_W), axis=-1)
    return x

_drawn_inputs = setup_inputs


def setup_inputs(seed=0):
    import zlib

    import numpy as np

    out = dict(_drawn_inputs(seed))
    spreads = {'L0_gnn_b_self': (0.0, 0.1),
     'L0_gnn_b_neigh': (0.0, 0.538),
     'L0_gnn_ln_gamma': (1.0, 0.2),
     'L0_gnn_ln_beta': (0.0, 0.1)}
    factors = {'L1_gnn_self_b': 3.779, 'L1_gnn_neigh_b': 3.494}
    for name, (base, spread) in spreads.items():
        noise = np.random.default_rng([zlib.crc32(name.encode()), seed]).standard_normal(out[name].shape)
        drawn = base * np.exp(spread * noise) if base else spread * noise
        out[name] = jnp.asarray(drawn.astype(out[name].dtype))
    for name, factor in factors.items():
        out[name] = (out[name] * factor).astype(out[name].dtype)
    return out
```

```python
from contextlib import ExitStack

import concourse.bass as bass
from concourse import mybir

F32 = mybir.dt.float32
F32R = mybir.dt.float32r
BF16 = mybir.dt.bfloat16
I32 = mybir.dt.int32
ALU = mybir.AluOpType
ACT = mybir.ActivationFunctionType
AX_X = mybir.AxisListType.X

P = 128
UNROLL = 4


class Tile:

    def __init__(self, loop, offset):
        self.loop, self.offset = loop, offset
        self.slot = offset % UNROLL
        self.half = offset % 2

    def times(self, size, add=0):
        if isinstance(self.loop, int):
            return self.offset * size + add
        return self.loop * (UNROLL * size) + (self.offset * size + add)

    def turn(self, size):
        whole = (self.offset // UNROLL + 1) * size
        return whole if isinstance(self.loop, int) else self.loop * size + whole

    def has(self, back):
        return not isinstance(self.loop, int) or self.offset >= back


class Count:

    def __init__(self, sem, per=1):
        self.sem, self.per, self.base = sem, per, 0

    def upto(self, tile, back=0):
        return tile.times(self.per, self.base + self.per * (1 - back))

    def all(self, n):
        return self.base + self.per * n

    def close(self, n):
        self.base += self.per * n


class Slots:

    def __init__(self, sems):
        self.sems, self.bases = sems, [0] * UNROLL

    def sem(self, tile):
        return self.sems[tile.slot]

    def landed(self, tile, back=0):
        return tile.turn(16) + (self.bases[tile.slot] - 16 * back)

    def used(self, n):
        return [(self.sems[k], self.bases[k] + 16 * len(range(k, n, UNROLL))) for k in range(UNROLL)]

    def close(self, n):
        self.bases = [v for _, v in self.used(n)]


def in_steps(eng, n, stages):
    deepest = max(lag for lag, _ in stages)
    first = -(-(deepest + UNROLL) // UNROLL)
    last = n // UNROLL

    def straight(steps):
        for s in steps:
            for lag, stage in stages:
                if 0 <= s - lag < n:
                    stage(Tile(0, s - lag))

    if last - first < 2:
        straight(range(n + deepest))
        return
    straight(range(first * UNROLL))
    with eng.Fori(first, last) as i:
        for j in range(UNROLL):
            for lag, stage in stages:
                stage(Tile(i, j - lag))
    straight(range(last * UNROLL, n + deepest))


def build(nc, x, src, dst, edge_weight, w_self0, b_self0, w_neigh0, b_neigh0, gamma, beta,
          w_self1, b_self1, w_neigh1, b_neigh1, w_neigh2, w_qkv, out):
    N, D = x.shape
    E = src.shape[0]
    DC = D // P
    NT = -(-N // P)
    NREST = N - (NT - 1) * P
    ET = -(-E // P)
    EP = ET * P
    ER = E // ET
    HEADS = 8
    FH = D // HEADS
    PAD_NODE = NT * P - 1
    NOWHERE = 4 * EP
    EPS = 1e-5
    BIG = 3.0e38
    assert ER * ET == E and ER <= P and PAD_NODE >= N and D == DC * P and NT <= P and NT * P < 32768

    records = nc.dram_tensor("records", [EP + 1, 4], F32, kind="Internal").ap()
    same_run_row = nc.dram_tensor("same_run_row", [1, EP], BF16, kind="Internal").ap()
    sorted_src_row = nc.dram_tensor("sorted_src_row", [1, EP + 1], F32, kind="Internal").ap()
    neigh_rows = nc.dram_tensor("neigh_rows", [EP + 1, D], F32, kind="Internal").ap()
    values = [nc.dram_tensor(f"values{i}", [N, D], F32, kind="Internal").ap() for i in range(3)]

    ctx = ExitStack()
    with ctx:
        def sb(name, shape, dt, where=ctx):
            return where.enter_context(nc.sbuf_tensor(name, shape, dt))

        def pb(name, shape, dt, where):
            return where.enter_context(nc.psum_tensor(name, shape, dt))

        def sem(name):
            return ctx.enter_context(nc.semaphore(name))

        def slots(name):
            return Slots([sem(f"{name}{k}") for k in range(UNROLL)])

        ident = sb("ident", [P, P], F32)
        src_at = sb("src_at", [P, ET], F32)
        dst_idx = sb("dst_idx", [P, ET], I32)
        src_idx = sb("src_idx", [P, ET], I32)
        weight_at = sb("weight_at", [P, ET], F32)
        invdeg_at = sb("invdeg_at", [P, ET], F32)
        node_idx = sb("node_idx", [P, NT], I32)
        eps = sb("eps", [P, 1], F32)
        same_run = sb("same_run", [P, EP], BF16)
        w_hi = [sb(f"w_hi{k}", [P, DC, D], F32R) for k in range(3)]
        w_lo = [sb(f"w_lo{k}", [P, DC, D], F32R) for k in range(3)]

        pool_steps = sem("pool_steps")
        weight_landed = sem("weight_landed")
        weight_hi_done = sem("weight_hi_done")
        weight_lo_done = sem("weight_lo_done")
        weights_split = [0]

        def weight_split_steps(where, jobs):
            stage = sb(f"w_stage_{weights_split[0]}", [P, len(jobs), DC, D], F32, where)
            base = weights_split[0]
            weights_split[0] += len(jobs)

            def load(sp):
                for k, (w, _) in enumerate(jobs):
                    sp.dma_start(stage[:, k], w.rearrange("(c p) n -> p c n", p=P)).then_inc(weight_landed, 16)

            def high(act):
                act.wait_ge(weight_landed, 16 * (base + len(jobs)))
                for k, (_, slot) in enumerate(jobs):
                    nc.scalar.activation(w_hi[slot][:], stage[:, k], ACT.Copy).then_inc(weight_hi_done, 1)

            def low(dve):
                for k, (_, slot) in enumerate(jobs):
                    dve.wait_ge(weight_hi_done, base + k + 1)
                    nc.vector.tensor_tensor(w_lo[slot][:], stage[:, k], w_hi[slot][:].bitcast(F32),
                                            ALU.subtract).then_inc(weight_lo_done, 1)

            return load, high, low

        with ExitStack() as ph:
            edge_ints = sb("edge_ints", [P, 2, ET], I32, ph)
            weight_in = sb("weight_in", [P, ET], F32, ph)
            src_all_i = sb("src_all_i", [P, E], I32, ph)
            src_all = sb("src_all", [P, EP], F32, ph)
            rec = sb("rec", [P, ET, 4], F32, ph)
            hi_i = sb("hi_i", [P, ET], I32, ph)
            lo_i = sb("lo_i", [P, ET], I32, ph)
            hi_of = sb("hi_of", [P, ET], F32, ph)
            lo_of = sb("lo_of", [P, ET], F32, ph)
            iota_i = sb("iota_i", [P, P], I32, ph)
            iota_part_i = sb("iota_part_i", [P, 1], I32, ph)
            iota = sb("iota", [P, P], F32, ph)
            iota_part = sb("iota_part", [P, 1], F32, ph)
            ident_b = sb("ident_b", [P, P], BF16, ph)
            earlier = sb("earlier", [P, P], F32, ph)
            below = sb("below", [P, P], F32, ph)
            ones_row = sb("ones_row", [P, P], F32, ph)
            hot_lo = sb("hot_lo", [P, ET * P], BF16, ph)
            hot_hi = sb("hot_hi", [P, ET * P], BF16, ph)
            hist = sb("hist", [P, (ET + 1) * P], F32, ph)
            prefix = sb("prefix", [P, P], F32, ph)
            row_offset = sb("row_offset", [P, 1], F32, ph)
            row_offset1 = sb("row_offset1", [P, 1], F32, ph)
            base = sb("base", [P, P], F32, ph)
            empty = sb("empty", [P, P], F32, ph)
            last_pos = sb("last_pos", [P, P], F32, ph)
            table = sb("table", [P, 2, 2 * P], F32, ph)
            hot_hi_t = sb("hot_hi_t", [P, 2, P], F32, ph)
            rank_a = sb("rank_a", [P, ET], F32, ph)
            rank_b = sb("rank_b", [P, ET], F32, ph)
            rank_i = sb("rank_i", [P, ET], I32, ph)
            junk = sb("junk_prep", [P, 3, P], F32, ph)
            cur_rank = sb("cur_rank", [P, UNROLL], I32, ph)
            cur_rec = sb("cur_rec", [P, UNROLL, 4], F32, ph)
            guard = sb("guard", [1, 4], F32, ph)
            back = sb("back", [ET, P + 1, 4], F32, ph)
            same_t = sb("same_t", [ET, P], BF16, ph)
            src_t = sb("src_t", [ET, P], F32, ph)
            col_t = sb("col_t", [ET, 3, P], F32, ph)
            p_hist = [pb(f"p_hist{k}", [P, P], F32, ph) for k in range(2)]
            p_hot = [pb(f"p_hot{k}", [P, P], BF16, ph) for k in range(2)]
            p_look = [pb(f"p_look{k}", [P, 2 * P], F32, ph) for k in range(2)]
            p_misc = pb("p_misc", [P, 512], F32, ph)

            edges_in = sem("edges_in")
            edge_clear = sem("edge_clear")
            iotas = sem("iotas")
            consts = sem("consts")
            fields = sem("fields")
            hot_done = Count(sem("hot_done"))
            hist_mm = Count(sem("hist_mm"))
            hist_sum = Count(sem("hist_sum"))
            chain = sem("prep_chain")
            prefix_done = sem("prefix_done")
            last_pos_done = sem("last_pos_done")
            offsets_mm = sem("offsets_mm")
            nodes_mm = sem("nodes_mm")
            table_done = Count(sem("table_done"))
            hot_turned = Count(sem("hot_turned"))
            hot_copied = Count(sem("hot_copied"))
            looked = Count(sem("looked"))
            ranked = Count(sem("ranked"))
            ranks_ready = sem("ranks_ready")
            picked = Count(sem("picked"), 2)
            scattered = slots("scattered")
            guard_out = sem("guard_out")
            back_in = sem("back_in")
            rows_ready = sem("rows_ready")
            rows_out = sem("rows_out")
            rows_in = sem("rows_in")
            cols_mm = sem("cols_mm")
            cols_ready = sem("cols_ready")
            w_load, w_high, w_low = weight_split_steps(ph, [(w_neigh0, 0), (w_self0, 1)])
            block = ph.enter_context(nc.Block())

            @block.sync
            def _(sp):
                sp.wait_ge(edge_clear, 1)
                sp.dma_start(edge_ints[0:ER, 0, :], src.rearrange("(p t) -> p t", t=ET)).then_inc(edges_in, 16)
                sp.dma_start(edge_ints[0:ER, 1, :], dst.rearrange("(p t) -> p t", t=ET)).then_inc(edges_in, 16)
                sp.dma_start(weight_in[0:ER, :], edge_weight.rearrange("(p t) -> p t", t=ET)).then_inc(edges_in, 16)
                sp.dma_start(src_all_i[:], src.partition_broadcast(P)).then_inc(edges_in, 16)
                w_load(sp)
                sp.wait_ge(edge_clear, 2)
                sp.dma_start(records[0:1, :], guard[:]).then_inc(guard_out, 16)
                sp.wait_ge(guard_out, 16)
                for s, v in scattered.used(ET):
                    sp.wait_ge(s, v)
                for t in range(0, ET, 8):
                    sp.dma_start(back[t:t + 8], bass.AP(records.tensor, 4 * P * t, [[4 * P, 8], [1, 4 * (P + 1)]])
                                 .rearrange("t (l f) -> t l f", f=4)).then_inc(back_in, 16)
                sp.wait_ge(rows_ready, 2)
                sp.dma_start(same_run_row.rearrange("o (t l) -> (o t) l", l=P), same_t[:]).then_inc(rows_out, 16)
                sp.dma_start(sorted_src_row[:, 1:EP + 1].rearrange("o (t l) -> (o t) l", l=P), src_t[:])\
                    .then_inc(rows_out, 16)
                sp.dma_start(sorted_src_row[:, 0:1], guard[:, 0:1]).then_inc(rows_out, 16)
                sp.wait_ge(rows_out, 48)
                sp.dma_start(same_run[:], same_run_row[0, :].partition_broadcast(P)).then_inc(rows_in, 16)
                sp.wait_ge(rows_in, 16)

            @block.gpsimd
            def _(pool):
                nc.gpsimd.iota(iota_i[:], [[1, P]], base=0, channel_multiplier=0).then_inc(iotas, 1)
                nc.gpsimd.iota(iota_part_i[:], [[0, 1]], base=0, channel_multiplier=1).then_inc(iotas, 1)

                def pick(t):
                    pool.wait_ge(ranks_ready, 1)
                    if t.has(UNROLL):
                        pool.wait_ge(scattered.sem(t), scattered.landed(t, 1))
                    nc.gpsimd.tensor_copy(cur_rank[:, t.slot:t.slot + 1], rank_i[:, bass.ds(t.times(1), 1)])\
                        .then_inc(picked.sem, 1)
                    nc.gpsimd.tensor_copy(cur_rec[:, t.slot, :], rec[:, bass.ds(t.times(1), 1), :])\
                        .then_inc(picked.sem, 1)
                    pool.wait_ge(picked.sem, picked.upto(t))
                    pool.sem_inc(pool_steps, 1)
                    nc.gpsimd.indirect_dma_start(
                        records, bass.IndirectOffsetOnAxis(ap=cur_rank[:, t.slot:t.slot + 1], axis=0),
                        cur_rec[:, t.slot, :], None).then_inc(scattered.sem(t), 16)

                in_steps(pool, ET, [(0, pick)])

            @block.scalar
            def _(act):
                w_high(act)

                def copy_hot(t):
                    act.wait_ge(hot_turned.sem, hot_turned.upto(t))
                    if t.has(2):
                        act.wait_ge(looked.sem, looked.upto(t, 2))
                    nc.scalar.activation(hot_hi_t[:, t.half, :], p_hot[t.half][:], ACT.Copy).then_inc(hot_copied.sem, 1)

                in_steps(act, ET, [(0, copy_hot)])

            @block.vector
            def _(dve):
                links = [0]

                def link(ins):
                    links[0] += 1
                    ins.then_inc(chain, 1)
                    dve.wait_ge(chain, links[0])

                nc.vector.memset(edge_ints[:, 0, :], PAD_NODE)
                nc.vector.memset(edge_ints[:, 1, :], 0)
                nc.vector.memset(weight_in[:], 0.0).then_inc(edge_clear, 1)
                nc.vector.memset(guard[:], -1.0).then_inc(edge_clear, 1)
                nc.vector.memset(src_all[:, E:EP], float(PAD_NODE))
                nc.vector.memset(ones_row[:], 1.0)
                nc.vector.memset(eps[:], EPS)
                link(nc.vector.memset(hist[:, 0:P], 0.0))
                dve.wait_ge(iotas, 2)
                nc.vector.tensor_copy(iota[:], iota_i[:])
                link(nc.vector.tensor_copy(iota_part[:], iota_part_i[:]))
                nc.vector.tensor_scalar(ident[:], iota[:], iota_part[:, 0:1], None, ALU.is_equal)
                nc.vector.tensor_scalar(ident_b[:], iota[:], iota_part[:, 0:1], None, ALU.is_equal).then_inc(consts, 1)
                nc.vector.tensor_scalar(earlier[:], iota[:], iota_part[:, 0:1], None, ALU.is_lt)
                nc.vector.tensor_scalar(below[:], iota[:], iota_part[:, 0:1], None, ALU.is_gt).then_inc(consts, 1)
                dve.wait_ge(edges_in, 64)
                nc.vector.tensor_copy(rec[:, :, 0], edge_ints[:, 0, :])
                nc.vector.tensor_copy(rec[:, :, 1], edge_ints[:, 1, :])
                nc.vector.tensor_copy(rec[:, :, 2], weight_in[:])
                nc.vector.tensor_copy(src_all[:, 0:E], src_all_i[:])
                nc.vector.tensor_scalar(hi_i[:], edge_ints[:, 0, :], 7, None, ALU.arith_shift_right)
                link(nc.vector.tensor_scalar(lo_i[:], edge_ints[:, 0, :], P - 1, None, ALU.bitwise_and))
                nc.vector.tensor_copy(hi_of[:], hi_i[:])
                link(nc.vector.tensor_copy(lo_of[:], lo_i[:]))

                def one_hot(t):
                    at = bass.ds(t.times(P), P)
                    nc.vector.tensor_scalar(hot_lo[:, at], iota[:], lo_of[:, bass.ds(t.times(1), 1)], None, ALU.is_equal)
                    nc.vector.tensor_scalar(hot_hi[:, at], iota[:], hi_of[:, bass.ds(t.times(1), 1)], None,
                                            ALU.is_equal).then_inc(hot_done.sem, 1)

                def add_hist(t):
                    dve.wait_ge(hist_mm.sem, hist_mm.upto(t))
                    if t.has(1):
                        dve.wait_ge(hist_sum.sem, hist_sum.upto(t, 1))
                    nc.vector.tensor_tensor(hist[:, bass.ds(t.times(P, P), P)], p_hist[t.half][:],
                                            hist[:, bass.ds(t.times(P), P)], ALU.add).then_inc(hist_sum.sem, 1)

                in_steps(dve, ET, [(0, one_hot), (2, add_hist)])
                total = hist[:, ET * P:(ET + 1) * P]
                dve.wait_ge(hist_sum.sem, hist_sum.all(ET))
                nc.vector.tensor_tensor_scan(prefix[:], ones_row[:], total, 0.0, ALU.mult, ALU.add)\
                    .then_inc(prefix_done, 1)
                dve.wait_ge(prefix_done, 1)
                dve.wait_ge(offsets_mm, 1)
                nc.vector.tensor_copy(row_offset[:], p_misc[:, 0:1])
                nc.vector.tensor_scalar(row_offset1[:], p_misc[:, 0:1], -1.0, None, ALU.add)
                link(nc.vector.tensor_scalar(empty[:], total, 0.0, float(NOWHERE), ALU.is_equal, ALU.mult))
                nc.vector.scalar_tensor_tensor(last_pos[:], prefix[:], row_offset1[:, 0:1], empty[:], ALU.add, ALU.add)\
                    .then_inc(last_pos_done, 1)
                nc.vector.tensor_copy(table[:, 0, P:2 * P], total)
                nc.vector.tensor_copy(table[:, 1, P:2 * P], total)
                link(nc.vector.scalar_tensor_tensor(base[:], prefix[:], row_offset[:, 0:1], total, ALU.add, ALU.subtract))

                def make_table(t):
                    if t.has(2):
                        dve.wait_ge(looked.sem, looked.upto(t, 2))
                    nc.vector.tensor_tensor(table[:, t.half, 0:P], base[:], hist[:, bass.ds(t.times(P), P)],
                                            ALU.add).then_inc(table_done.sem, 1)

                def rank(t):
                    column = bass.ds(t.times(1), 1)
                    same = src_all[:].rearrange("p (q t) -> p q t", t=ET)[:, :, column]
                    if t.has(1):
                        dve.wait_ge(ranked.sem, ranked.upto(t, 1))
                    nc.vector.scalar_tensor_tensor(junk[:, 0, :], same.rearrange("p q o -> p (q o)"), rec[:, column, 0],
                                                   earlier[:], ALU.is_equal, ALU.mult, accum_out=rank_b[:, column])
                    at = bass.ds(t.times(P), P)
                    dve.wait_ge(looked.sem, looked.upto(t))
                    nc.vector.scalar_tensor_tensor(junk[:, 1, :], p_look[t.half][:, 0:P], 1.0, hot_lo[:, at],
                                                   ALU.mult, ALU.mult, accum_out=rank_a[:, column])
                    nc.vector.scalar_tensor_tensor(junk[:, 2, :], p_look[t.half][:, P:2 * P], 1.0, hot_lo[:, at],
                                                   ALU.mult, ALU.mult, accum_out=rec[:, column, 3])\
                        .then_inc(ranked.sem, 1)

                in_steps(dve, ET, [(0, make_table), (2, rank)])
                dve.wait_ge(ranked.sem, ranked.all(ET))
                nc.vector.scalar_tensor_tensor(rank_i[:], rank_a[:], 1.0, rank_b[:], ALU.add, ALU.add)\
                    .then_inc(ranks_ready, 1)
                dve.wait_ge(nodes_mm, 1)
                nc.vector.tensor_scalar(node_idx[:], p_misc[:, 128:128 + NT], float(EP), None, ALU.min)
                w_low(dve)
                dve.wait_ge(back_in, 16 * (ET // 8))
                nc.vector.tensor_tensor(same_t[:], back[:, 1:P + 1, 0], back[:, 0:P, 0], ALU.is_equal)\
                    .then_inc(rows_ready, 1)
                nc.vector.tensor_copy(src_t[:], back[:, 1:P + 1, 0]).then_inc(rows_ready, 1)
                for f in range(3):
                    last = nc.vector.tensor_copy(col_t[:, f, :], back[:, 1:P + 1, f + 1])
                last.then_inc(rows_ready, 1)
                dve.wait_ge(cols_mm, 1)
                nc.vector.tensor_copy(src_at[:], p_misc[:, 256:256 + ET])
                nc.vector.tensor_scalar(src_idx[:], p_misc[:, 256:256 + ET], float(N - 1), None, ALU.min)
                nc.vector.tensor_copy(dst_idx[:], p_misc[:, 256 + ET:256 + 2 * ET])
                nc.vector.tensor_copy(weight_at[:], p_misc[:, 256 + 2 * ET:256 + 3 * ET])
                link(nc.vector.tensor_scalar(invdeg_at[:], p_misc[:, 256 + 3 * ET:256 + 4 * ET], 1.0, None, ALU.max))
                nc.vector.reciprocal(invdeg_at[:], invdeg_at[:]).then_inc(cols_ready, 1)

            @block.tensor
            def _(pe):
                def histogram(t):
                    at = bass.ds(t.times(P), P)
                    pe.wait_ge(hot_done.sem, hot_done.upto(t))
                    if t.has(2):
                        pe.wait_ge(hist_sum.sem, hist_sum.upto(t, 2))
                    nc.tensor.matmul(p_hist[t.half][:], hot_hi[:, at], hot_lo[:, at], start=True, stop=True)\
                        .then_inc(hist_mm.sem, 1)

                in_steps(pe, ET, [(0, histogram)])
                pe.wait_ge(consts, 2)
                pe.wait_ge(prefix_done, 1)
                nc.tensor.matmul(p_misc[:, 0:1], below[:], prefix[:, P - 1:P], start=True, stop=True)\
                    .then_inc(offsets_mm, 1)

                def turn(t):
                    pe.wait_ge(consts, 2)
                    if t.has(2):
                        pe.wait_ge(hot_copied.sem, hot_copied.upto(t, 2))
                    nc.tensor.transpose(p_hot[t.half][:], hot_hi[:, bass.ds(t.times(P), P)], ident_b[:])\
                        .then_inc(hot_turned.sem, 1)

                def look(t):
                    pe.wait_ge(hot_copied.sem, hot_copied.upto(t))
                    pe.wait_ge(table_done.sem, table_done.upto(t))
                    if t.has(2):
                        pe.wait_ge(ranked.sem, ranked.upto(t, 2))
                    nc.tensor.matmul(p_look[t.half][:], hot_hi_t[:, t.half, :], table[:, t.half, :],
                                     start=True, stop=True).then_inc(looked.sem, 1)

                in_steps(pe, ET, [(0, turn), (1, look)])
                pe.wait_ge(last_pos_done, 1)
                nc.tensor.transpose(p_misc[:, 128:256], last_pos[:], ident[:]).then_inc(nodes_mm, 1)
                pe.wait_ge(rows_ready, 3)
                for f in range(4):
                    rows = src_t[:] if f == 0 else col_t[:, f - 1, :]
                    last = nc.tensor.transpose(p_misc[:, 256 + f * ET:256 + (f + 1) * ET], rows, ident[0:ET, 0:ET])
                last.then_inc(cols_mm, 1)

        gathered = slots("gathered")
        gathered2 = slots("gathered2")
        index_picked = Count(sem("index_picked"))
        scaled = Count(sem("scaled"))
        turned = Count(sem("turned"))
        summed = Count(sem("summed"))
        high_done = Count(sem("high_done"))
        low_done = Count(sem("low_done"))
        product_done = Count(sem("product_done"))
        rows_done = Count(sem("rows_done"))
        rows_stored = slots("rows_stored")
        consts_in = Count(sem("consts_in"), 16)
        consts_made = Count(sem("consts_made"))
        fill_stored = Count(sem("fill_stored"), 16)
        x_landed = slots("x_landed")
        filled = Count(sem("filled"))
        preact_done = Count(sem("preact_done"))
        y_done = Count(sem("y_done"))
        x_plus_beta = Count(sem("x_plus_beta"))
        scaled_gamma = Count(sem("scaled_gamma"))
        y2_done = Count(sem("y2_done"))

        class Norm:

            def __init__(self, name):
                self.mean = Count(sem(f"{name}_mean"))
                self.squares = Count(sem(f"{name}_squares"))
                self.std = Count(sem(f"{name}_std"))
                self.rstd = Count(sem(f"{name}_rstd"))
                self.scale = Count(sem(f"{name}_scale"))
                self.applied = Count(sem(f"{name}_applied"))

            def close(self, n):
                for count in (self.mean, self.squares, self.std, self.rstd, self.scale, self.applied):
                    count.close(n)

        norm_inner = Norm("inner")
        norm_outer = Norm("outer")
        SUM, NEG_MEAN, SQUARES, STD, RSTD, SHIFT = range(6)

        def norm_steps(norm, y, y_ready, stats, junk, target, target_free):

            def mean(dve, t):
                dve.wait_ge(y_ready.sem, y_ready.upto(t))
                nc.vector.tensor_scalar(stats[:, t.slot, NEG_MEAN:NEG_MEAN + 1], stats[:, t.slot, SUM:SUM + 1],
                                        -1.0 / D, None, ALU.mult).then_inc(norm.mean.sem, 1)

            def squares(act, t):
                act.wait_ge(norm.mean.sem, norm.mean.upto(t))
                nc.scalar.activation(junk[:, t.half, :], y[:, t.slot, :], ACT.Square,
                                     bias=stats[:, t.slot, NEG_MEAN:NEG_MEAN + 1],
                                     accum_out=stats[:, t.slot, SQUARES:SQUARES + 1]).then_inc(norm.squares.sem, 1)

            def std(act, t):
                act.wait_ge(norm.squares.sem, norm.squares.upto(t))
                nc.scalar.activation(stats[:, t.slot, STD:STD + 1], stats[:, t.slot, SQUARES:SQUARES + 1], ACT.Sqrt,
                                     bias=eps[:, 0:1], scale=1.0 / D).then_inc(norm.std.sem, 1)

            def rstd(dve, t):
                dve.wait_ge(norm.std.sem, norm.std.upto(t))
                nc.vector.reciprocal(stats[:, t.slot, RSTD:RSTD + 1], stats[:, t.slot, STD:STD + 1])\
                    .then_inc(norm.rstd.sem, 1)

            def shift(dve, t):
                dve.wait_ge(norm.rstd.sem, norm.rstd.upto(t))
                nc.vector.tensor_tensor(stats[:, t.slot, SHIFT:SHIFT + 1], stats[:, t.slot, NEG_MEAN:NEG_MEAN + 1],
                                        stats[:, t.slot, RSTD:RSTD + 1], ALU.mult).then_inc(norm.scale.sem, 1)

            def apply(act, t):
                act.wait_ge(norm.scale.sem, norm.scale.upto(t))
                target_free(act, t)
                nc.scalar.activation(target(t), y[:, t.slot, :], ACT.Identity,
                                     bias=stats[:, t.slot, SHIFT:SHIFT + 1],
                                     scale=stats[:, t.slot, RSTD:RSTD + 1]).then_inc(norm.applied.sem, 1)

            return mean, squares, std, rstd, shift, apply

        def pick_index(pool, cur, indices, t):
            nc.gpsimd.tensor_copy(cur[:, t.slot:t.slot + 1], indices[:, bass.ds(t.times(1), 1)])\
                .then_inc(index_picked.sem, 1)
            pool.wait_ge(index_picked.sem, index_picked.upto(t))
            pool.sem_inc(pool_steps, 1)

        def split_product(bank, hi, lo, slot, w_cols=slice(None)):
            for c in range(DC):
                for a, w in ((hi, w_hi), (hi, w_lo), (lo, w_hi)):
                    last = nc.tensor.matmul(bank, a[:, c, :], w[slot][:, c, w_cols],
                                            start=(c == 0 and a is hi and w is w_hi),
                                            stop=(c == DC - 1 and a is lo))
            return last

        def edge_phase(layer, x_dram, slot, biases, jobs):
            by_weight, by_degree = layer == 2, layer == 0
            with ExitStack() as ph:
                e = sb(f"e{layer}", [P, UNROLL, D], F32, ph)
                cur = sb(f"cur_e{layer}", [P, UNROLL], I32, ph)
                hi = sb(f"edge_hi{layer}", [P, 2, DC, P], F32R, ph)
                lo = sb(f"edge_lo{layer}", [P, 2, DC, P], F32R, ph)
                rows = sb(f"rows{layer}", [P, UNROLL, D], F32, ph)
                bias_in = sb(f"bias_in_e{layer}", [P, 2, D], F32, ph)
                bias = sb(f"bias_e{layer}", [P, D], F32, ph)
                turned_bank = [pb(f"pt_e{layer}{k}", [P, DC, P], F32, ph) for k in range(2)]
                sums = sb(f"sums{layer}", [P, 2, DC, P], F32, ph)
                product_bank = [pb(f"pp_e{layer}{k}", [P, D], F32, ph) for k in range(2)]
                w_load, w_high, w_low = weight_split_steps(ph, jobs)
                block = ph.enter_context(nc.Block())

                @block.sync
                def _(sp):
                    for k, b in enumerate(biases):
                        sp.dma_start(bias_in[:, k, :], b.partition_broadcast(P)).then_inc(consts_in.sem, 16)
                    w_load(sp)
                    if biases:
                        sp.wait_ge(consts_made.sem, consts_made.all(1))
                        fill = bias_in[0:1, 0, :] if by_degree else bias[0:1, :]
                        sp.dma_start(neigh_rows[EP:EP + 1, :], fill).then_inc(fill_stored.sem, 16)

                    def store(t):
                        sp.wait_ge(rows_done.sem, rows_done.upto(t))
                        sp.dma_start(neigh_rows[bass.ds(t.times(P), P), :], rows[:, t.slot, :])\
                            .then_inc(rows_stored.sem(t), 16)

                    in_steps(sp, ET, [(0, store)])
                    for s, v in rows_stored.used(ET):
                        sp.wait_ge(s, v)
                    if biases:
                        sp.wait_ge(fill_stored.sem, fill_stored.all(1))

                @block.gpsimd
                def _(pool):
                    def gather(t):
                        if t.has(UNROLL):
                            pool.wait_ge(turned.sem, turned.upto(t, UNROLL))
                        pick_index(pool, cur, dst_idx, t)
                        nc.gpsimd.indirect_dma_start(
                            e[:, t.slot, :], None, x_dram,
                            bass.IndirectOffsetOnAxis(ap=cur[:, t.slot:t.slot + 1], axis=0))\
                            .then_inc(gathered.sem(t), 16)

                    in_steps(pool, ET, [(0, gather)])

                @block.scalar
                def _(act):
                    w_high(act)

                    def weigh(t):
                        act.wait_ge(gathered.sem(t), gathered.landed(t))
                        nc.scalar.activation(e[:, t.slot, :], e[:, t.slot, :], ACT.Copy,
                                             scale=weight_at[:, bass.ds(t.times(1), 1)]).then_inc(scaled.sem, 1)

                    def high(t):
                        act.wait_ge(summed.sem, summed.upto(t))
                        if t.has(2):
                            act.wait_ge(product_done.sem, product_done.upto(t, 2))
                        nc.scalar.activation(hi[:, t.half], sums[:, t.half], ACT.Copy).then_inc(high_done.sem, 1)

                    def rows_out_plain(t):
                        act.wait_ge(product_done.sem, product_done.upto(t))
                        if t.has(UNROLL):
                            act.wait_ge(rows_stored.sem(t), rows_stored.landed(t, 1))
                        nc.scalar.activation(rows[:, t.slot, :], product_bank[t.half][:], ACT.Copy)\
                            .then_inc(rows_done.sem, 1)

                    if by_weight:
                        in_steps(act, ET, [(0, weigh), (1, high), (4, rows_out_plain)])
                    else:
                        in_steps(act, ET, [(0, high)])

                @block.vector
                def _(dve):
                    if biases:
                        dve.wait_ge(consts_in.sem, consts_in.all(len(biases)))
                        nc.vector.tensor_tensor(bias[:], bias_in[:, 0, :], bias_in[:, 1, :], ALU.add)\
                            .then_inc(consts_made.sem, 1)
                    w_low(dve)

                    def run_sums(t):
                        dve.wait_ge(turned.sem, turned.upto(t))
                        if t.has(2):
                            dve.wait_ge(high_done.sem, high_done.upto(t, 2))
                            dve.wait_ge(low_done.sem, low_done.upto(t, 2))
                        if t.has(1):
                            dve.wait_ge(summed.sem, summed.upto(t, 1))
                        for c in range(DC):
                            start = sums[:, 1 - t.half, c, P - 1:P] if t.has(1) else 0.0
                            last = nc.vector.tensor_tensor_scan(
                                sums[:, t.half, c, :], same_run[:, bass.ds(t.times(P), P)],
                                turned_bank[t.half][:, c, :], start, ALU.mult, ALU.add)
                        last.then_inc(summed.sem, 1)

                    def low(t):
                        dve.wait_ge(high_done.sem, high_done.upto(t))
                        if t.has(2):
                            dve.wait_ge(product_done.sem, product_done.upto(t, 2))
                        nc.vector.tensor_tensor(lo[:, t.half], sums[:, t.half], hi[:, t.half].bitcast(F32),
                                                ALU.subtract).then_inc(low_done.sem, 1)

                    def rows_out_bias(t):
                        dve.wait_ge(product_done.sem, product_done.upto(t))
                        if t.has(UNROLL):
                            dve.wait_ge(rows_stored.sem(t), rows_stored.landed(t, 1))
                        if not t.has(1):
                            dve.wait_ge(consts_made.sem, consts_made.all(1))
                        factor = invdeg_at[:, bass.ds(t.times(1), 1)] if by_degree else 1.0
                        nc.vector.scalar_tensor_tensor(rows[:, t.slot, :], product_bank[t.half][:], factor, bias[:],
                                                       ALU.mult, ALU.add).then_inc(rows_done.sem, 1)

                    in_steps(dve, ET, [(0, run_sums), (1, low)] + ([] if by_weight else [(3, rows_out_bias)]))

                @block.tensor
                def _(pe):
                    def turn(t):
                        if by_weight:
                            pe.wait_ge(scaled.sem, scaled.upto(t))
                        else:
                            pe.wait_ge(gathered.sem(t), gathered.landed(t))
                        if t.has(2):
                            pe.wait_ge(summed.sem, summed.upto(t, 2))
                        for c in range(DC):
                            last = nc.tensor.transpose(turned_bank[t.half][:, c, :], e[:, t.slot, c * P:(c + 1) * P],
                                                       ident[:])
                        last.then_inc(turned.sem, 1)

                    def product(t):
                        pe.wait_ge(low_done.sem, low_done.upto(t))
                        if t.has(2):
                            pe.wait_ge(rows_done.sem, rows_done.upto(t, 2))
                        split_product(product_bank[t.half][:], hi[:, t.half], lo[:, t.half], slot)\
                            .then_inc(product_done.sem, 1)

                    in_steps(pe, ET, [(0, turn), (2, product)])

            for count in (index_picked, turned, summed, high_done, low_done, product_done, rows_done):
                count.close(ET)
            for ring in (gathered, rows_stored):
                ring.close(ET)
            if by_weight:
                scaled.close(ET)
            if biases:
                consts_in.close(len(biases))
                consts_made.close(1)
                fill_stored.close(1)

        def node_phase(layer, x_dram, y_dram, slot, jobs):
            inner = layer == 0
            with ExitStack() as ph:
                xs = sb(f"x{layer}", [P, UNROLL, D], F32, ph)
                g = sb(f"g{layer}", [P, UNROLL, D], F32, ph)
                cur = sb(f"cur_n{layer}", [P, UNROLL], I32, ph)
                hi = sb(f"x_hi{layer}", [P, 2, DC, P], F32R, ph)
                lo = sb(f"x_lo{layer}", [P, 2, DC, P], F32R, ph)
                y = sb(f"y{layer}", [P, UNROLL, D], F32, ph)
                done = sb(f"done{layer}", [P, UNROLL, D], F32, ph)
                junk = sb(f"junk_n{layer}", [P, 2, D], F32, ph)
                stats = sb(f"stats{layer}", [P, UNROLL, 6], F32, ph)
                gamma_beta = sb(f"gamma_beta{layer}", [P, 2, D], F32, ph)
                turned_bank = [pb(f"pt_n{layer}{k}", [P, DC, P], F32, ph) for k in range(2)]
                product_bank = [pb(f"pp_n{layer}{k}", [P, D], F32, ph) for k in range(2)]
                if inner:
                    xb = sb("xb", [P, UNROLL, D], F32, ph)
                    y2 = sb("y_outer", [P, UNROLL, D], F32, ph)
                    stats2 = sb("stats_outer", [P, UNROLL, 6], F32, ph)
                    centered = sb("centered", [P, 2, D], F32, ph)
                w_load, w_high, w_low = weight_split_steps(ph, jobs)
                rows_in = [gamma, beta] if inner else []

                def done_free(act, t):
                    if t.has(UNROLL):
                        act.wait_ge(rows_stored.sem(t), rows_stored.landed(t, 1))

                if inner:
                    mean, squares, std, rstd, _, _ = norm_steps(norm_inner, y, y_done, stats, junk, None, None)
                    mean2, squares2, std2, rstd2, shift2, apply2 = norm_steps(
                        norm_outer, y2, y2_done, stats2, junk, lambda t: done[:, t.slot, :], done_free)
                else:
                    mean, squares, std, rstd, shift, apply = norm_steps(
                        norm_outer, y, y_done, stats, junk, lambda t: done[:, t.slot, :], done_free)
                block = ph.enter_context(nc.Block())

                @block.sync
                def _(sp):
                    for k, b in enumerate(rows_in):
                        sp.dma_start(gamma_beta[:, k, :], b.partition_broadcast(P)).then_inc(consts_in.sem, 16)

                    def load(t):
                        if t.has(UNROLL):
                            sp.wait_ge(y_done.sem, y_done.upto(t, UNROLL))
                            if inner:
                                sp.wait_ge(x_plus_beta.sem, x_plus_beta.upto(t, UNROLL))
                        n = NREST if isinstance(t.loop, int) and t.offset == NT - 1 else P
                        sp.dma_start(xs[0:n, t.slot, :], x_dram[bass.ds(t.times(P), n), :])\
                            .then_inc(x_landed.sem(t), 16)

                    def store(t):
                        n = NREST if isinstance(t.loop, int) and t.offset == NT - 1 else P
                        sp.wait_ge(norm_outer.applied.sem, norm_outer.applied.upto(t))
                        sp.dma_start(y_dram[bass.ds(t.times(P), n), :], done[0:n, t.slot, :])\
                            .then_inc(rows_stored.sem(t), 16)

                    def weights(t):
                        if isinstance(t.loop, int) and t.offset == 0:
                            w_load(sp)

                    in_steps(sp, NT, [(0, load), (3, weights), (10 if inner else 7, store)])
                    for s, v in rows_stored.used(NT):
                        sp.wait_ge(s, v)

                @block.gpsimd
                def _(pool):
                    def fetch(t):
                        if t.has(UNROLL):
                            pool.wait_ge(preact_done.sem, preact_done.upto(t, UNROLL))
                        pick_index(pool, cur, node_idx, t)
                        nc.gpsimd.indirect_dma_start(
                            g[:, t.slot, :], None, neigh_rows,
                            bass.IndirectOffsetOnAxis(ap=cur[:, t.slot:t.slot + 1], axis=0))\
                            .then_inc(gathered.sem(t), 16)

                    def add_beta(t):
                        pool.wait_ge(x_landed.sem(t), x_landed.landed(t))
                        if t.has(UNROLL):
                            pool.wait_ge(y2_done.sem, y2_done.upto(t, UNROLL))
                        nc.gpsimd.tensor_tensor(xb[:, t.slot, :], xs[:, t.slot, :], gamma_beta[:, 1, :], ALU.add)\
                            .then_inc(x_plus_beta.sem, 1)

                    in_steps(pool, NT, [(0, fetch)] + ([(2, add_beta)] if inner else []))

                @block.scalar
                def _(act):
                    w_high(act)

                    def high(t):
                        act.wait_ge(turned.sem, turned.upto(t))
                        if t.has(2):
                            act.wait_ge(product_done.sem, product_done.upto(t, 2))
                        nc.scalar.activation(hi[:, t.half], turned_bank[t.half][:], ACT.Copy)\
                            .then_inc(high_done.sem, 1)

                    stages = [(0, high), (3, lambda t: squares(act, t)), (3, lambda t: std(act, t))]
                    if inner:
                        stages += [(6, lambda t: squares2(act, t)), (6, lambda t: std2(act, t)),
                                   (8, lambda t: apply2(act, t))]
                    else:
                        stages += [(5, lambda t: apply(act, t))]
                    in_steps(act, NT, stages)

                @block.vector
                def _(dve):
                    if inner:
                        dve.wait_ge(consts_in.sem, consts_in.all(len(rows_in)))
                    w_low(dve)

                    def low(t):
                        dve.wait_ge(high_done.sem, high_done.upto(t))
                        if t.has(2):
                            dve.wait_ge(product_done.sem, product_done.upto(t, 2))
                        nc.vector.tensor_tensor(lo[:, t.half], turned_bank[t.half][:], hi[:, t.half].bitcast(F32),
                                                ALU.subtract).then_inc(low_done.sem, 1)

                    def preact(t):
                        dve.wait_ge(product_done.sem, product_done.upto(t))
                        dve.wait_ge(gathered.sem(t), gathered.landed(t))
                        nc.vector.tensor_tensor(product_bank[t.half][:], product_bank[t.half][:], g[:, t.slot, :],
                                                ALU.add).then_inc(preact_done.sem, 1)

                    def residual(t):
                        dve.wait_ge(preact_done.sem, preact_done.upto(t))
                        if t.has(UNROLL):
                            if inner:
                                dve.wait_ge(norm_inner.squares.sem, norm_inner.squares.upto(t, UNROLL))
                                dve.wait_ge(scaled_gamma.sem, scaled_gamma.upto(t, UNROLL))
                            else:
                                dve.wait_ge(norm_outer.applied.sem, norm_outer.applied.upto(t, UNROLL))
                        nc.vector.scalar_tensor_tensor(
                            y[:, t.slot, :], product_bank[t.half][:], 0.0, xs[:, t.slot, :], ALU.max, ALU.add,
                            accum_out=stats[:, t.slot, SUM:SUM + 1]).then_inc(y_done.sem, 1)

                    def center(t):
                        dve.wait_ge(norm_inner.mean.sem, norm_inner.mean.upto(t))
                        if t.has(2):
                            dve.wait_ge(y2_done.sem, y2_done.upto(t, 2))
                        nc.vector.scalar_tensor_tensor(centered[:, t.half, :], y[:, t.slot, :],
                                                       stats[:, t.slot, NEG_MEAN:NEG_MEAN + 1], gamma_beta[:, 0, :],
                                                       ALU.add, ALU.mult).then_inc(scaled_gamma.sem, 1)

                    def outer(t):
                        dve.wait_ge(norm_inner.rstd.sem, norm_inner.rstd.upto(t))
                        dve.wait_ge(scaled_gamma.sem, scaled_gamma.upto(t))
                        dve.wait_ge(x_plus_beta.sem, x_plus_beta.upto(t))
                        if t.has(UNROLL):
                            dve.wait_ge(norm_outer.applied.sem, norm_outer.applied.upto(t, UNROLL))
                        nc.vector.scalar_tensor_tensor(
                            y2[:, t.slot, :], centered[:, t.half, :], stats[:, t.slot, RSTD:RSTD + 1],
                            xb[:, t.slot, :], ALU.mult, ALU.add,
                            accum_out=stats2[:, t.slot, SUM:SUM + 1]).then_inc(y2_done.sem, 1)

                    if inner:
                        stages = [(7, lambda t: rstd2(dve, t)), (2, preact), (7, lambda t: shift2(dve, t)),
                                  (5, lambda t: rstd(dve, t)), (2, residual), (5, outer), (3, center), (0, low),
                                  (2, lambda t: mean(dve, t)), (5, lambda t: mean2(dve, t))]
                    else:
                        stages = [(2, preact), (4, lambda t: rstd(dve, t)), (2, residual), (0, low),
                                  (4, lambda t: shift(dve, t)), (2, lambda t: mean(dve, t))]
                    in_steps(dve, NT, stages)

                @block.tensor
                def _(pe):
                    def turn(t):
                        pe.wait_ge(x_landed.sem(t), x_landed.landed(t))
                        if t.has(2):
                            pe.wait_ge(low_done.sem, low_done.upto(t, 2))
                        for c in range(DC):
                            last = nc.tensor.transpose(turned_bank[t.half][:, c, :], xs[:, t.slot, c * P:(c + 1) * P],
                                                       ident[:])
                        last.then_inc(turned.sem, 1)

                    def product(t):
                        pe.wait_ge(low_done.sem, low_done.upto(t))
                        if t.has(2):
                            pe.wait_ge(y_done.sem, y_done.upto(t, 2))
                        split_product(product_bank[t.half][:], hi[:, t.half], lo[:, t.half], slot)\
                            .then_inc(product_done.sem, 1)

                    in_steps(pe, NT, [(0, turn), (1, product)])

            for count in (index_picked, turned, high_done, low_done, product_done, preact_done, y_done):
                count.close(NT)
            for ring in (gathered, rows_stored, x_landed):
                ring.close(NT)
            consts_in.close(len(rows_in))
            norm_outer.close(NT)
            if inner:
                for count in (norm_inner.mean, norm_inner.squares, norm_inner.std, norm_inner.rstd):
                    count.close(NT)
                for count in (x_plus_beta, scaled_gamma, y2_done):
                    count.close(NT)

        def residual_phase(layer, x_dram, y_dram, jobs):
            with ExitStack() as ph:
                xs = sb(f"x{layer}", [P, UNROLL, D], F32, ph)
                g = sb(f"g{layer}", [P, UNROLL, D], F32, ph)
                cur = sb(f"cur_n{layer}", [P, UNROLL], I32, ph)
                y = sb(f"y{layer}", [P, UNROLL, D], F32, ph)
                done = sb(f"done{layer}", [P, UNROLL, D], F32, ph)
                junk = sb(f"junk_n{layer}", [P, 2, D], F32, ph)
                stats = sb(f"stats{layer}", [P, UNROLL, 6], F32, ph)
                w_load, w_high, w_low = weight_split_steps(ph, jobs) if jobs else (None, None, None)

                def done_free(act, t):
                    if t.has(UNROLL):
                        act.wait_ge(rows_stored.sem(t), rows_stored.landed(t, 1))

                mean, squares, std, rstd, shift, apply = norm_steps(
                    norm_outer, y, y_done, stats, junk, lambda t: done[:, t.slot, :], done_free)
                block = ph.enter_context(nc.Block())

                @block.sync
                def _(sp):
                    def load(t):
                        n = NREST if isinstance(t.loop, int) and t.offset == NT - 1 else P
                        if t.has(UNROLL):
                            sp.wait_ge(y_done.sem, y_done.upto(t, UNROLL))
                        sp.dma_start(xs[0:n, t.slot, :], x_dram[bass.ds(t.times(P), n), :])\
                            .then_inc(x_landed.sem(t), 16)

                    def store(t):
                        n = NREST if isinstance(t.loop, int) and t.offset == NT - 1 else P
                        sp.wait_ge(norm_outer.applied.sem, norm_outer.applied.upto(t))
                        sp.dma_start(y_dram[bass.ds(t.times(P), n), :], done[0:n, t.slot, :])\
                            .then_inc(rows_stored.sem(t), 16)

                    if jobs:
                        w_load(sp)
                    in_steps(sp, NT, [(0, load), (6, store)])
                    for s, v in rows_stored.used(NT):
                        sp.wait_ge(s, v)

                @block.gpsimd
                def _(pool):
                    def fetch(t):
                        if t.has(UNROLL):
                            pool.wait_ge(y_done.sem, y_done.upto(t, UNROLL))
                            pool.sem_inc(pool_steps, 1)
                        nc.gpsimd.memset(g[:, t.slot, :], 0.0).then_inc(filled.sem, 1)
                        pool.wait_ge(filled.sem, filled.upto(t))
                        pick_index(pool, cur, node_idx, t)
                        nc.gpsimd.indirect_dma_start(
                            g[:, t.slot, :], None, neigh_rows,
                            bass.IndirectOffsetOnAxis(ap=cur[:, t.slot:t.slot + 1], axis=0),
                            bounds_check=EP - 1, oob_is_err=False).then_inc(gathered.sem(t), 16)

                    in_steps(pool, NT, [(0, fetch)])

                @block.scalar
                def _(act):
                    if jobs:
                        w_high(act)
                    in_steps(act, NT, [(1, lambda t: squares(act, t)), (1, lambda t: std(act, t)),
                                       (3, lambda t: apply(act, t))])

                @block.vector
                def _(dve):
                    def residual(t):
                        dve.wait_ge(x_landed.sem(t), x_landed.landed(t))
                        dve.wait_ge(gathered.sem(t), gathered.landed(t))
                        if t.has(UNROLL):
                            dve.wait_ge(norm_outer.applied.sem, norm_outer.applied.upto(t, UNROLL))
                        nc.vector.scalar_tensor_tensor(
                            y[:, t.slot, :], xs[:, t.slot, :], 1.0, g[:, t.slot, :], ALU.mult, ALU.add,
                            accum_out=stats[:, t.slot, SUM:SUM + 1]).then_inc(y_done.sem, 1)

                    if jobs:
                        w_low(dve)
                    in_steps(dve, NT, [(2, lambda t: rstd(dve, t)), (0, residual), (2, lambda t: shift(dve, t)),
                                       (0, lambda t: mean(dve, t))])

            for count in (index_picked, filled, y_done):
                count.close(NT)
            for ring in (gathered, rows_stored, x_landed):
                ring.close(NT)
            norm_outer.close(NT)

        def attention(x_dram):
            with ExitStack() as keep:
                v_all = sb("v_all", [P, ET * D], F32, keep)
                scores = sb("scores", [P, ET * HEADS], F32, keep)
                exps = sb("exps", [P, ET * HEADS], F32, keep)
                query_product(x_dram, v_all, scores)
                softmax_terms(scores, exps)
                weighted_sums(v_all, exps)

        def query_product(x_dram, v_all, scores):
            with ExitStack() as ph:
                e = [sb(f"e_{side}", [P, UNROLL, D], F32, ph) for side in ("src", "dst")]
                cur = [sb(f"cur_{side}", [P, UNROLL], I32, ph) for side in ("src", "dst")]
                hi = [sb(f"hi_{side}", [P, 2, DC, P], F32R, ph) for side in ("src", "dst")]
                lo = [sb(f"lo_{side}", [P, 2, DC, P], F32R, ph) for side in ("src", "dst")]
                q = sb("q", [P, 2, D], F32, ph)
                qk = sb("qk", [P, 2, D], F32, ph)
                turned_bank = [pb(f"pt_{side}", [P, DC, P], F32, ph) for side in ("src", "dst")]
                banks = {n: [pb(f"p{n}{k}", [P, D], F32, ph) for k in range(2)] for n in "qkv"}
                landed = [gathered, gathered2]
                indices = [src_idx, dst_idx]
                v_copied = Count(sem("v_copied"))
                q_copied = Count(sem("q_copied"))
                qk_done = Count(sem("qk_done"))
                scored = Count(sem("scored"))
                q_product_done = Count(sem("q_product_done"))
                picked = Count(sem("both_picked"), 2)
                block = ph.enter_context(nc.Block())

                @block.gpsimd
                def _(pool):
                    def gather(t):
                        if t.has(UNROLL):
                            pool.wait_ge(turned.sem, turned.upto(t, UNROLL))
                        for side in range(2):
                            nc.gpsimd.tensor_copy(cur[side][:, t.slot:t.slot + 1],
                                                  indices[side][:, bass.ds(t.times(1), 1)]).then_inc(picked.sem, 1)
                        pool.wait_ge(picked.sem, picked.upto(t))
                        pool.sem_inc(pool_steps, 1)
                        for side in range(2):
                            nc.gpsimd.indirect_dma_start(
                                e[side][:, t.slot, :], None, x_dram,
                                bass.IndirectOffsetOnAxis(ap=cur[side][:, t.slot:t.slot + 1], axis=0))\
                                .then_inc(landed[side].sem(t), 16)

                    in_steps(pool, ET, [(0, gather)])

                @block.scalar
                def _(act):
                    def high(t):
                        act.wait_ge(turned.sem, turned.upto(t))
                        if t.has(2):
                            act.wait_ge(product_done.sem, product_done.upto(t, 2))
                        for side in range(2):
                            last = nc.scalar.activation(hi[side][:, t.half], turned_bank[side][:], ACT.Copy)
                        last.then_inc(high_done.sem, 1)

                    def copy_q(t):
                        act.wait_ge(q_product_done.sem, q_product_done.upto(t))
                        if t.has(2):
                            act.wait_ge(qk_done.sem, qk_done.upto(t, 2))
                        nc.scalar.activation(q[:, t.half, :], banks["q"][t.half][:], ACT.Copy,
                                             scale=float(FH) ** -0.5).then_inc(q_copied.sem, 1)

                    def copy_v(t):
                        act.wait_ge(product_done.sem, product_done.upto(t))
                        nc.scalar.activation(v_all[:, bass.ds(t.times(D), D)], banks["v"][t.half][:], ACT.Copy)\
                            .then_inc(v_copied.sem, 1)

                    in_steps(act, ET, [(0, high), (2, copy_q), (2, copy_v)])

                @block.vector
                def _(dve):
                    def low(t):
                        dve.wait_ge(high_done.sem, high_done.upto(t))
                        if t.has(2):
                            dve.wait_ge(product_done.sem, product_done.upto(t, 2))
                        for side in range(2):
                            last = nc.vector.tensor_tensor(lo[side][:, t.half], turned_bank[side][:],
                                                           hi[side][:, t.half].bitcast(F32), ALU.subtract)
                        last.then_inc(low_done.sem, 1)

                    def score(t):
                        dve.wait_ge(product_done.sem, product_done.upto(t))
                        dve.wait_ge(q_copied.sem, q_copied.upto(t))
                        if t.has(2):
                            dve.wait_ge(scored.sem, scored.upto(t, 2))
                        nc.vector.tensor_tensor(qk[:, t.half, :], banks["k"][t.half][:], q[:, t.half, :], ALU.mult)\
                            .then_inc(qk_done.sem, 1)
                        dve.wait_ge(qk_done.sem, qk_done.upto(t))
                        nc.vector.tensor_reduce(scores[:, bass.ds(t.times(HEADS), HEADS)],
                                                qk[:, t.half, :].rearrange("p (h f) -> p h f", h=HEADS),
                                                AX_X, ALU.add).then_inc(scored.sem, 1)

                    in_steps(dve, ET, [(0, low), (2, score)])

                @block.tensor
                def _(pe):
                    def turn(t):
                        for side in range(2):
                            pe.wait_ge(landed[side].sem(t), landed[side].landed(t))
                        if t.has(1):
                            pe.wait_ge(low_done.sem, low_done.upto(t, 1))
                        for side in range(2):
                            for c in range(DC):
                                last = nc.tensor.transpose(turned_bank[side][:, c, :],
                                                           e[side][:, t.slot, c * P:(c + 1) * P], ident[:])
                        last.then_inc(turned.sem, 1)

                    def product(t):
                        pe.wait_ge(low_done.sem, low_done.upto(t))
                        if t.has(2):
                            pe.wait_ge(q_copied.sem, q_copied.upto(t, 2))
                            pe.wait_ge(qk_done.sem, qk_done.upto(t, 2))
                            pe.wait_ge(v_copied.sem, v_copied.upto(t, 2))
                        split_product(banks["q"][t.half][:], hi[0][:, t.half], lo[0][:, t.half], Q_SLOT)\
                            .then_inc(q_product_done.sem, 1)
                        split_product(banks["k"][t.half][:], hi[1][:, t.half], lo[1][:, t.half], K_SLOT)
                        split_product(banks["v"][t.half][:], hi[1][:, t.half], lo[1][:, t.half], V_SLOT)\
                            .then_inc(product_done.sem, 1)

                    in_steps(pe, ET, [(0, turn), (1, product)])

            for count in (turned, high_done, low_done, product_done):
                count.close(ET)
            gathered.close(ET)
            gathered2.close(ET)

        def softmax_terms(scores, exps):
            with ExitStack() as ph:
                by_head = sb("by_head", [HEADS, EP], F32, ph)
                penalty = sb("penalty", [HEADS, EP + 1], F32, ph)
                most = sb("most", [HEADS, EP], F32, ph)
                PER = 4
                head_bank = [pb(f"ph{k}", [HEADS, PER * P], F32, ph) for k in range(2)]
                exp_bank = pb("p_exp", [P, ET * HEADS], F32, ph)
                heads_turned = sem("heads_turned")
                heads_copied = sem("heads_copied")
                penalty_steps = sem("penalty_steps")
                most_steps = sem("most_steps")
                shifted = sem("shifted")
                exp_done = sem("exp_done")
                exps_turned = sem("exps_turned")
                exps_copied = sem("exps_copied")
                block = ph.enter_context(nc.Block())
                groups = range(0, ET, PER)

                @block.tensor
                def _(pe):
                    for n, t0 in enumerate(groups):
                        if n >= 2:
                            pe.wait_ge(heads_copied, n - 1)
                        for k in range(PER):
                            t = t0 + k
                            last = nc.tensor.transpose(head_bank[n % 2][:, k * P:(k + 1) * P],
                                                       scores[:, t * HEADS:(t + 1) * HEADS], ident[:])
                        last.then_inc(heads_turned, 1)
                    pe.wait_ge(exp_done, 1)
                    for t in range(ET):
                        last = nc.tensor.transpose(exp_bank[:, t * HEADS:(t + 1) * HEADS],
                                                   by_head[:, t * P:(t + 1) * P], ident[0:HEADS, 0:HEADS])
                    last.then_inc(exps_turned, 1)

                @block.scalar
                def _(act):
                    for n, t0 in enumerate(groups):
                        act.wait_ge(heads_turned, n + 1)
                        nc.scalar.activation(by_head[:, t0 * P:(t0 + PER) * P], head_bank[n % 2][:], ACT.Copy)\
                            .then_inc(heads_copied, 1)
                    act.wait_ge(shifted, 1)
                    nc.scalar.activation(by_head[:], by_head[:], ACT.Exp).then_inc(exp_done, 1)

                @block.vector
                def _(dve):
                    nc.vector.memset(penalty[:, EP:EP + 1], -BIG)
                    nc.vector.tensor_scalar(penalty[:, 0:EP], same_run[0:HEADS, :], BIG, -BIG, ALU.mult, ALU.add)\
                        .then_inc(penalty_steps, 1)
                    dve.wait_ge(penalty_steps, 1)
                    dve.wait_ge(heads_copied, len(groups))
                    nc.vector.tensor_tensor_scan(most[:], penalty[:, 0:EP], by_head[:], 0.0, ALU.add, ALU.max)\
                        .then_inc(most_steps, 1)
                    dve.wait_ge(most_steps, 1)
                    nc.vector.tensor_tensor_scan(most[:, ::-1], penalty[:, EP:0:-1], most[:, ::-1], 0.0,
                                                 ALU.add, ALU.max).then_inc(most_steps, 1)
                    dve.wait_ge(most_steps, 2)
                    nc.vector.tensor_tensor(by_head[:], by_head[:], most[:], ALU.subtract).then_inc(shifted, 1)
                    dve.wait_ge(exps_turned, 1)
                    nc.vector.tensor_copy(exps[:], exp_bank[:]).then_inc(exps_copied, 1)

        def weighted_sums(v_all, exps):
            with ExitStack() as ph:
                sorted_src = sb("sorted_src", [P, EP + 1], F32, ph)
                only_last = sb("only_last", [P, 1], F32, ph)
                same = sb("same", [P, 2, P], F32, ph)
                carry = sb("carry", [P, 2, P], F32, ph)
                ev = sb("ev", [P, 2, D], F32, ph)
                sums = sb("sums", [P, 2, D + HEADS], F32, ph)
                den = sb("den", [P, 2, HEADS], F32, ph)
                rows = sb("rows3", [P, UNROLL, D], F32, ph)
                sum_bank = [pb(f"p_sum{k}", [P, D], F32, ph) for k in range(2)]
                den_bank = [pb(f"p_den{k}", [P, HEADS], F32, ph) for k in range(2)]
                src_row_in = sem("src_row_in")
                matched = Count(sem("matched"))
                weighed = Count(sem("weighed"))
                own_done = Count(sem("own_done"))
                totals_done = Count(sem("totals_done"))
                totals_copied = Count(sem("totals_copied"), 2)
                den_kept = Count(sem("den_kept"))
                den_done = Count(sem("den_done"))
                block = ph.enter_context(nc.Block())

                @block.sync
                def _(sp):
                    sp.dma_start(sorted_src[:], sorted_src_row[0, :].partition_broadcast(P)).then_inc(src_row_in, 16)

                    def store(t):
                        sp.wait_ge(rows_done.sem, rows_done.upto(t))
                        sp.dma_start(neigh_rows[bass.ds(t.times(P), P), :], rows[:, t.slot, :])\
                            .then_inc(rows_stored.sem(t), 16)

                    in_steps(sp, ET, [(0, store)])
                    for s, v in rows_stored.used(ET):
                        sp.wait_ge(s, v)

                @block.vector
                def _(dve):
                    nc.vector.tensor_copy(only_last[:], ident[:, P - 1:P])
                    dve.wait_ge(src_row_in, 16)

                    def match(t):
                        if t.has(2):
                            dve.wait_ge(own_done.sem, own_done.upto(t, 2))
                            dve.wait_ge(totals_done.sem, totals_done.upto(t, 2))
                        mine = sorted_src[:, bass.ds(t.times(P, 1), P)]
                        nc.vector.tensor_scalar(same[:, t.half, :], mine, src_at[:, bass.ds(t.times(1), 1)], None,
                                                ALU.is_equal)
                        nc.vector.tensor_scalar(carry[:, t.half, :], mine, sorted_src[:, bass.ds(t.times(P), 1)],
                                                ident[:, P - 1:P], ALU.is_equal, ALU.mult).then_inc(matched.sem, 1)

                    def weigh(t):
                        terms = exps[:, bass.ds(t.times(HEADS), HEADS)].unsqueeze(2).to_broadcast([P, HEADS, FH])
                        nc.vector.tensor_tensor(ev[:, t.half, :].rearrange("p (h f) -> p h f", h=HEADS),
                                                v_all[:, bass.ds(t.times(D), D)].rearrange("p (h f) -> p h f", h=HEADS),
                                                terms, ALU.mult).then_inc(weighed.sem, 1)

                    def divide(t):
                        dve.wait_ge(totals_copied.sem, totals_copied.upto(t))
                        if t.has(2):
                            dve.wait_ge(rows_done.sem, rows_done.upto(t, 2))
                        nc.vector.tensor_scalar(den[:, t.half, :], sums[:, t.half, D:D + HEADS], 1e-30, None, ALU.max)\
                            .then_inc(den_kept.sem, 1)
                        dve.wait_ge(den_kept.sem, den_kept.upto(t))
                        nc.vector.reciprocal(den[:, t.half, :], den[:, t.half, :]).then_inc(den_done.sem, 1)
                        dve.wait_ge(den_done.sem, den_done.upto(t))
                        if t.has(UNROLL):
                            dve.wait_ge(rows_stored.sem(t), rows_stored.landed(t, 1))
                        nc.vector.tensor_tensor(rows[:, t.slot, :].rearrange("p (h f) -> p h f", h=HEADS),
                                                sum_bank[t.half][:].rearrange("p (h f) -> p h f", h=HEADS),
                                                den[:, t.half, :].unsqueeze(2).to_broadcast([P, HEADS, FH]), ALU.mult)\
                            .then_inc(rows_done.sem, 1)

                    in_steps(dve, ET, [(0, match), (0, weigh), (2, divide)])

                @block.tensor
                def _(pe):
                    def own(t):
                        pe.wait_ge(matched.sem, matched.upto(t))
                        pe.wait_ge(weighed.sem, weighed.upto(t))
                        if t.has(2):
                            pe.wait_ge(rows_done.sem, rows_done.upto(t, 2))
                            pe.wait_ge(totals_copied.sem, totals_copied.upto(t, 2))
                        alone = not t.has(1)
                        nc.tensor.matmul(sum_bank[t.half][:], same[:, t.half, :], ev[:, t.half, :],
                                         start=True, stop=alone)
                        nc.tensor.matmul(den_bank[t.half][:], same[:, t.half, :],
                                         exps[:, bass.ds(t.times(HEADS), HEADS)], start=True, stop=alone)\
                            .then_inc(own_done.sem, 1)

                    def carried(t):
                        if not t.has(1):
                            pe.sem_inc(totals_done.sem, 1)
                            return
                        pe.wait_ge(totals_copied.sem, totals_copied.upto(t, 1))
                        nc.tensor.matmul(sum_bank[t.half][:], carry[:, t.half, :], sums[:, 1 - t.half, 0:D],
                                         start=False, stop=True)
                        nc.tensor.matmul(den_bank[t.half][:], carry[:, t.half, :], sums[:, 1 - t.half, D:D + HEADS],
                                         start=False, stop=True).then_inc(totals_done.sem, 1)

                    in_steps(pe, ET, [(0, own), (1, carried)])

                @block.scalar
                def _(act):
                    def copy_sums(t):
                        act.wait_ge(own_done.sem, own_done.upto(t))
                        act.wait_ge(totals_done.sem, totals_done.upto(t))
                        if t.has(2):
                            act.wait_ge(den_kept.sem, den_kept.upto(t, 2))
                        nc.scalar.activation(sums[:, t.half, 0:D], sum_bank[t.half][:], ACT.Copy)\
                            .then_inc(totals_copied.sem, 1)
                        nc.scalar.activation(sums[:, t.half, D:D + HEADS], den_bank[t.half][:], ACT.Copy)\
                            .then_inc(totals_copied.sem, 1)

                    in_steps(act, ET, [(0, copy_sums)])

            rows_done.close(ET)
            rows_stored.close(ET)

        edge_phase(0, x, 0, (b_self0, b_neigh0), [(w_neigh1, 2)])
        node_phase(0, x, values[0], 1, [(w_self1, 0)])
        edge_phase(1, values[0], 2, (b_self1, b_neigh1), [(w_neigh2, 1)])
        Q_SLOT, K_SLOT, V_SLOT = 2, 0, 1
        node_phase(1, values[0], values[1], 0, [(w_qkv[:, 0:D], Q_SLOT)])
        edge_phase(2, values[1], 1, (), [(w_qkv[:, D:2 * D], K_SLOT)])
        residual_phase(2, values[1], values[2], [(w_qkv[:, 2 * D:3 * D], V_SLOT)])
        attention(values[2])
        residual_phase(3, values[2], out, [])


_INS = ["x", "src", "dst", "edge_weight", "L0_gnn_W_self", "L0_gnn_b_self", "L0_gnn_W_neigh", "L0_gnn_b_neigh",
        "L0_gnn_ln_gamma", "L0_gnn_ln_beta", "L1_gnn_self_w", "L1_gnn_self_b", "L1_gnn_neigh_w", "L1_gnn_neigh_b",
        "L2_gnn_weight", "L3_gnn_W"]
_TURNED = {"L0_gnn_W_self", "L0_gnn_W_neigh", "L1_gnn_self_w", "L1_gnn_neigh_w", "L2_gnn_weight"}


def kernel(**inputs):
    import numpy as np
    import concourse.bacc as bacc
    from concourse.bass_utils import run_bass_kernel_spmd

    nc = bacc.Bacc("TRN2", target_bir_lowering=False, num_devices=1)
    arrays, args = {}, []
    for name in _INS:
        a = np.asarray(inputs[name])
        a = np.ascontiguousarray(a.T if name in _TURNED else a)
        arrays[f"in_{name}"] = a
        args.append(nc.dram_tensor(f"in_{name}", a.shape, mybir.dt.from_np(a.dtype), kind="ExternalInput").ap())
    n, d = inputs["x"].shape
    out = nc.dram_tensor("out_x", [n, d], F32, kind="ExternalOutput").ap()
    build(nc, *args, out)
    result = run_bass_kernel_spmd(nc, [arrays], core_ids=[0])
    return result.results[0]["out_x"]
```

```python
from contextlib import ExitStack

import concourse.bass as bass
from concourse import mybir

F32 = mybir.dt.float32
F32R = mybir.dt.float32r
BF16 = mybir.dt.bfloat16
I32 = mybir.dt.int32
ALU = mybir.AluOpType
ACT = mybir.ActivationFunctionType
AX_X = mybir.AxisListType.X

P = 128
UNROLL = 4


class Tile:

    def __init__(self, loop, offset):
        self.loop, self.offset = loop, offset
        self.slot = offset % UNROLL
        self.half = offset % 2

    def times(self, size, add=0):
        if isinstance(self.loop, int):
            return self.offset * size + add
        return self.loop * (UNROLL * size) + (self.offset * size + add)

    def turn(self, size):
        whole = (self.offset // UNROLL + 1) * size
        return whole if isinstance(self.loop, int) else self.loop * size + whole

    def has(self, back):
        return not isinstance(self.loop, int) or self.offset >= back


class Count:

    def __init__(self, sem, per=1):
        self.sem, self.per, self.base = sem, per, 0

    def upto(self, tile, back=0):
        return tile.times(self.per, self.base + self.per * (1 - back))

    def all(self, n):
        return self.base + self.per * n

    def close(self, n):
        self.base += self.per * n


class Slots:

    def __init__(self, sems):
        self.sems, self.bases = sems, [0] * UNROLL

    def sem(self, tile):
        return self.sems[tile.slot]

    def landed(self, tile, back=0):
        return tile.turn(16) + (self.bases[tile.slot] - 16 * back)

    def used(self, n):
        return [(self.sems[k], self.bases[k] + 16 * len(range(k, n, UNROLL))) for k in range(UNROLL)]

    def close(self, n):
        self.bases = [v for _, v in self.used(n)]


def in_steps(eng, n, stages):
    deepest = max(lag for lag, _ in stages)
    first = -(-(deepest + UNROLL) // UNROLL)
    last = n // UNROLL

    def straight(steps):
        for s in steps:
            for lag, stage in stages:
                if 0 <= s - lag < n:
                    stage(Tile(0, s - lag))

    if last - first < 2:
        straight(range(n + deepest))
        return
    straight(range(first * UNROLL))
    with eng.Fori(first, last) as i:
        for j in range(UNROLL):
            for lag, stage in stages:
                stage(Tile(i, j - lag))
    straight(range(last * UNROLL, n + deepest))


def build(nc, x, src, dst, edge_weight, w_self0, b_self0, w_neigh0, b_neigh0, gamma, beta,
          w_self1, b_self1, w_neigh1, b_neigh1, w_neigh2, w_qkv, out):
    N, D = x.shape
    E = src.shape[0]
    DC = D // P
    NT = -(-N // P)
    NREST = N - (NT - 1) * P
    PAIRS = N // (2 * P)
    PAIR_REST = N - PAIRS * 2 * P
    ET = -(-E // P)
    EP = ET * P
    ER = E // ET
    HEADS = 8
    FH = D // HEADS
    PAD_NODE = NT * P - 1
    NOWHERE = 4 * EP
    EPS = 1e-5
    BIG = 3.0e38
    NESTED_VARIANCE = [(1.0, EPS), (1.0 + EPS, EPS ** 2), (1.0 + EPS + EPS ** 2, EPS ** 3)]
    assert ER * ET == E and ER <= P and PAD_NODE >= N and D == DC * P and NT <= P and NT * P < 32768
    assert PAIRS == ET - 1 and 0 < PAIR_REST <= P

    records = nc.dram_tensor("records", [EP + 2, 4], F32, kind="Internal").ap()
    same_run_row = nc.dram_tensor("same_run_row", [1, EP], BF16, kind="Internal").ap()
    sorted_src_row = nc.dram_tensor("sorted_src_row", [1, EP + 1], F32, kind="Internal").ap()
    neigh_rows = nc.dram_tensor("neigh_rows", [EP + 1, D], F32, kind="Internal").ap()
    values = [nc.dram_tensor(f"values{i}", [N, D], F32, kind="Internal").ap() for i in range(3)]

    ctx = ExitStack()
    with ctx:
        def sb(name, shape, dt, where=ctx):
            return where.enter_context(nc.sbuf_tensor(name, shape, dt))

        def pb(name, shape, dt, where):
            return where.enter_context(nc.psum_tensor(name, shape, dt))

        def sem(name):
            return ctx.enter_context(nc.semaphore(name))

        def slots(name):
            return Slots([sem(f"{name}{k}") for k in range(UNROLL)])

        ident = sb("ident", [P, P], F32)
        src_at = sb("src_at", [P, ET], F32)
        dst_idx = sb("dst_idx", [P, ET], I32)
        src_idx = sb("src_idx", [P, ET], I32)
        weight_at = sb("weight_at", [P, ET], F32)
        invdeg_at = sb("invdeg_at", [P, ET], F32)
        last_idx = sb("last_idx", [P, ET], I32)
        node_idx = sb("node_idx", [P, NT], I32)
        eps = sb("eps", [P, 1], F32)
        var_factor = sb("var_factor", [P, 3], F32)
        var_term = sb("var_term", [P, 3], F32)
        mean_factor = sb("mean_factor", [P, 1], F32)
        last_scale = sb("last_scale", [P, NT], F32)
        same_run = sb("same_run", [P, EP], BF16)
        w_hi = [sb(f"w_hi{k}", [P, DC, D], F32R) for k in range(3)]
        w_lo = [sb(f"w_lo{k}", [P, DC, D], F32R) for k in range(3)]

        pool_steps = sem("pool_steps")
        rows_in = sem("rows_in")
        weight_landed = sem("weight_landed")
        weight_hi_done = sem("weight_hi_done")
        weight_lo_done = sem("weight_lo_done")
        weights_split = [0]

        def weight_split_steps(where, jobs):
            stage = sb(f"w_stage_{weights_split[0]}", [P, len(jobs), DC, D], F32, where)
            base = weights_split[0]
            weights_split[0] += len(jobs)

            def load(sp):
                for k, (w, _) in enumerate(jobs):
                    sp.dma_start(stage[:, k], w.rearrange("(c p) n -> p c n", p=P)).then_inc(weight_landed, 16)

            def high(act):
                act.wait_ge(weight_landed, 16 * (base + len(jobs)))
                for k, (_, slot) in enumerate(jobs):
                    nc.scalar.activation(w_hi[slot][:], stage[:, k], ACT.Copy).then_inc(weight_hi_done, 1)

            def low(dve):
                for k, (_, slot) in enumerate(jobs):
                    dve.wait_ge(weight_hi_done, base + k + 1)
                    nc.vector.tensor_tensor(w_lo[slot][:], stage[:, k], w_hi[slot][:].bitcast(F32),
                                            ALU.subtract).then_inc(weight_lo_done, 1)

            return load, high, low

        with ExitStack() as ph:
            edge_ints = sb("edge_ints", [P, 2, ET], I32, ph)
            weight_in = sb("weight_in", [P, ET], F32, ph)
            src_all_i = sb("src_all_i", [P, E], I32, ph)
            src_all = sb("src_all", [P, EP], F32, ph)
            rec = sb("rec", [P, ET, 4], F32, ph)
            hi_i = sb("hi_i", [P, ET], I32, ph)
            lo_i = sb("lo_i", [P, ET], I32, ph)
            hi_of = sb("hi_of", [P, ET], F32, ph)
            lo_of = sb("lo_of", [P, ET], F32, ph)
            iota_i = sb("iota_i", [P, P], I32, ph)
            iota_part_i = sb("iota_part_i", [P, 1], I32, ph)
            iota = sb("iota", [P, P], F32, ph)
            iota_part = sb("iota_part", [P, 1], F32, ph)
            ident_b = sb("ident_b", [P, P], BF16, ph)
            earlier = sb("earlier", [P, P], F32, ph)
            below = sb("below", [P, P], F32, ph)
            ones_row = sb("ones_row", [P, P], F32, ph)
            hot_lo = sb("hot_lo", [P, ET * P], BF16, ph)
            hot_hi = sb("hot_hi", [P, ET * P], BF16, ph)
            hist = sb("hist", [P, (ET + 1) * P], F32, ph)
            prefix = sb("prefix", [P, P], F32, ph)
            row_offset = sb("row_offset", [P, 1], F32, ph)
            row_offset1 = sb("row_offset1", [P, 1], F32, ph)
            base = sb("base", [P, P], F32, ph)
            empty = sb("empty", [P, P], F32, ph)
            last_pos = sb("last_pos", [P, P], F32, ph)
            table = sb("table", [P, 2, 2 * P], F32, ph)
            hot_hi_t = sb("hot_hi_t", [P, 2, P], F32, ph)
            rank_a = sb("rank_a", [P, ET], F32, ph)
            rank_b = sb("rank_b", [P, ET], F32, ph)
            rank_i = sb("rank_i", [P, ET], I32, ph)
            junk = sb("junk_prep", [P, 3, P], F32, ph)
            cur_rank = sb("cur_rank", [P, UNROLL], I32, ph)
            cur_rec = sb("cur_rec", [P, UNROLL, 4], F32, ph)
            guard = sb("guard", [1, 4], F32, ph)
            back = sb("back", [ET, P + 2, 4], F32, ph)
            same_t = sb("same_t", [ET, P], BF16, ph)
            src_t = sb("src_t", [ET, P], F32, ph)
            same_next = sb("same_next", [ET, P], F32, ph)
            last_t = sb("last_t", [ET, P], F32, ph)
            col_t = sb("col_t", [ET, 3, P], F32, ph)
            p_hist = [pb(f"p_hist{k}", [P, P], F32, ph) for k in range(2)]
            p_hot = [pb(f"p_hot{k}", [P, P], BF16, ph) for k in range(2)]
            p_look = [pb(f"p_look{k}", [P, 2 * P], F32, ph) for k in range(2)]
            p_misc = pb("p_misc", [P, 512], F32, ph)

            edges_in = sem("edges_in")
            edge_clear = sem("edge_clear")
            iotas = sem("iotas")
            consts = sem("consts")
            fields = sem("fields")
            hot_done = Count(sem("hot_done"))
            hist_mm = Count(sem("hist_mm"))
            hist_sum = Count(sem("hist_sum"))
            chain = sem("prep_chain")
            prefix_done = sem("prefix_done")
            last_pos_done = sem("last_pos_done")
            offsets_mm = sem("offsets_mm")
            nodes_mm = sem("nodes_mm")
            table_done = Count(sem("table_done"))
            hot_turned = Count(sem("hot_turned"))
            hot_copied = Count(sem("hot_copied"))
            looked = Count(sem("looked"))
            ranked = Count(sem("ranked"))
            rank_summed = Count(sem("rank_summed"))
            picked = Count(sem("picked"), 2)
            scattered = slots("scattered")
            guard_out = sem("guard_out")
            back_in = sem("back_in")
            rows_ready = sem("rows_ready")
            rows_out = sem("rows_out")
            cols_mm = sem("cols_mm")
            cols_ready = sem("cols_ready")
            w_load, w_high, w_low = weight_split_steps(ph, [(w_neigh0, 0), (w_self0, 1)])
            block = ph.enter_context(nc.Block())

            @block.sync
            def _(sp):
                sp.wait_ge(edge_clear, 1)
                sp.dma_start(edge_ints[0:ER, 0, :], src.rearrange("(p t) -> p t", t=ET)).then_inc(edges_in, 16)
                sp.dma_start(edge_ints[0:ER, 1, :], dst.rearrange("(p t) -> p t", t=ET)).then_inc(edges_in, 16)
                sp.dma_start(weight_in[0:ER, :], edge_weight.rearrange("(p t) -> p t", t=ET)).then_inc(edges_in, 16)
                sp.dma_start(src_all_i[:], src.partition_broadcast(P)).then_inc(edges_in, 16)
                w_load(sp)
                sp.wait_ge(edge_clear, 2)
                sp.dma_start(records[0:1, :], guard[:]).then_inc(guard_out, 16)
                sp.dma_start(records[EP + 1:EP + 2, :], guard[:]).then_inc(guard_out, 16)
                sp.wait_ge(guard_out, 32)
                for s, v in scattered.used(ET):
                    sp.wait_ge(s, v)
                for t in range(0, ET, 8):
                    sp.dma_start(back[t:t + 8], bass.AP(records.tensor, 4 * P * t, [[4 * P, 8], [1, 4 * (P + 2)]])
                                 .rearrange("t (l f) -> t l f", f=4)).then_inc(back_in, 16)
                sp.wait_ge(rows_ready, 2)
                sp.dma_start(same_run_row.rearrange("o (t l) -> (o t) l", l=P), same_t[:]).then_inc(rows_out, 16)
                sp.dma_start(sorted_src_row[:, 1:EP + 1].rearrange("o (t l) -> (o t) l", l=P), src_t[:])\
                    .then_inc(rows_out, 16)
                sp.dma_start(sorted_src_row[:, 0:1], guard[:, 0:1]).then_inc(rows_out, 16)
                sp.wait_ge(rows_out, 48)
                sp.dma_start(same_run[:], same_run_row[0, :].partition_broadcast(P)).then_inc(rows_in, 16)

            @block.gpsimd
            def _(pool):
                nc.gpsimd.iota(iota_i[:], [[1, P]], base=0, channel_multiplier=0).then_inc(iotas, 1)
                nc.gpsimd.iota(iota_part_i[:], [[0, 1]], base=0, channel_multiplier=1).then_inc(iotas, 1)

                def pick(t):
                    pool.wait_ge(rank_summed.sem, rank_summed.upto(t))
                    if t.has(UNROLL):
                        pool.wait_ge(scattered.sem(t), scattered.landed(t, 1))
                    nc.gpsimd.tensor_copy(cur_rank[:, t.slot:t.slot + 1], rank_i[:, bass.ds(t.times(1), 1)])\
                        .then_inc(picked.sem, 1)
                    nc.gpsimd.tensor_copy(cur_rec[:, t.slot, :], rec[:, bass.ds(t.times(1), 1), :])\
                        .then_inc(picked.sem, 1)
                    pool.wait_ge(picked.sem, picked.upto(t))
                    pool.sem_inc(pool_steps, 1)
                    nc.gpsimd.indirect_dma_start(
                        records, bass.IndirectOffsetOnAxis(ap=cur_rank[:, t.slot:t.slot + 1], axis=0),
                        cur_rec[:, t.slot, :], None).then_inc(scattered.sem(t), 16)

                in_steps(pool, ET, [(0, pick)])

            @block.scalar
            def _(act):
                w_high(act)

                def copy_hot(t):
                    act.wait_ge(hot_turned.sem, hot_turned.upto(t))
                    if t.has(2):
                        act.wait_ge(looked.sem, looked.upto(t, 2))
                    nc.scalar.activation(hot_hi_t[:, t.half, :], p_hot[t.half][:], ACT.Copy).then_inc(hot_copied.sem, 1)

                in_steps(act, ET, [(0, copy_hot)])

            @block.vector
            def _(dve):
                links = [0]

                def link(ins):
                    links[0] += 1
                    ins.then_inc(chain, 1)
                    dve.wait_ge(chain, links[0])

                nc.vector.memset(edge_ints[:, 0, :], PAD_NODE)
                nc.vector.memset(edge_ints[:, 1, :], 0)
                nc.vector.memset(weight_in[:], 0.0).then_inc(edge_clear, 1)
                nc.vector.memset(guard[:], -1.0).then_inc(edge_clear, 1)
                nc.vector.memset(src_all[:, E:EP], float(PAD_NODE))
                nc.vector.memset(ones_row[:], 1.0)
                nc.vector.memset(eps[:], EPS)
                nc.vector.memset(mean_factor[:], -1.0 / D)
                for k, (factor, term) in enumerate(NESTED_VARIANCE):
                    nc.vector.memset(var_factor[:, k:k + 1], factor / D)
                    nc.vector.memset(var_term[:, k:k + 1], term)
                link(nc.vector.memset(hist[:, 0:P], 0.0))
                dve.wait_ge(iotas, 2)
                nc.vector.tensor_copy(iota[:], iota_i[:])
                link(nc.vector.tensor_copy(iota_part[:], iota_part_i[:]))
                nc.vector.tensor_scalar(ident[:], iota[:], iota_part[:, 0:1], None, ALU.is_equal)
                nc.vector.tensor_scalar(ident_b[:], iota[:], iota_part[:, 0:1], None, ALU.is_equal).then_inc(consts, 1)
                nc.vector.tensor_scalar(earlier[:], iota[:], iota_part[:, 0:1], None, ALU.is_lt)
                nc.vector.tensor_scalar(below[:], iota[:], iota_part[:, 0:1], None, ALU.is_gt).then_inc(consts, 1)
                dve.wait_ge(edges_in, 64)
                nc.vector.tensor_copy(rec[:, :, 0], edge_ints[:, 0, :])
                nc.vector.tensor_copy(rec[:, :, 1], edge_ints[:, 1, :])
                nc.vector.tensor_copy(rec[:, :, 2], weight_in[:])
                nc.vector.tensor_copy(src_all[:, 0:E], src_all_i[:])
                nc.vector.tensor_scalar(hi_i[:], edge_ints[:, 0, :], 7, None, ALU.arith_shift_right)
                link(nc.vector.tensor_scalar(lo_i[:], edge_ints[:, 0, :], P - 1, None, ALU.bitwise_and))
                nc.vector.tensor_copy(hi_of[:], hi_i[:])
                link(nc.vector.tensor_copy(lo_of[:], lo_i[:]))

                def one_hot(t):
                    at = bass.ds(t.times(P), P)
                    nc.vector.tensor_scalar(hot_lo[:, at], iota[:], lo_of[:, bass.ds(t.times(1), 1)], None, ALU.is_equal)
                    nc.vector.tensor_scalar(hot_hi[:, at], iota[:], hi_of[:, bass.ds(t.times(1), 1)], None,
                                            ALU.is_equal).then_inc(hot_done.sem, 1)

                def add_hist(t):
                    dve.wait_ge(hist_mm.sem, hist_mm.upto(t))
                    if t.has(1):
                        dve.wait_ge(hist_sum.sem, hist_sum.upto(t, 1))
                    nc.vector.tensor_tensor(hist[:, bass.ds(t.times(P, P), P)], p_hist[t.half][:],
                                            hist[:, bass.ds(t.times(P), P)], ALU.add).then_inc(hist_sum.sem, 1)

                in_steps(dve, ET, [(0, one_hot), (2, add_hist)])
                total = hist[:, ET * P:(ET + 1) * P]
                dve.wait_ge(hist_sum.sem, hist_sum.all(ET))
                nc.vector.tensor_tensor_scan(prefix[:], ones_row[:], total, 0.0, ALU.mult, ALU.add)\
                    .then_inc(prefix_done, 1)
                dve.wait_ge(prefix_done, 1)
                dve.wait_ge(offsets_mm, 1)
                nc.vector.tensor_scalar(row_offset[:], p_misc[:, 0:1], 1.0, None, ALU.add)
                nc.vector.tensor_scalar(row_offset1[:], p_misc[:, 0:1], -1.0, None, ALU.add)
                link(nc.vector.tensor_scalar(empty[:], total, 0.0, float(NOWHERE), ALU.is_equal, ALU.mult))
                nc.vector.scalar_tensor_tensor(last_pos[:], prefix[:], row_offset1[:, 0:1], empty[:], ALU.add, ALU.add)\
                    .then_inc(last_pos_done, 1)
                nc.vector.tensor_copy(table[:, 0, P:2 * P], total)
                nc.vector.tensor_copy(table[:, 1, P:2 * P], total)
                link(nc.vector.scalar_tensor_tensor(base[:], prefix[:], row_offset[:, 0:1], total, ALU.add, ALU.subtract))

                def make_table(t):
                    if t.has(2):
                        dve.wait_ge(looked.sem, looked.upto(t, 2))
                    nc.vector.tensor_tensor(table[:, t.half, 0:P], base[:], hist[:, bass.ds(t.times(P), P)],
                                            ALU.add).then_inc(table_done.sem, 1)

                def rank(t):
                    column = bass.ds(t.times(1), 1)
                    same = src_all[:].rearrange("p (q t) -> p q t", t=ET)[:, :, column]
                    if t.has(1):
                        dve.wait_ge(ranked.sem, ranked.upto(t, 1))
                    nc.vector.scalar_tensor_tensor(junk[:, 0, :], same.rearrange("p q o -> p (q o)"), rec[:, column, 0],
                                                   earlier[:], ALU.is_equal, ALU.mult, accum_out=rank_b[:, column])
                    at = bass.ds(t.times(P), P)
                    dve.wait_ge(looked.sem, looked.upto(t))
                    nc.vector.scalar_tensor_tensor(junk[:, 1, :], p_look[t.half][:, 0:P], 1.0, hot_lo[:, at],
                                                   ALU.mult, ALU.mult, accum_out=rank_a[:, column])
                    nc.vector.scalar_tensor_tensor(junk[:, 2, :], p_look[t.half][:, P:2 * P], 1.0, hot_lo[:, at],
                                                   ALU.mult, ALU.mult, accum_out=rec[:, column, 3])\
                        .then_inc(ranked.sem, 1)

                def sum_rank(t):
                    column = bass.ds(t.times(1), 1)
                    dve.wait_ge(ranked.sem, ranked.upto(t))
                    nc.vector.tensor_tensor(rank_i[:, column], rank_a[:, column], rank_b[:, column], ALU.add)\
                        .then_inc(rank_summed.sem, 1)

                in_steps(dve, ET, [(0, make_table), (3, sum_rank), (2, rank)])
                dve.wait_ge(nodes_mm, 1)
                nc.vector.tensor_scalar(node_idx[:], p_misc[:, 128:128 + NT], float(EP), None, ALU.min)
                w_low(dve)
                dve.wait_ge(back_in, 16 * (ET // 8))
                nc.vector.tensor_tensor(same_t[:], back[:, 1:P + 1, 0], back[:, 0:P, 0], ALU.is_equal)\
                    .then_inc(rows_ready, 1)
                nc.vector.tensor_copy(src_t[:], back[:, 1:P + 1, 0]).then_inc(rows_ready, 1)
                for f in range(3):
                    last = nc.vector.tensor_copy(col_t[:, f, :], back[:, 1:P + 1, f + 1])
                link(nc.vector.tensor_tensor(same_next[:], back[:, 2:P + 2, 0], back[:, 1:P + 1, 0], ALU.is_equal))
                last = nc.vector.scalar_tensor_tensor(last_t[:], same_next[:], float(NOWHERE), back[:, 1:P + 1, 0],
                                                      ALU.mult, ALU.add)
                last.then_inc(rows_ready, 1)
                dve.wait_ge(cols_mm, 1)
                nc.vector.tensor_copy(last_idx[:], p_misc[:, 256 + 4 * ET:256 + 5 * ET])
                nc.vector.tensor_copy(src_at[:], p_misc[:, 256:256 + ET])
                nc.vector.tensor_scalar(src_idx[:], p_misc[:, 256:256 + ET], float(N - 1), None, ALU.min)
                nc.vector.tensor_copy(dst_idx[:], p_misc[:, 256 + ET:256 + 2 * ET])
                nc.vector.tensor_copy(weight_at[:], p_misc[:, 256 + 2 * ET:256 + 3 * ET])
                link(nc.vector.tensor_scalar(invdeg_at[:], p_misc[:, 256 + 3 * ET:256 + 4 * ET], 1.0, None, ALU.max))
                nc.vector.reciprocal(invdeg_at[:], invdeg_at[:]).then_inc(cols_ready, 1)

            @block.tensor
            def _(pe):
                def histogram(t):
                    at = bass.ds(t.times(P), P)
                    pe.wait_ge(hot_done.sem, hot_done.upto(t))
                    if t.has(2):
                        pe.wait_ge(hist_sum.sem, hist_sum.upto(t, 2))
                    nc.tensor.matmul(p_hist[t.half][:], hot_hi[:, at], hot_lo[:, at], start=True, stop=True)\
                        .then_inc(hist_mm.sem, 1)

                in_steps(pe, ET, [(0, histogram)])
                pe.wait_ge(consts, 2)
                pe.wait_ge(prefix_done, 1)
                nc.tensor.matmul(p_misc[:, 0:1], below[:], prefix[:, P - 1:P], start=True, stop=True)\
                    .then_inc(offsets_mm, 1)

                def turn(t):
                    pe.wait_ge(consts, 2)
                    if t.has(2):
                        pe.wait_ge(hot_copied.sem, hot_copied.upto(t, 2))
                    nc.tensor.transpose(p_hot[t.half][:], hot_hi[:, bass.ds(t.times(P), P)], ident_b[:])\
                        .then_inc(hot_turned.sem, 1)

                def look(t):
                    pe.wait_ge(hot_copied.sem, hot_copied.upto(t))
                    pe.wait_ge(table_done.sem, table_done.upto(t))
                    if t.has(2):
                        pe.wait_ge(ranked.sem, ranked.upto(t, 2))
                    nc.tensor.matmul(p_look[t.half][:], hot_hi_t[:, t.half, :], table[:, t.half, :],
                                     start=True, stop=True).then_inc(looked.sem, 1)

                in_steps(pe, ET, [(0, turn), (1, look)])
                pe.wait_ge(last_pos_done, 1)
                nc.tensor.transpose(p_misc[:, 128:256], last_pos[:], ident[:]).then_inc(nodes_mm, 1)
                pe.wait_ge(rows_ready, 3)
                for f, rows in enumerate((src_t[:], col_t[:, 0, :], col_t[:, 1, :], col_t[:, 2, :], last_t[:])):
                    last = nc.tensor.transpose(p_misc[:, 256 + f * ET:256 + (f + 1) * ET], rows, ident[0:ET, 0:ET])
                last.then_inc(cols_mm, 1)

        gathered = slots("gathered")
        gathered2 = slots("gathered2")
        index_picked = Count(sem("index_picked"))
        last_picked = Count(sem("last_picked"))
        own_picked = Count(sem("own_picked"))
        both_picked = Count(sem("both_picked"), 2)
        scaled = Count(sem("scaled"))
        turned = Count(sem("turned"))
        summed = Count(sem("summed"))
        high_done = Count(sem("high_done"))
        low_done = Count(sem("low_done"))
        product_done = Count(sem("product_done"))
        rows_done = Count(sem("rows_done"))
        rows_stored = slots("rows_stored")
        stored_twice = slots("stored_twice")
        rows_scattered = slots("rows_scattered")
        out_stored = slots("out_stored")
        consts_in = Count(sem("consts_in"), 16)
        consts_made = Count(sem("consts_made"))
        fill_stored = Count(sem("fill_stored"), 16)
        x_landed = slots("x_landed")
        filled = Count(sem("filled"))
        preact_done = Count(sem("preact_done"))
        y_done = Count(sem("y_done"))
        x_plus_beta = Count(sem("x_plus_beta"))
        scaled_gamma = Count(sem("scaled_gamma"))
        y2_done = Count(sem("y2_done"))

        class Norm:

            def __init__(self, name, nested=False):
                self.mean = Count(sem(f"{name}_mean"))
                self.squares = Count(sem(f"{name}_squares"))
                self.variance = Count(sem(f"{name}_variance")) if nested else None
                self.std = Count(sem(f"{name}_std"))
                self.rstd = Count(sem(f"{name}_rstd"))
                self.scale = Count(sem(f"{name}_scale"))
                self.applied = Count(sem(f"{name}_applied"))

            def close(self, n, counts=None):
                for count in counts or (self.mean, self.squares, self.std, self.rstd, self.scale, self.applied):
                    count.close(n)

        norm_inner = Norm("inner")
        norm_outer = Norm("outer", nested=True)
        applied_twice = Count(sem("applied_twice"))
        ratio_done = Count(sem("ratio_done"))
        out_scaled = Count(sem("out_scaled"), 2)
        SUM, NEG_MEAN, SQUARES, VARIANCE, STD, RSTD, SHIFT = 0, 1, 2, 3, 6, 9, 12
        STATS = 15

        def norm_steps(norm, y, y_ready, stats, junk, target, target_free, width=1):

            def column(t, k, w=1):
                return stats[:, t.slot, k:k + w]

            def mean(eng, t):
                eng.wait_ge(y_ready.sem, y_ready.upto(t))
                eng.tensor_tensor(column(t, NEG_MEAN), column(t, SUM), mean_factor[:], ALU.mult)\
                    .then_inc(norm.mean.sem, 1)

            def squares(act, t):
                act.wait_ge(norm.mean.sem, norm.mean.upto(t))
                nc.scalar.activation(junk[:, t.half, :], y[:, t.slot, :], ACT.Square, bias=column(t, NEG_MEAN),
                                     accum_out=column(t, SQUARES)).then_inc(norm.squares.sem, 1)

            def variance(dve, t):
                dve.wait_ge(norm.squares.sem, norm.squares.upto(t))
                nc.vector.scalar_tensor_tensor(column(t, VARIANCE, 3), var_factor[:], column(t, SQUARES), var_term[:],
                                               ALU.mult, ALU.add).then_inc(norm.variance.sem, 1)

            def std(act, t):
                if width == 3:
                    act.wait_ge(norm.variance.sem, norm.variance.upto(t))
                    nc.scalar.activation(column(t, STD, 3), column(t, VARIANCE, 3), ACT.Sqrt)\
                        .then_inc(norm.std.sem, 1)
                else:
                    act.wait_ge(norm.squares.sem, norm.squares.upto(t))
                    nc.scalar.activation(column(t, STD), column(t, SQUARES), ACT.Sqrt, bias=eps[:, 0:1],
                                         scale=1.0 / D).then_inc(norm.std.sem, 1)

            def rstd(dve, t):
                dve.wait_ge(norm.std.sem, norm.std.upto(t))
                nc.vector.reciprocal(column(t, RSTD, width), column(t, STD, width)).then_inc(norm.rstd.sem, 1)

            def shift(eng, t):
                eng.wait_ge(norm.rstd.sem, norm.rstd.upto(t))
                if width == 1:
                    shifted = eng.tensor_tensor(column(t, SHIFT), column(t, RSTD), column(t, NEG_MEAN), ALU.mult)
                else:
                    shifted = eng.tensor_scalar(column(t, SHIFT, width), column(t, RSTD, width), column(t, NEG_MEAN),
                                                None, ALU.mult)
                shifted.then_inc(norm.scale.sem, 1)

            def apply(act, t):
                act.wait_ge(norm.scale.sem, norm.scale.upto(t))
                target_free(act, t)
                nc.scalar.activation(target(t), y[:, t.slot, :], ACT.Identity, bias=column(t, SHIFT),
                                     scale=column(t, RSTD)).then_inc(norm.applied.sem, 1)

            steps = dict(mean=mean, squares=squares, variance=variance, std=std, rstd=rstd, shift=shift, apply=apply)
            return lambda name, eng: lambda t: steps[name](eng, t)

        def pick_index(pool, t, picked, cur, indices):
            nc.gpsimd.tensor_copy(cur[:, t.slot:t.slot + 1], indices[:, bass.ds(t.times(1), 1)])\
                .then_inc(picked.sem, 1)

        def index_ready(pool, t, picked):
            pool.wait_ge(picked.sem, picked.upto(t))
            pool.sem_inc(pool_steps, 1)

        def gather_rows(to, x_dram, cur, t, landed):
            nc.gpsimd.indirect_dma_start(to[:, t.slot, :], None, x_dram,
                                         bass.IndirectOffsetOnAxis(ap=cur[:, t.slot:t.slot + 1], axis=0))\
                .then_inc(landed.sem(t), 16)

        def scatter_steps(norm, cur, done, y_dram):
            def pick_last(t):
                if t.has(UNROLL):
                    nc.gpsimd.wait_ge(rows_scattered.sem(t), rows_scattered.landed(t, 1))
                pick_index(nc.gpsimd, t, last_picked, cur, last_idx)

            def scatter(t):
                nc.gpsimd.wait_ge(norm.applied.sem, norm.applied.upto(t))
                index_ready(nc.gpsimd, t, last_picked)
                nc.gpsimd.indirect_dma_start(
                    y_dram, bass.IndirectOffsetOnAxis(ap=cur[:, t.slot:t.slot + 1], axis=0),
                    done[:, t.slot, :], None, bounds_check=N - 1, oob_is_err=False).then_inc(rows_scattered.sem(t), 16)

            return pick_last, scatter

        def split_product(bank, hi, lo, slot, w_cols=slice(None)):
            for c in range(DC):
                for a, w in ((hi, w_hi), (hi, w_lo), (lo, w_hi)):
                    last = nc.tensor.matmul(bank, a[:, c, :], w[slot][:, c, w_cols],
                                            start=(c == 0 and a is hi and w is w_hi),
                                            stop=(c == DC - 1 and a is lo))
            return last

        def edge_phase(layer, x_dram, slot, biases, jobs, y_dram=None):
            by_weight, by_degree, to_nodes = layer == 2, layer == 0, y_dram is not None
            with ExitStack() as ph:
                e = sb(f"e{layer}", [P, UNROLL, D], F32, ph)
                cur = sb(f"cur_e{layer}", [P, UNROLL], I32, ph)
                hi = sb(f"edge_hi{layer}", [P, UNROLL, DC, P], F32R, ph)
                lo = sb(f"edge_lo{layer}", [P, UNROLL, DC, P], F32R, ph)
                rows = sb(f"rows{layer}", [P, UNROLL, D], F32, ph)
                bias_in = sb(f"bias_in_e{layer}", [P, 2, D], F32, ph)
                bias = sb(f"bias_e{layer}", [P, D], F32, ph)
                turned_bank = [pb(f"pt_e{layer}{k}", [P, DC, P], F32, ph) for k in range(2)]
                sums = sb(f"sums{layer}", [P, UNROLL, DC, P], F32, ph)
                product_bank = [pb(f"pp_e{layer}{k}", [P, D], F32, ph) for k in range(2)]
                if to_nodes:
                    own = sb(f"own{layer}", [P, UNROLL, D], F32, ph)
                    cur_own = sb(f"cur_own{layer}", [P, UNROLL], I32, ph)
                    cur_last = sb(f"cur_last{layer}", [P, UNROLL], I32, ph)
                    y = sb(f"y{layer}", [P, UNROLL, D], F32, ph)
                    junk = sb(f"junk_e{layer}", [P, 2, D], F32, ph)
                    stats = sb(f"stats{layer}", [P, UNROLL, STATS], F32, ph)

                    def rows_free(act, t):
                        if t.has(UNROLL):
                            act.wait_ge(rows_scattered.sem(t), rows_scattered.landed(t, 1))

                    norm = norm_steps(norm_outer, y, y_done, stats, junk, lambda t: rows[:, t.slot, :], rows_free)
                    pick_last, scatter = scatter_steps(norm_outer, cur_last, rows, y_dram)
                w_load, w_high, w_low = weight_split_steps(ph, jobs)
                block = ph.enter_context(nc.Block())

                @block.sync
                def _(sp):
                    for k, b in enumerate(biases):
                        sp.dma_start(bias_in[:, k, :], b.partition_broadcast(P)).then_inc(consts_in.sem, 16)
                    w_load(sp)
                    if biases:
                        sp.wait_ge(consts_made.sem, consts_made.all(1))
                        fill = bias_in[0:1, 0, :] if by_degree else bias[0:1, :]
                        sp.dma_start(neigh_rows[EP:EP + 1, :], fill).then_inc(fill_stored.sem, 16)

                    def store(t):
                        sp.wait_ge(rows_done.sem, rows_done.upto(t))
                        sp.dma_start(neigh_rows[bass.ds(t.times(P), P), :], rows[:, t.slot, :])\
                            .then_inc(rows_stored.sem(t), 16)

                    if not to_nodes:
                        in_steps(sp, ET, [(0, store)])
                    for s, v in (rows_scattered if to_nodes else rows_stored).used(ET):
                        sp.wait_ge(s, v)
                    if biases:
                        sp.wait_ge(fill_stored.sem, fill_stored.all(1))

                @block.gpsimd
                def _(pool):
                    def pick_neighbour(t):
                        if t.has(UNROLL):
                            pool.wait_ge(turned.sem, turned.upto(t, UNROLL))
                        pick_index(pool, t, index_picked, cur, dst_idx)

                    def gather(t):
                        index_ready(pool, t, index_picked)
                        gather_rows(e, x_dram, cur, t, gathered)

                    def pick_own(t):
                        if t.has(UNROLL):
                            pool.wait_ge(y_done.sem, y_done.upto(t, UNROLL))
                        pick_index(pool, t, own_picked, cur_own, src_idx)

                    def gather_own(t):
                        index_ready(pool, t, own_picked)
                        gather_rows(own, x_dram, cur_own, t, gathered2)

                    if to_nodes:
                        in_steps(pool, ET, [(0, pick_neighbour), (4, pick_own), (10, pick_last),
                                            (0, gather), (4, gather_own), (10, scatter)])
                    else:
                        in_steps(pool, ET, [(0, pick_neighbour), (0, gather)])

                @block.scalar
                def _(act):
                    def weigh(t):
                        act.wait_ge(gathered.sem(t), gathered.landed(t))
                        nc.scalar.activation(e[:, t.slot, :], e[:, t.slot, :], ACT.Copy,
                                             scale=weight_at[:, bass.ds(t.times(1), 1)]).then_inc(scaled.sem, 1)

                    def high(t):
                        act.wait_ge(summed.sem, summed.upto(t))
                        if t.has(UNROLL):
                            act.wait_ge(product_done.sem, product_done.upto(t, UNROLL))
                        nc.scalar.activation(hi[:, t.slot], sums[:, t.slot], ACT.Copy).then_inc(high_done.sem, 1)

                    stages = [(2, high)]
                    if by_weight:
                        stages = [(0, weigh)] + stages
                    if to_nodes:
                        stages += [(6, norm("squares", act)), (6, norm("std", act)), (8, norm("apply", act))]
                    in_steps(act, ET, stages)
                    act.wait_ge(product_done.sem, product_done.all(ET))
                    w_high(act)

                @block.vector
                def _(dve):
                    if biases:
                        dve.wait_ge(consts_in.sem, consts_in.all(len(biases)))
                        nc.vector.tensor_tensor(bias[:], bias_in[:, 0, :], bias_in[:, 1, :], ALU.add)\
                            .then_inc(consts_made.sem, 1)

                    if layer == 0:
                        dve.wait_ge(rows_in, 16)

                    def run_sums(t):
                        dve.wait_ge(turned.sem, turned.upto(t))
                        if t.has(UNROLL):
                            dve.wait_ge(high_done.sem, high_done.upto(t, UNROLL))
                            dve.wait_ge(low_done.sem, low_done.upto(t, UNROLL))
                        if t.has(1):
                            dve.wait_ge(summed.sem, summed.upto(t, 1))
                        for c in range(DC):
                            start = sums[:, (t.slot - 1) % UNROLL, c, P - 1:P] if t.has(1) else 0.0
                            last = nc.vector.tensor_tensor_scan(
                                sums[:, t.slot, c, :], same_run[:, bass.ds(t.times(P), P)],
                                turned_bank[t.half][:, c, :], start, ALU.mult, ALU.add)
                        last.then_inc(summed.sem, 1)

                    def low(t):
                        dve.wait_ge(high_done.sem, high_done.upto(t))
                        if t.has(UNROLL):
                            dve.wait_ge(product_done.sem, product_done.upto(t, UNROLL))
                        nc.vector.tensor_tensor(lo[:, t.slot], sums[:, t.slot], hi[:, t.slot].bitcast(F32),
                                                ALU.subtract).then_inc(low_done.sem, 1)

                    def rows_out(t):
                        dve.wait_ge(product_done.sem, product_done.upto(t))
                        if t.has(UNROLL):
                            dve.wait_ge(rows_stored.sem(t), rows_stored.landed(t, 1))
                        if not t.has(1):
                            dve.wait_ge(consts_made.sem, consts_made.all(1))
                        factor = invdeg_at[:, bass.ds(t.times(1), 1)] if by_degree else 1.0
                        nc.vector.scalar_tensor_tensor(rows[:, t.slot, :], product_bank[t.half][:], factor, bias[:],
                                                       ALU.mult, ALU.add).then_inc(rows_done.sem, 1)

                    def residual(t):
                        dve.wait_ge(product_done.sem, product_done.upto(t))
                        dve.wait_ge(gathered2.sem(t), gathered2.landed(t))
                        if t.has(UNROLL):
                            dve.wait_ge(norm_outer.applied.sem, norm_outer.applied.upto(t, UNROLL))
                        nc.vector.scalar_tensor_tensor(
                            y[:, t.slot, :], product_bank[t.half][:], 1.0, own[:, t.slot, :], ALU.mult, ALU.add,
                            accum_out=stats[:, t.slot, SUM:SUM + 1]).then_inc(y_done.sem, 1)

                    if to_nodes:
                        in_steps(dve, ET, [(7, norm("rstd", dve)), (5, residual), (7, norm("shift", dve)),
                                           (2, low), (5, norm("mean", dve)), (1, run_sums)])
                    else:
                        in_steps(dve, ET, [(2, low), (4, rows_out), (1, run_sums)])
                    w_low(dve)

                @block.tensor
                def _(pe):
                    def turn(t):
                        if by_weight:
                            pe.wait_ge(scaled.sem, scaled.upto(t))
                        else:
                            pe.wait_ge(gathered.sem(t), gathered.landed(t))
                        if t.has(2):
                            pe.wait_ge(summed.sem, summed.upto(t, 2))
                        for c in range(DC):
                            last = nc.tensor.transpose(turned_bank[t.half][:, c, :], e[:, t.slot, c * P:(c + 1) * P],
                                                       ident[:])
                        last.then_inc(turned.sem, 1)

                    def product(t):
                        pe.wait_ge(low_done.sem, low_done.upto(t))
                        if t.has(2):
                            reader = y_done if to_nodes else rows_done
                            pe.wait_ge(reader.sem, reader.upto(t, 2))
                        split_product(product_bank[t.half][:], hi[:, t.slot], lo[:, t.slot], slot)\
                            .then_inc(product_done.sem, 1)

                    in_steps(pe, ET, [(0, turn), (3, product)])

            for count in (index_picked, turned, summed, high_done, low_done, product_done):
                count.close(ET)
            for ring in (gathered, rows_scattered if to_nodes else rows_stored):
                ring.close(ET)
            if by_weight:
                scaled.close(ET)
            if biases:
                consts_in.close(len(biases))
                consts_made.close(1)
                fill_stored.close(1)
            if to_nodes:
                for count in (own_picked, y_done, last_picked):
                    count.close(ET)
                gathered2.close(ET)
                norm_outer.close(ET)
            else:
                rows_done.close(ET)

        def node_phase(layer, x_dram, y_drams, slot, jobs):
            inner = layer == 0
            nested = not inner
            with ExitStack() as ph:
                xs = sb(f"x{layer}", [P, UNROLL, D], F32, ph)
                g = sb(f"g{layer}", [P, UNROLL, D], F32, ph)
                cur = sb(f"cur_n{layer}", [P, UNROLL], I32, ph)
                hi = sb(f"x_hi{layer}", [P, 2, DC, P], F32R, ph)
                lo = sb(f"x_lo{layer}", [P, 2, DC, P], F32R, ph)
                y = sb(f"y{layer}", [P, UNROLL, D], F32, ph)
                done = [sb(f"done{layer}{k}", [P, UNROLL, D], F32, ph) for k in range(len(y_drams))]
                junk = sb(f"junk_n{layer}", [P, 2, D], F32, ph)
                stats = sb(f"stats{layer}", [P, UNROLL, STATS], F32, ph)
                gamma_beta = sb(f"gamma_beta{layer}", [P, 2, D], F32, ph)
                turned_bank = [pb(f"pt_n{layer}{k}", [P, DC, P], F32, ph) for k in range(2)]
                product_bank = [pb(f"pp_n{layer}{k}", [P, D], F32, ph) for k in range(2)]
                if inner:
                    xb = sb("xb", [P, UNROLL, D], F32, ph)
                    y2 = sb("y_outer", [P, UNROLL, D], F32, ph)
                    stats2 = sb("stats_outer", [P, UNROLL, STATS], F32, ph)
                    centered = sb("centered", [P, 2, D], F32, ph)
                w_load, w_high, w_low = weight_split_steps(ph, jobs)
                rows_in = [gamma, beta] if inner else []
                stores = [rows_stored, stored_twice][:len(y_drams)]

                def done_free(act, t):
                    if t.has(UNROLL):
                        act.wait_ge(rows_stored.sem(t), rows_stored.landed(t, 1))

                if inner:
                    norm1 = norm_steps(norm_inner, y, y_done, stats, junk, None, None)
                    norm2 = norm_steps(norm_outer, y2, y2_done, stats2, junk, lambda t: done[0][:, t.slot, :], done_free)
                else:
                    norm1 = norm_steps(norm_outer, y, y_done, stats, junk, lambda t: done[0][:, t.slot, :], done_free,
                                       width=3)
                block = ph.enter_context(nc.Block())

                @block.sync
                def _(sp):
                    for k, b in enumerate(rows_in):
                        sp.dma_start(gamma_beta[:, k, :], b.partition_broadcast(P)).then_inc(consts_in.sem, 16)

                    def load(t):
                        if t.has(UNROLL):
                            sp.wait_ge(y_done.sem, y_done.upto(t, UNROLL))
                            if inner:
                                sp.wait_ge(x_plus_beta.sem, x_plus_beta.upto(t, UNROLL))
                        n = NREST if isinstance(t.loop, int) and t.offset == NT - 1 else P
                        sp.dma_start(xs[0:n, t.slot, :], x_dram[bass.ds(t.times(P), n), :])\
                            .then_inc(x_landed.sem(t), 16)

                    def store(t):
                        n = NREST if isinstance(t.loop, int) and t.offset == NT - 1 else P
                        for k, y_dram in enumerate(y_drams):
                            applied = (norm_outer.applied, applied_twice)[k]
                            sp.wait_ge(applied.sem, applied.upto(t))
                            sp.dma_start(y_dram[bass.ds(t.times(P), n), :], done[k][0:n, t.slot, :])\
                                .then_inc(stores[k].sem(t), 16)

                    def weights(t):
                        if isinstance(t.loop, int) and t.offset == 0:
                            w_load(sp)

                    in_steps(sp, NT, [(0, load), (3, weights), (11 if inner else 7, store)])
                    for ring in stores:
                        for s, v in ring.used(NT):
                            sp.wait_ge(s, v)

                @block.gpsimd
                def _(pool):
                    def fetch(t):
                        if t.has(UNROLL):
                            pool.wait_ge(preact_done.sem, preact_done.upto(t, UNROLL))
                        pick_index(pool, t, index_picked, cur, node_idx)
                        index_ready(pool, t, index_picked)
                        gather_rows(g, neigh_rows, cur, t, gathered)

                    def add_beta(t):
                        pool.wait_ge(x_landed.sem(t), x_landed.landed(t))
                        if t.has(UNROLL):
                            pool.wait_ge(y2_done.sem, y2_done.upto(t, UNROLL))
                        nc.gpsimd.tensor_tensor(xb[:, t.slot, :], xs[:, t.slot, :], gamma_beta[:, 1, :], ALU.add)\
                            .then_inc(x_plus_beta.sem, 1)

                    def apply_twice(t):
                        pool.wait_ge(norm_outer.scale.sem, norm_outer.scale.upto(t))
                        if t.has(UNROLL):
                            pool.wait_ge(stored_twice.sem(t), stored_twice.landed(t, 1))
                        pool.sem_inc(pool_steps, 1)
                        nc.gpsimd.tensor_scalar(done[1][:, t.slot, :], y[:, t.slot, :],
                                                stats[:, t.slot, RSTD + 1:RSTD + 2], stats[:, t.slot, SHIFT + 1:SHIFT + 2],
                                                ALU.mult, ALU.add).then_inc(applied_twice.sem, 1)

                    if inner:
                        in_steps(pool, NT, [(0, fetch), (2, add_beta), (3, norm1("mean", pool)),
                                            (6, norm2("mean", pool)), (8, norm2("shift", pool))])
                    else:
                        in_steps(pool, NT, [(0, fetch), (5, apply_twice)])

                @block.scalar
                def _(act):
                    def high(t):
                        act.wait_ge(turned.sem, turned.upto(t))
                        if t.has(2):
                            act.wait_ge(product_done.sem, product_done.upto(t, 2))
                        nc.scalar.activation(hi[:, t.half], turned_bank[t.half][:], ACT.Copy)\
                            .then_inc(high_done.sem, 1)

                    if inner:
                        stages = [(9, norm2("apply", act)), (0, high), (4, norm1("squares", act)),
                                  (7, norm2("squares", act)), (4, norm1("std", act)), (7, norm2("std", act))]
                    else:
                        stages = [(0, high), (4, norm1("std", act)), (3, norm1("squares", act)),
                                  (5, norm1("apply", act))]
                    in_steps(act, NT, stages)
                    w_high(act)

                @block.vector
                def _(dve):
                    if inner:
                        dve.wait_ge(consts_in.sem, consts_in.all(len(rows_in)))

                    def low(t):
                        dve.wait_ge(high_done.sem, high_done.upto(t))
                        if t.has(2):
                            dve.wait_ge(product_done.sem, product_done.upto(t, 2))
                        nc.vector.tensor_tensor(lo[:, t.half], turned_bank[t.half][:], hi[:, t.half].bitcast(F32),
                                                ALU.subtract).then_inc(low_done.sem, 1)

                    def preact(t):
                        dve.wait_ge(product_done.sem, product_done.upto(t))
                        dve.wait_ge(gathered.sem(t), gathered.landed(t))
                        nc.vector.tensor_tensor(product_bank[t.half][:], product_bank[t.half][:], g[:, t.slot, :],
                                                ALU.add).then_inc(preact_done.sem, 1)

                    def residual(t):
                        dve.wait_ge(preact_done.sem, preact_done.upto(t))
                        if t.has(UNROLL):
                            if inner:
                                dve.wait_ge(norm_inner.squares.sem, norm_inner.squares.upto(t, UNROLL))
                                dve.wait_ge(scaled_gamma.sem, scaled_gamma.upto(t, UNROLL))
                            else:
                                for applied in (norm_outer.applied, applied_twice):
                                    dve.wait_ge(applied.sem, applied.upto(t, UNROLL))
                        nc.vector.scalar_tensor_tensor(
                            y[:, t.slot, :], product_bank[t.half][:], 0.0, xs[:, t.slot, :], ALU.max, ALU.add,
                            accum_out=stats[:, t.slot, SUM:SUM + 1]).then_inc(y_done.sem, 1)

                    def center(t):
                        dve.wait_ge(norm_inner.mean.sem, norm_inner.mean.upto(t))
                        if t.has(2):
                            dve.wait_ge(y2_done.sem, y2_done.upto(t, 2))
                        nc.vector.scalar_tensor_tensor(centered[:, t.half, :], y[:, t.slot, :],
                                                       stats[:, t.slot, NEG_MEAN:NEG_MEAN + 1], gamma_beta[:, 0, :],
                                                       ALU.add, ALU.mult).then_inc(scaled_gamma.sem, 1)

                    def outer(t):
                        dve.wait_ge(norm_inner.rstd.sem, norm_inner.rstd.upto(t))
                        dve.wait_ge(scaled_gamma.sem, scaled_gamma.upto(t))
                        dve.wait_ge(x_plus_beta.sem, x_plus_beta.upto(t))
                        if t.has(UNROLL):
                            dve.wait_ge(norm_outer.applied.sem, norm_outer.applied.upto(t, UNROLL))
                        nc.vector.scalar_tensor_tensor(
                            y2[:, t.slot, :], centered[:, t.half, :], stats[:, t.slot, RSTD:RSTD + 1],
                            xb[:, t.slot, :], ALU.mult, ALU.add,
                            accum_out=stats2[:, t.slot, SUM:SUM + 1]).then_inc(y2_done.sem, 1)

                    def ratio(t):
                        dve.wait_ge(norm_outer.rstd.sem, norm_outer.rstd.upto(t))
                        nc.vector.tensor_tensor(last_scale[:, bass.ds(t.times(1), 1)],
                                                stats[:, t.slot, STD + 1:STD + 2], stats[:, t.slot, RSTD + 2:RSTD + 3],
                                                ALU.mult).then_inc(ratio_done.sem, 1)

                    if inner:
                        stages = [(8, norm2("rstd", dve)), (2, preact), (5, norm1("rstd", dve)), (0, low),
                                  (4, center), (2, residual), (5, outer)]
                    else:
                        stages = [(4, norm1("rstd", dve)), (2, preact), (4, norm1("shift", dve)),
                                  (3, norm1("variance", dve)), (2, residual), (0, low), (5, ratio),
                                  (2, norm1("mean", dve))]
                    in_steps(dve, NT, stages)
                    w_low(dve)

                @block.tensor
                def _(pe):
                    def turn(t):
                        pe.wait_ge(x_landed.sem(t), x_landed.landed(t))
                        if t.has(2):
                            pe.wait_ge(low_done.sem, low_done.upto(t, 2))
                        for c in range(DC):
                            last = nc.tensor.transpose(turned_bank[t.half][:, c, :], xs[:, t.slot, c * P:(c + 1) * P],
                                                       ident[:])
                        last.then_inc(turned.sem, 1)

                    def product(t):
                        pe.wait_ge(low_done.sem, low_done.upto(t))
                        if t.has(2):
                            pe.wait_ge(y_done.sem, y_done.upto(t, 2))
                        split_product(product_bank[t.half][:], hi[:, t.half], lo[:, t.half], slot)\
                            .then_inc(product_done.sem, 1)

                    in_steps(pe, NT, [(0, turn), (1, product)])

            for count in (index_picked, turned, high_done, low_done, product_done, preact_done, y_done):
                count.close(NT)
            for ring in [gathered, x_landed] + stores:
                ring.close(NT)
            consts_in.close(len(rows_in))
            norm_outer.close(NT)
            if nested:
                for count in (norm_outer.variance, applied_twice, ratio_done):
                    count.close(NT)
            if inner:
                for count in (norm_inner.mean, norm_inner.squares, norm_inner.std, norm_inner.rstd):
                    count.close(NT)
                for count in (x_plus_beta, scaled_gamma, y2_done):
                    count.close(NT)

        def attention(x_dram, y_dram):
            with ExitStack() as keep:
                v_all = sb("v_all", [P, ET * D], F32, keep)
                scores = sb("scores", [P, ET * HEADS], F32, keep)
                exps = sb("exps", [P, ET * HEADS], F32, keep)
                query_product(x_dram, y_dram, v_all, scores)
                softmax_terms(scores, exps)
                weighted_sums(v_all, exps, x_dram, y_dram)

        def query_product(x_dram, y_dram, v_all, scores):
            with ExitStack() as ph:
                e = [sb(f"e_{side}", [P, UNROLL, D], F32, ph) for side in ("src", "dst")]
                cur = [sb(f"cur_{side}", [P, UNROLL], I32, ph) for side in ("src", "dst")]
                hi = [sb(f"hi_{side}", [P, 2, DC, P], F32R, ph) for side in ("src", "dst")]
                lo = [sb(f"lo_{side}", [P, 2, DC, P], F32R, ph) for side in ("src", "dst")]
                pair = sb("pair", [P, UNROLL, 2, D], F32, ph)
                q = sb("q", [P, 2, D], F32, ph)
                qk = sb("qk", [P, 2, D], F32, ph)
                turned_bank = [pb(f"pt_{side}", [P, DC, P], F32, ph) for side in ("src", "dst")]
                banks = {n: [pb(f"p{n}{k}", [P, D], F32, ph) for k in range(2)] for n in "qkv"}
                landed = [gathered, gathered2]
                indices = [src_idx, dst_idx]
                v_copied = Count(sem("v_copied"))
                q_copied = Count(sem("q_copied"))
                qk_done = Count(sem("qk_done"))
                scored = Count(sem("scored"))
                q_product_done = Count(sem("q_product_done"))
                block = ph.enter_context(nc.Block())

                @block.sync
                def _(sp):
                    def rows_of(dram, t):
                        if isinstance(t.loop, int) and t.offset == PAIRS:
                            return dram[PAIRS * 2 * P:N, :], pair[0:PAIR_REST, t.slot, 0, :]
                        return (dram[bass.ds(t.times(2 * P), 2 * P), :].rearrange("(k p) d -> p k d", p=P),
                                pair[:, t.slot])

                    def load(t):
                        if t.has(UNROLL):
                            sp.wait_ge(out_stored.sem(t), out_stored.landed(t, 1))
                        rows, place = rows_of(x_dram, t)
                        sp.dma_start(place, rows).then_inc(x_landed.sem(t), 16)

                    def store(t):
                        sp.wait_ge(out_scaled.sem, out_scaled.upto(t))
                        rows, place = rows_of(y_dram, t)
                        sp.dma_start(rows, place).then_inc(out_stored.sem(t), 16)

                    in_steps(sp, ET, [(1, load), (3, store)])
                    for s, v in out_stored.used(ET):
                        sp.wait_ge(s, v)

                @block.gpsimd
                def _(pool):
                    def gather(t):
                        if t.has(UNROLL):
                            pool.wait_ge(turned.sem, turned.upto(t, UNROLL))
                        pick_index(pool, t, both_picked, cur[0], src_idx)
                        pick_index(pool, t, both_picked, cur[1], dst_idx)
                        index_ready(pool, t, both_picked)
                        for side in range(2):
                            gather_rows(e[side], x_dram, cur[side], t, landed[side])

                    in_steps(pool, ET, [(0, gather)])

                @block.scalar
                def _(act):
                    def high(t):
                        act.wait_ge(turned.sem, turned.upto(t))
                        if t.has(2):
                            act.wait_ge(product_done.sem, product_done.upto(t, 2))
                        for side in range(2):
                            last = nc.scalar.activation(hi[side][:, t.half], turned_bank[side][:], ACT.Copy)
                        last.then_inc(high_done.sem, 1)

                    def copy_q(t):
                        act.wait_ge(q_product_done.sem, q_product_done.upto(t))
                        if t.has(2):
                            act.wait_ge(qk_done.sem, qk_done.upto(t, 2))
                        nc.scalar.activation(q[:, t.half, :], banks["q"][t.half][:], ACT.Copy,
                                             scale=float(FH) ** -0.5).then_inc(q_copied.sem, 1)

                    def copy_v(t):
                        act.wait_ge(product_done.sem, product_done.upto(t))
                        nc.scalar.activation(v_all[:, bass.ds(t.times(D), D)], banks["v"][t.half][:], ACT.Copy)\
                            .then_inc(v_copied.sem, 1)

                    in_steps(act, ET, [(0, high), (2, copy_q), (2, copy_v)])

                @block.vector
                def _(dve):
                    def low(t):
                        dve.wait_ge(high_done.sem, high_done.upto(t))
                        if t.has(2):
                            dve.wait_ge(product_done.sem, product_done.upto(t, 2))
                        for side in range(2):
                            last = nc.vector.tensor_tensor(lo[side][:, t.half], turned_bank[side][:],
                                                           hi[side][:, t.half].bitcast(F32), ALU.subtract)
                        last.then_inc(low_done.sem, 1)

                    def score(t):
                        dve.wait_ge(product_done.sem, product_done.upto(t))
                        dve.wait_ge(q_copied.sem, q_copied.upto(t))
                        if t.has(2):
                            dve.wait_ge(scored.sem, scored.upto(t, 2))
                        nc.vector.tensor_tensor(qk[:, t.half, :], banks["k"][t.half][:], q[:, t.half, :], ALU.mult)\
                            .then_inc(qk_done.sem, 1)
                        dve.wait_ge(qk_done.sem, qk_done.upto(t))
                        nc.vector.tensor_reduce(scores[:, bass.ds(t.times(HEADS), HEADS)],
                                                qk[:, t.half, :].rearrange("p (h f) -> p h f", h=HEADS),
                                                AX_X, ALU.add).then_inc(scored.sem, 1)

                    def last_norm(t):
                        dve.wait_ge(x_landed.sem(t), x_landed.landed(t))
                        for k in range(2):
                            if isinstance(t.loop, int) and t.offset == PAIRS and k == 1:
                                dve.sem_inc(out_scaled.sem, 1)
                                continue
                            nc.vector.tensor_scalar(pair[:, t.slot, k, :], pair[:, t.slot, k, :],
                                                    last_scale[:, bass.ds(t.times(2, k), 1)], None,
                                                    ALU.mult).then_inc(out_scaled.sem, 1)

                    in_steps(dve, ET, [(0, low), (2, score), (2, last_norm)])

                @block.tensor
                def _(pe):
                    def turn(t):
                        for side in range(2):
                            pe.wait_ge(landed[side].sem(t), landed[side].landed(t))
                        if t.has(1):
                            pe.wait_ge(low_done.sem, low_done.upto(t, 1))
                        for side in range(2):
                            for c in range(DC):
                                last = nc.tensor.transpose(turned_bank[side][:, c, :],
                                                           e[side][:, t.slot, c * P:(c + 1) * P], ident[:])
                        last.then_inc(turned.sem, 1)

                    def product(t):
                        pe.wait_ge(low_done.sem, low_done.upto(t))
                        if t.has(2):
                            pe.wait_ge(q_copied.sem, q_copied.upto(t, 2))
                            pe.wait_ge(qk_done.sem, qk_done.upto(t, 2))
                            pe.wait_ge(v_copied.sem, v_copied.upto(t, 2))
                        split_product(banks["q"][t.half][:], hi[0][:, t.half], lo[0][:, t.half], Q_SLOT)\
                            .then_inc(q_product_done.sem, 1)
                        split_product(banks["k"][t.half][:], hi[1][:, t.half], lo[1][:, t.half], K_SLOT)
                        split_product(banks["v"][t.half][:], hi[1][:, t.half], lo[1][:, t.half], V_SLOT)\
                            .then_inc(product_done.sem, 1)

                    in_steps(pe, ET, [(0, turn), (1, product)])

            for count in (both_picked, turned, high_done, low_done, product_done):
                count.close(ET)
            for ring in (gathered, gathered2, x_landed, out_stored):
                ring.close(ET)
            out_scaled.close(ET)

        def softmax_terms(scores, exps):
            with ExitStack() as ph:
                by_head = sb("by_head", [HEADS, EP], F32, ph)
                penalty = sb("penalty", [HEADS, EP + 1], F32, ph)
                most = sb("most", [HEADS, EP], F32, ph)
                PER = 4
                head_bank = [pb(f"ph{k}", [HEADS, PER * P], F32, ph) for k in range(2)]
                exp_bank = pb("p_exp", [P, ET * HEADS], F32, ph)
                heads_turned = sem("heads_turned")
                heads_copied = sem("heads_copied")
                penalty_steps = sem("penalty_steps")
                most_steps = sem("most_steps")
                shifted = sem("shifted")
                exp_done = sem("exp_done")
                exps_turned = sem("exps_turned")
                exps_copied = sem("exps_copied")
                block = ph.enter_context(nc.Block())
                groups = range(0, ET, PER)

                @block.tensor
                def _(pe):
                    for n, t0 in enumerate(groups):
                        if n >= 2:
                            pe.wait_ge(heads_copied, n - 1)
                        for k in range(PER):
                            t = t0 + k
                            last = nc.tensor.transpose(head_bank[n % 2][:, k * P:(k + 1) * P],
                                                       scores[:, t * HEADS:(t + 1) * HEADS], ident[:])
                        last.then_inc(heads_turned, 1)
                    pe.wait_ge(exp_done, 1)
                    for t in range(ET):
                        last = nc.tensor.transpose(exp_bank[:, t * HEADS:(t + 1) * HEADS],
                                                   by_head[:, t * P:(t + 1) * P], ident[0:HEADS, 0:HEADS])
                    last.then_inc(exps_turned, 1)

                @block.scalar
                def _(act):
                    for n, t0 in enumerate(groups):
                        act.wait_ge(heads_turned, n + 1)
                        nc.scalar.activation(by_head[:, t0 * P:(t0 + PER) * P], head_bank[n % 2][:], ACT.Copy)\
                            .then_inc(heads_copied, 1)
                    act.wait_ge(shifted, 1)
                    nc.scalar.activation(by_head[:], by_head[:], ACT.Exp).then_inc(exp_done, 1)

                @block.vector
                def _(dve):
                    nc.vector.memset(penalty[:, EP:EP + 1], -BIG)
                    nc.vector.tensor_scalar(penalty[:, 0:EP], same_run[0:HEADS, :], BIG, -BIG, ALU.mult, ALU.add)\
                        .then_inc(penalty_steps, 1)
                    dve.wait_ge(penalty_steps, 1)
                    dve.wait_ge(heads_copied, len(groups))
                    nc.vector.tensor_tensor_scan(most[:], penalty[:, 0:EP], by_head[:], 0.0, ALU.add, ALU.max)\
                        .then_inc(most_steps, 1)
                    dve.wait_ge(most_steps, 1)
                    nc.vector.tensor_tensor_scan(most[:, ::-1], penalty[:, EP:0:-1], most[:, ::-1], 0.0,
                                                 ALU.add, ALU.max).then_inc(most_steps, 1)
                    dve.wait_ge(most_steps, 2)
                    nc.vector.tensor_tensor(by_head[:], by_head[:], most[:], ALU.subtract).then_inc(shifted, 1)
                    dve.wait_ge(exps_turned, 1)
                    nc.vector.tensor_copy(exps[:], exp_bank[:]).then_inc(exps_copied, 1)

        def weighted_sums(v_all, exps, x_dram, y_dram):
            with ExitStack() as ph:
                sorted_src = sb("sorted_src", [P, EP + 1], F32, ph)
                same = sb("same", [P, UNROLL, P], F32, ph)
                carry = sb("carry", [P, UNROLL, P], F32, ph)
                ev = sb("ev", [P, 2, D], F32, ph)
                sums = sb("sums", [P, UNROLL, D + HEADS], F32, ph)
                den = sb("den", [P, 2, HEADS], F32, ph)
                own_rows = sb("own_rows", [P, UNROLL, D], F32, ph)
                cur_own = sb("cur_own3", [P, UNROLL], I32, ph)
                cur_last = sb("cur_last3", [P, UNROLL], I32, ph)
                y = sb("y3", [P, UNROLL, D], F32, ph)
                rows = sb("rows3", [P, UNROLL, D], F32, ph)
                junk = sb("junk3", [P, 2, D], F32, ph)
                stats = sb("stats3", [P, UNROLL, STATS], F32, ph)
                sum_bank = [pb(f"p_sum{k}", [P, D], F32, ph) for k in range(UNROLL)]
                den_bank = [pb(f"p_den{k}", [P, HEADS], F32, ph) for k in range(UNROLL)]
                src_row_in = sem("src_row_in")
                matched = Count(sem("matched"))
                weighed = Count(sem("weighed"))
                own_done = Count(sem("own_done"))
                totals_done = Count(sem("totals_done"))
                totals_copied = Count(sem("totals_copied"), 2)
                den_kept = Count(sem("den_kept"))
                den_done = Count(sem("den_done"))
                divided = Count(sem("divided"))

                def rows_free(act, t):
                    if t.has(UNROLL):
                        act.wait_ge(rows_scattered.sem(t), rows_scattered.landed(t, 1))

                norm = norm_steps(norm_outer, y, y_done, stats, junk, lambda t: rows[:, t.slot, :], rows_free)
                pick_last, scatter = scatter_steps(norm_outer, cur_last, rows, y_dram)
                block = ph.enter_context(nc.Block())

                @block.sync
                def _(sp):
                    sp.dma_start(sorted_src[:], sorted_src_row[0, :].partition_broadcast(P)).then_inc(src_row_in, 16)
                    for s, v in rows_scattered.used(ET):
                        sp.wait_ge(s, v)

                @block.gpsimd
                def _(pool):
                    def pick_own(t):
                        if t.has(UNROLL):
                            pool.wait_ge(y_done.sem, y_done.upto(t, UNROLL))
                        pick_index(pool, t, index_picked, cur_own, src_idx)

                    def gather_own(t):
                        index_ready(pool, t, index_picked)
                        gather_rows(own_rows, x_dram, cur_own, t, gathered)

                    in_steps(pool, ET, [(0, pick_own), (9, pick_last), (0, gather_own), (9, scatter)])

                @block.vector
                def _(dve):
                    dve.wait_ge(src_row_in, 16)

                    def match(t):
                        if t.has(UNROLL):
                            dve.wait_ge(totals_done.sem, totals_done.upto(t, UNROLL))
                        mine = sorted_src[:, bass.ds(t.times(P, 1), P)]
                        nc.vector.tensor_scalar(same[:, t.slot, :], mine, src_at[:, bass.ds(t.times(1), 1)], None,
                                                ALU.is_equal)
                        nc.vector.tensor_scalar(carry[:, t.slot, :], mine, sorted_src[:, bass.ds(t.times(P), 1)],
                                                ident[:, P - 1:P], ALU.is_equal, ALU.mult).then_inc(matched.sem, 1)

                    def weigh(t):
                        if t.has(2):
                            dve.wait_ge(own_done.sem, own_done.upto(t, 2))
                        terms = exps[:, bass.ds(t.times(HEADS), HEADS)].unsqueeze(2).to_broadcast([P, HEADS, FH])
                        nc.vector.tensor_tensor(ev[:, t.half, :].rearrange("p (h f) -> p h f", h=HEADS),
                                                v_all[:, bass.ds(t.times(D), D)].rearrange("p (h f) -> p h f", h=HEADS),
                                                terms, ALU.mult).then_inc(weighed.sem, 1)

                    def guard_denominator(t):
                        dve.wait_ge(totals_copied.sem, totals_copied.upto(t))
                        if t.has(2):
                            dve.wait_ge(divided.sem, divided.upto(t, 2))
                        nc.vector.tensor_scalar(den[:, t.half, :], sums[:, t.slot, D:D + HEADS], 1e-30, None, ALU.max)\
                            .then_inc(den_kept.sem, 1)

                    def invert(t):
                        dve.wait_ge(den_kept.sem, den_kept.upto(t))
                        nc.vector.reciprocal(den[:, t.half, :], den[:, t.half, :]).then_inc(den_done.sem, 1)

                    def divide(t):
                        dve.wait_ge(den_done.sem, den_done.upto(t))
                        if t.has(UNROLL):
                            dve.wait_ge(norm_outer.applied.sem, norm_outer.applied.upto(t, UNROLL))
                        nc.vector.tensor_tensor(y[:, t.slot, :].rearrange("p (h f) -> p h f", h=HEADS),
                                                sums[:, t.slot, 0:D].rearrange("p (h f) -> p h f", h=HEADS),
                                                den[:, t.half, :].unsqueeze(2).to_broadcast([P, HEADS, FH]), ALU.mult)\
                            .then_inc(divided.sem, 1)

                    def residual(t):
                        dve.wait_ge(divided.sem, divided.upto(t))
                        dve.wait_ge(gathered.sem(t), gathered.landed(t))
                        nc.vector.scalar_tensor_tensor(
                            y[:, t.slot, :], y[:, t.slot, :], 1.0, own_rows[:, t.slot, :], ALU.mult, ALU.add,
                            accum_out=stats[:, t.slot, SUM:SUM + 1]).then_inc(y_done.sem, 1)

                    in_steps(dve, ET, [(0, match), (3, guard_denominator), (0, weigh), (3, invert), (3, divide),
                                       (5, norm("rstd", dve)), (3, residual), (5, norm("shift", dve)),
                                       (3, norm("mean", dve))])

                @block.tensor
                def _(pe):
                    def own(t):
                        pe.wait_ge(matched.sem, matched.upto(t))
                        pe.wait_ge(weighed.sem, weighed.upto(t))
                        if t.has(UNROLL):
                            pe.wait_ge(totals_copied.sem, totals_copied.upto(t, UNROLL))
                        alone = not t.has(1)
                        nc.tensor.matmul(den_bank[t.slot][:], same[:, t.slot, :],
                                         exps[:, bass.ds(t.times(HEADS), HEADS)], start=True, stop=alone)
                        nc.tensor.matmul(sum_bank[t.slot][:], same[:, t.slot, :], ev[:, t.half, :],
                                         start=True, stop=alone).then_inc(own_done.sem, 1)

                    def carried(t):
                        if not t.has(1):
                            pe.sem_inc(totals_done.sem, 1)
                            return
                        before = (t.slot - 1) % UNROLL
                        pe.wait_ge(totals_copied.sem, totals_copied.upto(t, 1))
                        nc.tensor.matmul(den_bank[t.slot][:], carry[:, t.slot, :], sums[:, before, D:D + HEADS],
                                         start=False, stop=True)
                        nc.tensor.matmul(sum_bank[t.slot][:], carry[:, t.slot, :], sums[:, before, 0:D],
                                         start=False, stop=True).then_inc(totals_done.sem, 1)

                    in_steps(pe, ET, [(0, own), (1, carried)])

                @block.scalar
                def _(act):
                    def copy_sums(t):
                        act.wait_ge(own_done.sem, own_done.upto(t))
                        act.wait_ge(totals_done.sem, totals_done.upto(t))
                        if t.has(UNROLL):
                            act.wait_ge(divided.sem, divided.upto(t, UNROLL))
                        nc.scalar.activation(sums[:, t.slot, 0:D], sum_bank[t.slot][:], ACT.Copy)\
                            .then_inc(totals_copied.sem, 1)
                        nc.scalar.activation(sums[:, t.slot, D:D + HEADS], den_bank[t.slot][:], ACT.Copy)\
                            .then_inc(totals_copied.sem, 1)

                    in_steps(act, ET, [(4, norm("squares", act)), (6, norm("apply", act)), (4, norm("std", act)),
                                       (1, copy_sums)])

            for count in (index_picked, y_done, last_picked):
                count.close(ET)
            gathered.close(ET)
            rows_scattered.close(ET)
            norm_outer.close(ET)

        edge_phase(0, x, 0, (b_self0, b_neigh0), [(w_neigh1, 2)])
        node_phase(0, x, [values[0]], 1, [(w_self1, 0)])
        edge_phase(1, values[0], 2, (b_self1, b_neigh1), [(w_neigh2, 1)])
        Q_SLOT, K_SLOT, V_SLOT = 2, 0, 1
        node_phase(1, values[0], [values[1], values[2]], 0, [(w_qkv[:, 0:D], Q_SLOT)])
        edge_phase(2, values[1], 1, (), [(w_qkv[:, D:2 * D], K_SLOT), (w_qkv[:, 2 * D:3 * D], V_SLOT)],
                   y_dram=values[2])
        attention(values[2], out)


_INS = ["x", "src", "dst", "edge_weight", "L0_gnn_W_self", "L0_gnn_b_self", "L0_gnn_W_neigh", "L0_gnn_b_neigh",
        "L0_gnn_ln_gamma", "L0_gnn_ln_beta", "L1_gnn_self_w", "L1_gnn_self_b", "L1_gnn_neigh_w", "L1_gnn_neigh_b",
        "L2_gnn_weight", "L3_gnn_W"]
_TURNED = {"L0_gnn_W_self", "L0_gnn_W_neigh", "L1_gnn_self_w", "L1_gnn_neigh_w", "L2_gnn_weight"}


def kernel(**inputs):
    import numpy as np
    import concourse.bacc as bacc
    from concourse.bass_utils import run_bass_kernel_spmd

    nc = bacc.Bacc("TRN2", target_bir_lowering=False, num_devices=1)
    arrays, args = {}, []
    for name in _INS:
        a = np.asarray(inputs[name])
        a = np.ascontiguousarray(a.T if name in _TURNED else a)
        arrays[f"in_{name}"] = a
        args.append(nc.dram_tensor(f"in_{name}", a.shape, mybir.dt.from_np(a.dtype), kind="ExternalInput").ap())
    n, d = inputs["x"].shape
    out = nc.dram_tensor("out_x", [n, d], F32, kind="ExternalOutput").ap()
    build(nc, *args, out)
    result = run_bass_kernel_spmd(nc, [arrays], core_ids=[0])
    return result.results[0]["out_x"]
```

```python
from contextlib import ExitStack

import concourse.bass as bass
from concourse import mybir

F32 = mybir.dt.float32
F32R = mybir.dt.float32r
BF16 = mybir.dt.bfloat16
I32 = mybir.dt.int32
ALU = mybir.AluOpType
ACT = mybir.ActivationFunctionType
AX_X = mybir.AxisListType.X

P = 128
UNROLL = 4


class Tile:

    def __init__(self, loop, offset):
        self.loop, self.offset = loop, offset
        self.slot = offset % UNROLL
        self.half = offset % 2

    def times(self, size, add=0):
        if isinstance(self.loop, int):
            return self.offset * size + add
        return self.loop * (UNROLL * size) + (self.offset * size + add)

    def turn(self, size):
        whole = (self.offset // UNROLL + 1) * size
        return whole if isinstance(self.loop, int) else self.loop * size + whole

    def has(self, back):
        return not isinstance(self.loop, int) or self.offset >= back


class Count:

    def __init__(self, sem, per=1):
        self.sem, self.per, self.base = sem, per, 0

    def upto(self, tile, back=0):
        return tile.times(self.per, self.base + self.per * (1 - back))

    def all(self, n):
        return self.base + self.per * n

    def close(self, n):
        self.base += self.per * n


class Slots:

    def __init__(self, sems):
        self.sems, self.bases = sems, [0] * UNROLL

    def sem(self, tile):
        return self.sems[tile.slot]

    def landed(self, tile, back=0):
        return tile.turn(16) + (self.bases[tile.slot] - 16 * back)

    def used(self, n):
        return [(self.sems[k], self.bases[k] + 16 * len(range(k, n, UNROLL))) for k in range(UNROLL)]

    def close(self, n):
        self.bases = [v for _, v in self.used(n)]


def in_steps(eng, n, stages):
    deepest = max(lag for lag, _ in stages)
    first = -(-(deepest + UNROLL) // UNROLL)
    last = n // UNROLL

    def straight(steps):
        for s in steps:
            for lag, stage in stages:
                if 0 <= s - lag < n:
                    stage(Tile(0, s - lag))

    if last - first < 2:
        straight(range(n + deepest))
        return
    straight(range(first * UNROLL))
    with eng.Fori(first, last) as i:
        for j in range(UNROLL):
            for lag, stage in stages:
                stage(Tile(i, j - lag))
    straight(range(last * UNROLL, n + deepest))


def build(nc, x, src, dst, edge_weight, w_self0, b_self0, w_neigh0, b_neigh0, gamma, beta,
          w_self1, b_self1, w_neigh1, b_neigh1, w_neigh2, w_qkv, out):
    N, D = x.shape
    E = src.shape[0]
    DC = D // P
    NT = -(-N // P)
    NREST = N - (NT - 1) * P
    PAIRS = N // (2 * P)
    PAIR_REST = N - PAIRS * 2 * P
    ET = -(-E // P)
    EP = ET * P
    ER = E // ET
    HEADS = 8
    FH = D // HEADS
    PAD_NODE = NT * P - 1
    NOWHERE = 4 * EP
    EPS = 1e-5
    BIG = 3.0e38
    NESTED_VARIANCE = [(1.0, EPS), (1.0 + EPS, EPS ** 2), (1.0 + EPS + EPS ** 2, EPS ** 3)]
    assert ER * ET == E and ER <= P and PAD_NODE >= N and D == DC * P and NT <= P and NT * P < 32768
    assert PAIRS == ET - 1 and 0 < PAIR_REST <= P

    records = nc.dram_tensor("records", [EP + 2, 4], F32, kind="Internal").ap()
    same_run_row = nc.dram_tensor("same_run_row", [1, EP], BF16, kind="Internal").ap()
    sorted_src_row = nc.dram_tensor("sorted_src_row", [1, EP + 1], F32, kind="Internal").ap()
    neigh_rows = nc.dram_tensor("neigh_rows", [EP + 1, D], F32, kind="Internal").ap()
    values = [nc.dram_tensor(f"values{i}", [N, D], F32, kind="Internal").ap() for i in range(3)]

    ctx = ExitStack()
    with ctx:
        def sb(name, shape, dt, where=ctx):
            return where.enter_context(nc.sbuf_tensor(name, shape, dt))

        def pb(name, shape, dt, where):
            return where.enter_context(nc.psum_tensor(name, shape, dt))

        def sem(name):
            return ctx.enter_context(nc.semaphore(name))

        def slots(name):
            return Slots([sem(f"{name}{k}") for k in range(UNROLL)])

        ident = sb("ident", [P, P], F32)
        src_at = sb("src_at", [P, ET], F32)
        dst_idx = sb("dst_idx", [P, ET], I32)
        src_idx = sb("src_idx", [P, ET], I32)
        weight_at = sb("weight_at", [P, ET], F32)
        invdeg_at = sb("invdeg_at", [P, ET], F32)
        last_idx = sb("last_idx", [P, ET], I32)
        node_idx = sb("node_idx", [P, NT], I32)
        var_term = sb("var_term", [P, 3], F32)
        mean_factor = sb("mean_factor", [P, 1], F32)
        last_scale = sb("last_scale", [P, NT], F32)
        same_run = sb("same_run", [P, EP], BF16)
        w_hi = [sb(f"w_hi{k}", [P, DC, D], F32R) for k in range(3)]
        w_lo = [sb(f"w_lo{k}", [P, DC, D], F32R) for k in range(3)]

        pool_steps = sem("pool_steps")
        rows_in = sem("rows_in")
        weight_landed = sem("weight_landed")
        weight_hi_done = sem("weight_hi_done")
        weight_lo_done = sem("weight_lo_done")
        weights_split, weights_loaded = [0], [0]

        class WeightSplit:

            def __init__(self, where, jobs, landed=None):
                self.jobs = jobs
                self.chunks_before = DC * weights_split[0]
                self.landed = landed or weight_landed
                self.landed_value = 16 * len(jobs) if landed else 16 * (weights_loaded[0] + len(jobs))
                weights_loaded[0] += 0 if landed else len(jobs)
                self.stage = sb(f"w_stage_{weights_split[0]}", [P, len(jobs), DC, D], F32, where)
                weights_split[0] += len(jobs)

            def load(self, sp):
                for k, (w, _) in enumerate(self.jobs):
                    sp.dma_start(self.stage[:, k], w.rearrange("(c p) n -> p c n", p=P)).then_inc(self.landed, 16)

            def high_chunk(self, act, n):
                k, c = divmod(n, DC)
                act.wait_ge(self.landed, self.landed_value)
                nc.scalar.activation(w_hi[self.jobs[k][1]][:, c], self.stage[:, k, c], ACT.Copy)\
                    .then_inc(weight_hi_done, 1)

            def low_chunk(self, dve, n):
                k, c = divmod(n, DC)
                slot = self.jobs[k][1]
                dve.wait_ge(weight_hi_done, self.chunks_before + n + 1)
                nc.vector.tensor_tensor(w_lo[slot][:, c], self.stage[:, k, c], w_hi[slot][:, c].bitcast(F32),
                                        ALU.subtract).then_inc(weight_lo_done, 1)

            def high(self, act):
                for n in range(DC * len(self.jobs)):
                    self.high_chunk(act, n)

            def low(self, dve):
                for n in range(DC * len(self.jobs)):
                    self.low_chunk(dve, n)

            def early(self, chunk, eng):
                def stage(t):
                    if isinstance(t.loop, int) and t.offset < DC * len(self.jobs):
                        chunk(eng, t.offset)
                return stage

        with ExitStack() as ph:
            HOT_TILES, HIST_TILES = 10, 4
            assert ET % HOT_TILES == 0 and ET % HIST_TILES == 0
            edge_ints = sb("edge_ints", [P, 2, ET], I32, ph)
            weight_in = sb("weight_in", [P, ET], F32, ph)
            src_all_i = sb("src_all_i", [P, E], I32, ph)
            src_all = sb("src_all", [P, EP], F32, ph)
            rec = sb("rec", [P, ET, 4], F32, ph)
            hi_i = sb("hi_i", [P, ET], I32, ph)
            lo_i = sb("lo_i", [P, ET], I32, ph)
            hi_of = sb("hi_of", [P, ET], F32, ph)
            lo_of = sb("lo_of", [P, ET], F32, ph)
            iota_i = sb("iota_i", [P, P], I32, ph)
            iota_part_i = sb("iota_part_i", [P, 1], I32, ph)
            iota = sb("iota", [P, P], F32, ph)
            iota_part = sb("iota_part", [P, 1], F32, ph)
            ident_b = sb("ident_b", [P, P], BF16, ph)
            earlier = sb("earlier", [P, P], F32, ph)
            below = sb("below", [P, P], F32, ph)
            ones_row = sb("ones_row", [P, P], F32, ph)
            hot_lo = sb("hot_lo", [P, ET * P], BF16, ph)
            hot_hi = sb("hot_hi", [P, ET * P], BF16, ph)
            hist = sb("hist", [P, P, ET + 1], F32, ph)
            tile_mask = sb("tile_mask", [P, P, ET + 1], BF16, ph)
            prefix = sb("prefix", [P, P], F32, ph)
            row_offset = sb("row_offset", [P, 1], F32, ph)
            row_offset1 = sb("row_offset1", [P, 1], F32, ph)
            base = sb("base", [P, P], F32, ph)
            empty = sb("empty", [P, P], F32, ph)
            last_pos = sb("last_pos", [P, P], F32, ph)
            table = sb("table", [P, 2, 2 * P], F32, ph)
            hot_hi_t = sb("hot_hi_t", [P, 2, P], F32, ph)
            rank_a = sb("rank_a", [P, ET], F32, ph)
            rank_b = sb("rank_b", [P, ET], F32, ph)
            junk = sb("junk_prep", [P, 3, P], F32, ph)
            cur_rank = sb("cur_rank", [P, UNROLL], I32, ph)
            cur_rec = sb("cur_rec", [P, UNROLL, 4], F32, ph)
            guard = sb("guard", [1, 4], F32, ph)
            back = sb("back", [ET, P + 2, 4], F32, ph)
            same_t = sb("same_t", [ET, P], BF16, ph)
            src_t = sb("src_t", [ET, P], F32, ph)
            same_next = sb("same_next", [ET, P], F32, ph)
            last_t = sb("last_t", [ET, P], F32, ph)
            col_t = sb("col_t", [ET, 3, P], F32, ph)
            p_hist = [pb(f"p_hist{k}", [P, HIST_TILES * P], F32, ph) for k in range(2)]
            p_hot = [pb(f"p_hot{k}", [P, P], BF16, ph) for k in range(2)]
            p_look = [pb(f"p_look{k}", [P, 2 * P], F32, ph) for k in range(2)]
            p_misc = pb("p_misc", [P, 512], F32, ph)

            edges_in = sem("edges_in")
            src_all_in = sem("src_all_in")
            src_all_done = sem("src_all_done")
            edge_clear = sem("edge_clear")
            iotas = sem("iotas")
            consts = sem("consts")
            hot_done = sem("hot_done")
            hist_mm = sem("hist_mm")
            hist_copied = sem("hist_copied")
            hist_sum = sem("hist_sum")
            mask_made = sem("mask_made")
            chain = sem("prep_chain")
            prefix_done = sem("prefix_done")
            last_pos_done = sem("last_pos_done")
            offsets_mm = sem("offsets_mm")
            nodes_mm = sem("nodes_mm")
            table_done = Count(sem("table_done"))
            hot_turned = Count(sem("hot_turned"))
            hot_copied = Count(sem("hot_copied"))
            looked = Count(sem("looked"))
            ranked = Count(sem("ranked"))
            rank_summed = Count(sem("rank_summed"))
            rec_copied = Count(sem("rec_copied"))
            scattered = slots("scattered")
            guard_out = sem("guard_out")
            back_in = sem("back_in")
            rows_ready = sem("rows_ready")
            rows_out = sem("rows_out")
            cols_mm = sem("cols_mm")
            cols_ready = sem("cols_ready")
            first_weights = WeightSplit(ph, [(w_neigh0, 0), (w_self0, 1)])
            block = ph.enter_context(nc.Block())

            @block.sync
            def _(sp):
                sp.wait_ge(edge_clear, 1)
                sp.dma_start(edge_ints[0:ER, 0, :], src.rearrange("(p t) -> p t", t=ET)).then_inc(edges_in, 16)
                sp.dma_start(edge_ints[0:ER, 1, :], dst.rearrange("(p t) -> p t", t=ET)).then_inc(edges_in, 16)
                sp.dma_start(weight_in[0:ER, :], edge_weight.rearrange("(p t) -> p t", t=ET)).then_inc(edges_in, 16)
                sp.dma_start(src_all_i[:], src.partition_broadcast(P)).then_inc(src_all_in, 16)
                first_weights.load(sp)
                sp.wait_ge(edge_clear, 2)
                sp.dma_start(records[0:1, :], guard[:]).then_inc(guard_out, 16)
                sp.dma_start(records[EP + 1:EP + 2, :], guard[:]).then_inc(guard_out, 16)
                sp.wait_ge(guard_out, 32)
                for s, v in scattered.used(ET):
                    sp.wait_ge(s, v)
                for t in range(0, ET, 8):
                    sp.dma_start(back[t:t + 8], bass.AP(records.tensor, 4 * P * t, [[4 * P, 8], [1, 4 * (P + 2)]])
                                 .rearrange("t (l f) -> t l f", f=4)).then_inc(back_in, 16)
                sp.wait_ge(rows_ready, 2)
                sp.dma_start(same_run_row.rearrange("o (t l) -> (o t) l", l=P), same_t[:]).then_inc(rows_out, 16)
                sp.dma_start(sorted_src_row[:, 1:EP + 1].rearrange("o (t l) -> (o t) l", l=P), src_t[:])\
                    .then_inc(rows_out, 16)
                sp.dma_start(sorted_src_row[:, 0:1], guard[:, 0:1]).then_inc(rows_out, 16)
                sp.wait_ge(rows_out, 48)
                sp.dma_start(same_run[:], same_run_row[0, :].partition_broadcast(P)).then_inc(rows_in, 16)

            @block.gpsimd
            def _(pool):
                nc.gpsimd.iota(iota_i[:], [[1, P]], base=0, channel_multiplier=0).then_inc(iotas, 1)
                nc.gpsimd.iota(iota_part_i[:], [[0, 1]], base=0, channel_multiplier=1).then_inc(iotas, 1)

                nc.gpsimd.memset(tile_mask[:], 1.0).then_inc(mask_made, 1)
                pool.wait_ge(mask_made, 1)
                nc.gpsimd.memset(tile_mask[:, :, 0:1], 0.0).then_inc(mask_made, 1)
                pool.wait_ge(src_all_in, 16)
                nc.gpsimd.tensor_copy(src_all[:, 0:E], src_all_i[:]).then_inc(src_all_done, 1)

                def scatter_records(t):
                    pool.wait_ge(rank_summed.sem, rank_summed.upto(t))
                    pool.wait_ge(rec_copied.sem, rec_copied.upto(t))
                    pool.sem_inc(pool_steps, 1)
                    nc.gpsimd.indirect_dma_start(
                        records, bass.IndirectOffsetOnAxis(ap=cur_rank[:, t.slot:t.slot + 1], axis=0),
                        cur_rec[:, t.slot, :], None).then_inc(scattered.sem(t), 16)

                in_steps(pool, ET, [(0, scatter_records)])

            @block.scalar
            def _(act):
                for group in range(ET // HIST_TILES):
                    act.wait_ge(hist_mm, group + 1)
                    at = group * HIST_TILES + 1
                    nc.scalar.activation(hist[:, :, at:at + HIST_TILES],
                                         p_hist[group % 2][:].rearrange("p (t j) -> p j t", j=P), ACT.Copy)\
                        .then_inc(hist_copied, 1)
                first_weights.high(act)

                def copy_hot(t):
                    act.wait_ge(hot_turned.sem, hot_turned.upto(t))
                    if t.has(2):
                        act.wait_ge(looked.sem, looked.upto(t, 2))
                    nc.scalar.activation(hot_hi_t[:, t.half, :], p_hot[t.half][:], ACT.Copy).then_inc(hot_copied.sem, 1)

                def copy_rec(t):
                    act.wait_ge(ranked.sem, ranked.upto(t))
                    if t.has(UNROLL):
                        act.wait_ge(scattered.sem(t), scattered.landed(t, 1))
                    nc.scalar.activation(cur_rec[:, t.slot, :].unsqueeze(1), rec[:, bass.ds(t.times(1), 1), :],
                                         ACT.Copy).then_inc(rec_copied.sem, 1)

                in_steps(act, ET, [(0, copy_hot), (3, copy_rec)])

            @block.vector
            def _(dve):
                links = [0]

                def link(ins):
                    links[0] += 1
                    ins.then_inc(chain, 1)
                    dve.wait_ge(chain, links[0])

                nc.vector.memset(edge_ints[:, 0, :], PAD_NODE)
                nc.vector.memset(edge_ints[:, 1, :], 0)
                nc.vector.memset(weight_in[:], 0.0).then_inc(edge_clear, 1)
                nc.vector.memset(guard[:], -1.0).then_inc(edge_clear, 1)
                nc.vector.memset(src_all[:, E:EP], float(PAD_NODE))
                nc.vector.memset(ones_row[:], 1.0)
                nc.vector.memset(mean_factor[:], -1.0 / D)
                for k, (_, term) in enumerate(NESTED_VARIANCE):
                    nc.vector.memset(var_term[:, k:k + 1], term)
                link(nc.vector.memset(hist[:, :, 0:1], 0.0))
                dve.wait_ge(iotas, 2)
                nc.vector.tensor_copy(iota[:], iota_i[:])
                link(nc.vector.tensor_copy(iota_part[:], iota_part_i[:]))
                nc.vector.tensor_scalar(ident[:], iota[:], iota_part[:, 0:1], None, ALU.is_equal)
                nc.vector.tensor_scalar(ident_b[:], iota[:], iota_part[:, 0:1], None, ALU.is_equal).then_inc(consts, 1)
                nc.vector.tensor_scalar(earlier[:], iota[:], iota_part[:, 0:1], None, ALU.is_lt)
                nc.vector.tensor_scalar(below[:], iota[:], iota_part[:, 0:1], None, ALU.is_gt).then_inc(consts, 1)
                dve.wait_ge(edges_in, 48)
                nc.vector.tensor_copy(rec[:, :, 0], edge_ints[:, 0, :])
                nc.vector.tensor_copy(rec[:, :, 1], edge_ints[:, 1, :])
                nc.vector.tensor_copy(rec[:, :, 2], weight_in[:])
                nc.vector.tensor_scalar(hi_i[:], edge_ints[:, 0, :], 7, None, ALU.arith_shift_right)
                link(nc.vector.tensor_scalar(lo_i[:], edge_ints[:, 0, :], P - 1, None, ALU.bitwise_and))
                nc.vector.tensor_copy(hi_of[:], hi_i[:])
                link(nc.vector.tensor_copy(lo_of[:], lo_i[:]))

                for t in range(0, ET, HOT_TILES):
                    for hot, part in ((hot_lo, lo_of), (hot_hi, hi_of)):
                        last = nc.vector.tensor_tensor(
                            hot[:, t * P:(t + HOT_TILES) * P].rearrange("p (t j) -> p t j", j=P),
                            iota[:].unsqueeze(1).to_broadcast([P, HOT_TILES, P]),
                            part[:, t:t + HOT_TILES].unsqueeze(2).to_broadcast([P, HOT_TILES, P]), ALU.is_equal)
                    last.then_inc(hot_done, 1)

                dve.wait_ge(mask_made, 2)
                dve.wait_ge(hist_copied, ET // HIST_TILES)
                by_tile = hist[:].rearrange("p j t -> p (j t)")
                nc.vector.tensor_tensor_scan(by_tile, tile_mask[:].rearrange("p j t -> p (j t)"), by_tile, 0.0,
                                             ALU.mult, ALU.add).then_inc(hist_sum, 1)
                total = hist[:, :, ET:ET + 1].rearrange("p j o -> p (j o)")
                dve.wait_ge(hist_sum, 1)
                nc.vector.tensor_tensor_scan(prefix[:], ones_row[:], total, 0.0, ALU.mult, ALU.add)\
                    .then_inc(prefix_done, 1)
                dve.wait_ge(prefix_done, 1)
                dve.wait_ge(offsets_mm, 1)
                nc.vector.tensor_scalar(row_offset[:], p_misc[:, 0:1], 1.0, None, ALU.add)
                nc.vector.tensor_scalar(row_offset1[:], p_misc[:, 0:1], -1.0, None, ALU.add)
                link(nc.vector.tensor_scalar(empty[:], total, 0.0, float(NOWHERE), ALU.is_equal, ALU.mult))
                nc.vector.scalar_tensor_tensor(last_pos[:], prefix[:], row_offset1[:, 0:1], empty[:], ALU.add, ALU.add)\
                    .then_inc(last_pos_done, 1)
                nc.vector.tensor_copy(table[:, 0, P:2 * P], total)
                nc.vector.tensor_copy(table[:, 1, P:2 * P], total)
                link(nc.vector.scalar_tensor_tensor(base[:], prefix[:], row_offset[:, 0:1], total, ALU.add, ALU.subtract))

                def make_table(t):
                    if t.has(2):
                        dve.wait_ge(looked.sem, looked.upto(t, 2))
                    nc.vector.tensor_tensor(table[:, t.half, 0:P], base[:],
                                            hist[:, :, bass.ds(t.times(1), 1)].rearrange("p j o -> p (j o)"),
                                            ALU.add).then_inc(table_done.sem, 1)

                def rank(t):
                    column = bass.ds(t.times(1), 1)
                    same = src_all[:].rearrange("p (q t) -> p q t", t=ET)[:, :, column]
                    if t.has(1):
                        dve.wait_ge(ranked.sem, ranked.upto(t, 1))
                    nc.vector.scalar_tensor_tensor(junk[:, 0, :], same.rearrange("p q o -> p (q o)"), rec[:, column, 0],
                                                   earlier[:], ALU.is_equal, ALU.mult, accum_out=rank_b[:, column])
                    at = bass.ds(t.times(P), P)
                    dve.wait_ge(looked.sem, looked.upto(t))
                    nc.vector.scalar_tensor_tensor(junk[:, 1, :], p_look[t.half][:, 0:P], 1.0, hot_lo[:, at],
                                                   ALU.mult, ALU.mult, accum_out=rank_a[:, column])
                    nc.vector.scalar_tensor_tensor(junk[:, 2, :], p_look[t.half][:, P:2 * P], 1.0, hot_lo[:, at],
                                                   ALU.mult, ALU.mult, accum_out=rec[:, column, 3])\
                        .then_inc(ranked.sem, 1)

                def sum_rank(t):
                    column = bass.ds(t.times(1), 1)
                    dve.wait_ge(ranked.sem, ranked.upto(t))
                    if t.has(UNROLL):
                        dve.wait_ge(scattered.sem(t), scattered.landed(t, 1))
                    nc.vector.tensor_tensor(cur_rank[:, t.slot:t.slot + 1], rank_a[:, column], rank_b[:, column],
                                            ALU.add)\
                        .then_inc(rank_summed.sem, 1)

                dve.wait_ge(src_all_done, 1)
                in_steps(dve, ET, [(0, make_table), (3, sum_rank), (2, rank)])
                dve.wait_ge(nodes_mm, 1)
                nc.vector.tensor_scalar(node_idx[:], p_misc[:, 128:128 + NT], float(EP), None, ALU.min)
                first_weights.low(dve)
                dve.wait_ge(back_in, 16 * (ET // 8))
                nc.vector.tensor_tensor(same_t[:], back[:, 1:P + 1, 0], back[:, 0:P, 0], ALU.is_equal)\
                    .then_inc(rows_ready, 1)
                nc.vector.tensor_copy(src_t[:], back[:, 1:P + 1, 0]).then_inc(rows_ready, 1)
                for f in range(3):
                    last = nc.vector.tensor_copy(col_t[:, f, :], back[:, 1:P + 1, f + 1])
                link(nc.vector.tensor_tensor(same_next[:], back[:, 2:P + 2, 0], back[:, 1:P + 1, 0], ALU.is_equal))
                last = nc.vector.scalar_tensor_tensor(last_t[:], same_next[:], float(NOWHERE), back[:, 1:P + 1, 0],
                                                      ALU.mult, ALU.add)
                last.then_inc(rows_ready, 1)
                dve.wait_ge(cols_mm, 1)
                nc.vector.tensor_copy(last_idx[:], p_misc[:, 256 + 4 * ET:256 + 5 * ET])
                nc.vector.tensor_copy(src_at[:], p_misc[:, 256:256 + ET])
                nc.vector.tensor_scalar(src_idx[:], p_misc[:, 256:256 + ET], float(N - 1), None, ALU.min)
                nc.vector.tensor_copy(dst_idx[:], p_misc[:, 256 + ET:256 + 2 * ET])
                nc.vector.tensor_copy(weight_at[:], p_misc[:, 256 + 2 * ET:256 + 3 * ET])
                link(nc.vector.tensor_scalar(invdeg_at[:], p_misc[:, 256 + 3 * ET:256 + 4 * ET], 1.0, None, ALU.max))
                nc.vector.reciprocal(invdeg_at[:], invdeg_at[:]).then_inc(cols_ready, 1)

            @block.tensor
            def _(pe):
                for t in range(ET):
                    if t % HOT_TILES == 0:
                        pe.wait_ge(hot_done, t // HOT_TILES + 1)
                    group, k = divmod(t, HIST_TILES)
                    if k == 0 and group >= 2:
                        pe.wait_ge(hist_copied, group - 1)
                    last = nc.tensor.matmul(p_hist[group % 2][:, k * P:(k + 1) * P], hot_hi[:, t * P:(t + 1) * P],
                                            hot_lo[:, t * P:(t + 1) * P], start=True, stop=True)
                    if k == HIST_TILES - 1:
                        last.then_inc(hist_mm, 1)
                pe.wait_ge(consts, 2)
                pe.wait_ge(prefix_done, 1)
                nc.tensor.matmul(p_misc[:, 0:1], below[:], prefix[:, P - 1:P], start=True, stop=True)\
                    .then_inc(offsets_mm, 1)

                def turn(t):
                    pe.wait_ge(consts, 2)
                    if t.has(2):
                        pe.wait_ge(hot_copied.sem, hot_copied.upto(t, 2))
                    nc.tensor.transpose(p_hot[t.half][:], hot_hi[:, bass.ds(t.times(P), P)], ident_b[:])\
                        .then_inc(hot_turned.sem, 1)

                def look(t):
                    pe.wait_ge(hot_copied.sem, hot_copied.upto(t))
                    pe.wait_ge(table_done.sem, table_done.upto(t))
                    if t.has(2):
                        pe.wait_ge(ranked.sem, ranked.upto(t, 2))
                    nc.tensor.matmul(p_look[t.half][:], hot_hi_t[:, t.half, :], table[:, t.half, :],
                                     start=True, stop=True).then_inc(looked.sem, 1)

                in_steps(pe, ET, [(0, turn), (1, look)])
                pe.wait_ge(last_pos_done, 1)
                nc.tensor.transpose(p_misc[:, 128:256], last_pos[:], ident[:]).then_inc(nodes_mm, 1)
                pe.wait_ge(rows_ready, 3)
                for f, rows in enumerate((src_t[:], col_t[:, 0, :], col_t[:, 1, :], col_t[:, 2, :], last_t[:])):
                    last = nc.tensor.transpose(p_misc[:, 256 + f * ET:256 + (f + 1) * ET], rows, ident[0:ET, 0:ET])
                last.then_inc(cols_mm, 1)

        gathered = slots("gathered")
        gathered2 = slots("gathered2")
        index_picked = Count(sem("index_picked"))
        last_picked = Count(sem("last_picked"))
        own_picked = Count(sem("own_picked"))
        both_picked = Count(sem("both_picked"), 2)
        scaled = Count(sem("scaled"))
        turned = Count(sem("turned"))
        summed = Count(sem("summed"))
        high_done = Count(sem("high_done"))
        low_done = Count(sem("low_done"))
        product_done = Count(sem("product_done"))
        rows_done = Count(sem("rows_done"))
        rows_stored = slots("rows_stored")
        stored_twice = slots("stored_twice")
        rows_scattered = slots("rows_scattered")
        out_stored = slots("out_stored")
        consts_in = Count(sem("consts_in"), 16)
        node_gathered = slots("node_gathered")
        node_stored = slots("node_stored")
        node_index_picked = Count(sem("node_index_picked"))
        node_turned = Count(sem("node_turned"))
        node_high_done = Count(sem("node_high_done"))
        node_low_done = Count(sem("node_low_done"))
        node_product_done = Count(sem("node_product_done"))
        node_consts_in = Count(sem("node_consts_in"), 16)
        consts_made = Count(sem("consts_made"))
        fill_stored = Count(sem("fill_stored"), 16)
        x_landed = slots("x_landed")
        preact_done = Count(sem("preact_done"))
        y_done = Count(sem("y_done"))
        x_plus_beta = Count(sem("x_plus_beta"))
        scaled_gamma = Count(sem("scaled_gamma"))
        y2_done = Count(sem("y2_done"))

        class Norm:

            def __init__(self, name):
                self.mean = Count(sem(f"{name}_mean"))
                self.squares = Count(sem(f"{name}_squares"))
                self.std = Count(sem(f"{name}_std"))
                self.rstd = Count(sem(f"{name}_rstd"))
                self.scale = Count(sem(f"{name}_scale"))
                self.applied = Count(sem(f"{name}_applied"))

            def close(self, n, counts=None):
                for count in counts or (self.mean, self.squares, self.std, self.rstd, self.scale, self.applied):
                    count.close(n)

        norm_inner = Norm("inner")
        norm_outer = Norm("outer")
        applied_twice = Count(sem("applied_twice"))
        ratio_done = Count(sem("ratio_done"))
        out_scaled = Count(sem("out_scaled"), 2)
        SUM, NEG_MEAN, SQUARES, STD, RSTD, SHIFT = 0, 1, 2, 3, 6, 9
        STATS = 12

        def norm_steps(norm, y, y_ready, stats, junk, target, target_free, width=1):

            def column(t, k, w=1):
                return stats[:, t.slot, k:k + w]

            def mean(eng, t):
                eng.wait_ge(y_ready.sem, y_ready.upto(t))
                eng.tensor_tensor(column(t, NEG_MEAN), column(t, SUM), mean_factor[:], ALU.mult)\
                    .then_inc(norm.mean.sem, 1)

            def squares(act, t):
                act.wait_ge(norm.mean.sem, norm.mean.upto(t))
                nc.scalar.activation(junk[:, t.half, :], y[:, t.slot, :], ACT.Square, bias=column(t, NEG_MEAN),
                                     accum_out=column(t, SQUARES)).then_inc(norm.squares.sem, 1)

            def std(act, t):
                act.wait_ge(norm.squares.sem, norm.squares.upto(t))
                for k, (factor, _) in enumerate(NESTED_VARIANCE[:width]):
                    last = nc.scalar.activation(column(t, STD + k), column(t, SQUARES), ACT.Sqrt,
                                                bias=var_term[:, k:k + 1], scale=factor / D)
                last.then_inc(norm.std.sem, 1)

            def rstd(dve, t):
                dve.wait_ge(norm.std.sem, norm.std.upto(t))
                nc.vector.reciprocal(column(t, RSTD, width), column(t, STD, width)).then_inc(norm.rstd.sem, 1)

            def shift(eng, t):
                eng.wait_ge(norm.rstd.sem, norm.rstd.upto(t))
                if width == 1:
                    shifted = eng.tensor_tensor(column(t, SHIFT), column(t, RSTD), column(t, NEG_MEAN), ALU.mult)
                else:
                    shifted = eng.tensor_scalar(column(t, SHIFT, width), column(t, RSTD, width), column(t, NEG_MEAN),
                                                None, ALU.mult)
                shifted.then_inc(norm.scale.sem, 1)

            def apply(act, t):
                act.wait_ge(norm.scale.sem, norm.scale.upto(t))
                target_free(act, t)
                nc.scalar.activation(target(t), y[:, t.slot, :], ACT.Identity, bias=column(t, SHIFT),
                                     scale=column(t, RSTD)).then_inc(norm.applied.sem, 1)

            steps = dict(mean=mean, squares=squares, std=std, rstd=rstd, shift=shift, apply=apply)
            return lambda name, eng: lambda t: steps[name](eng, t)

        def pick_index(eng, t, picked, cur, indices):
            eng.tensor_copy(cur[:, t.slot:t.slot + 1], indices[:, bass.ds(t.times(1), 1)])\
                .then_inc(picked.sem, 1)

        def index_ready(pool, t, picked):
            pool.wait_ge(picked.sem, picked.upto(t))
            pool.sem_inc(pool_steps, 1)

        def gather_rows(to, x_dram, cur, t, landed):
            nc.gpsimd.indirect_dma_start(to[:, t.slot, :], None, x_dram,
                                         bass.IndirectOffsetOnAxis(ap=cur[:, t.slot:t.slot + 1], axis=0))\
                .then_inc(landed.sem(t), 16)

        def scatter_steps(norm, cur, done, y_dram):
            def pick_last(eng, t):
                if t.has(UNROLL):
                    eng.wait_ge(rows_scattered.sem(t), rows_scattered.landed(t, 1))
                pick_index(eng, t, last_picked, cur, last_idx)

            def scatter(t):
                nc.gpsimd.wait_ge(norm.applied.sem, norm.applied.upto(t))
                index_ready(nc.gpsimd, t, last_picked)
                nc.gpsimd.indirect_dma_start(
                    y_dram, bass.IndirectOffsetOnAxis(ap=cur[:, t.slot:t.slot + 1], axis=0),
                    done[:, t.slot, :], None, bounds_check=N - 1, oob_is_err=False).then_inc(rows_scattered.sem(t), 16)

            return pick_last, scatter

        def split_product(bank, hi, lo, slot, w_cols=slice(None)):
            for c in range(DC):
                for a, w in ((hi, w_hi), (hi, w_lo), (lo, w_hi)):
                    last = nc.tensor.matmul(bank, a[:, c, :], w[slot][:, c, w_cols],
                                            start=(c == 0 and a is hi and w is w_hi),
                                            stop=(c == DC - 1 and a is lo))
            return last

        def edge_programs(ph, layer, x_dram, slot, biases, jobs, late_jobs=(), y_dram=None, load_first=None):
            by_weight, by_degree, to_nodes = layer == 2, layer == 0, y_dram is not None
            e = sb(f"e{layer}", [P, UNROLL, D], F32, ph)
            cur = sb(f"cur_e{layer}", [P, UNROLL], I32, ph)
            hi = sb(f"edge_hi{layer}", [P, UNROLL, DC, P], F32R, ph)
            lo = sb(f"edge_lo{layer}", [P, UNROLL, DC, P], F32R, ph)
            rows = sb(f"rows{layer}", [P, UNROLL, D], F32, ph)
            bias_in = sb(f"bias_in_e{layer}", [P, 2, D], F32, ph)
            bias = sb(f"bias_e{layer}", [P, D], F32, ph)
            turned_bank = [pb(f"pt_e{layer}{k}", [P, DC, P], F32, ph) for k in range(2)]
            sums = sb(f"sums{layer}", [P, UNROLL, DC, P], F32, ph)
            product_bank = [pb(f"pp_e{layer}{k}", [P, D], F32, ph) for k in range(2)]
            if to_nodes:
                own = sb(f"own{layer}", [P, UNROLL, D], F32, ph)
                cur_own = sb(f"cur_own{layer}", [P, UNROLL], I32, ph)
                cur_last = sb(f"cur_last{layer}", [P, UNROLL], I32, ph)
                y = sb(f"y{layer}", [P, UNROLL, D], F32, ph)
                junk = sb(f"junk_e{layer}", [P, 2, D], F32, ph)
                stats = sb(f"stats{layer}", [P, UNROLL, STATS], F32, ph)

                def rows_free(act, t):
                    if t.has(UNROLL):
                        act.wait_ge(rows_scattered.sem(t), rows_scattered.landed(t, 1))

                norm = norm_steps(norm_outer, y, y_done, stats, junk, lambda t: rows[:, t.slot, :], rows_free)
                pick_last, scatter = scatter_steps(norm_outer, cur_last, rows, y_dram)
            weights = WeightSplit(ph, jobs)
            late_weights = WeightSplit(ph, late_jobs, sem("late_weight_landed")) if late_jobs else None
            def sync(sp):
                for k, b in enumerate(biases):
                    sp.dma_start(bias_in[:, k, :], b.partition_broadcast(P)).then_inc(consts_in.sem, 16)
                if biases:
                    sp.wait_ge(consts_made.sem, consts_made.all(1))
                    fill = bias_in[0:1, 0, :] if by_degree else bias[0:1, :]
                    sp.dma_start(neigh_rows[EP:EP + 1, :], fill).then_inc(fill_stored.sem, 16)

                def store(t):
                    sp.wait_ge(rows_done.sem, rows_done.upto(t))
                    sp.dma_start(neigh_rows[bass.ds(t.times(P), P), :], rows[:, t.slot, :])\
                        .then_inc(rows_stored.sem(t), 16)

                def load_weights(t):
                    if isinstance(t.loop, int) and t.offset == 0:
                        weights.load(sp)
                        if late_jobs:
                            late_weights.load(sp)

                def prefetch(t):
                    if isinstance(t.loop, int) and t.offset == 0:
                        load_first(sp)

                if to_nodes:
                    load_weights(Tile(0, 0))
                else:
                    in_steps(sp, ET, [(0, store), (0, load_weights), (8, prefetch)])
                if to_nodes:
                    for s, v in rows_scattered.used(ET):
                        sp.wait_ge(s, v)

            def gpsimd(pool):
                def pick_neighbour(t):
                    if t.has(UNROLL):
                        pool.wait_ge(turned.sem, turned.upto(t, UNROLL))
                    pick_index(pool, t, index_picked, cur, dst_idx)

                def gather(t):
                    index_ready(pool, t, index_picked)
                    gather_rows(e, x_dram, cur, t, gathered)

                def gather_own(t):
                    if t.has(UNROLL):
                        pool.wait_ge(y_done.sem, y_done.upto(t, UNROLL))
                    index_ready(pool, t, own_picked)
                    gather_rows(own, x_dram, cur_own, t, gathered2)

                if to_nodes:
                    in_steps(pool, ET, [(0, pick_neighbour), (4, gather_own), (0, gather), (10, scatter)])
                else:
                    in_steps(pool, ET, [(0, pick_neighbour), (0, gather)])

            def scalar(act):
                def weigh(t):
                    act.wait_ge(gathered.sem(t), gathered.landed(t))
                    nc.scalar.activation(e[:, t.slot, :], e[:, t.slot, :], ACT.Copy,
                                         scale=weight_at[:, bass.ds(t.times(1), 1)]).then_inc(scaled.sem, 1)

                def high(t):
                    act.wait_ge(summed.sem, summed.upto(t))
                    if t.has(UNROLL):
                        act.wait_ge(product_done.sem, product_done.upto(t, UNROLL))
                    nc.scalar.activation(hi[:, t.slot], sums[:, t.slot], ACT.Copy).then_inc(high_done.sem, 1)

                stages = [(2, high), (6, weights.early(weights.high_chunk, act))]
                if by_weight:
                    stages = [(0, weigh)] + stages
                if to_nodes:
                    stages += [(6, norm("squares", act)), (6, norm("std", act)), (8, norm("apply", act))]
                in_steps(act, ET, stages)
                if late_jobs:
                    act.wait_ge(product_done.sem, product_done.all(ET))
                    late_weights.high(act)

            def vector(dve):
                if biases:
                    dve.wait_ge(consts_in.sem, consts_in.all(len(biases)))
                    nc.vector.tensor_tensor(bias[:], bias_in[:, 0, :], bias_in[:, 1, :], ALU.add)\
                        .then_inc(consts_made.sem, 1)

                if layer == 0:
                    dve.wait_ge(rows_in, 16)

                def run_sums(t):
                    dve.wait_ge(turned.sem, turned.upto(t))
                    if t.has(UNROLL):
                        dve.wait_ge(high_done.sem, high_done.upto(t, UNROLL))
                        dve.wait_ge(low_done.sem, low_done.upto(t, UNROLL))
                    if t.has(1):
                        dve.wait_ge(summed.sem, summed.upto(t, 1))
                    for c in range(DC):
                        start = sums[:, (t.slot - 1) % UNROLL, c, P - 1:P] if t.has(1) else 0.0
                        last = nc.vector.tensor_tensor_scan(
                            sums[:, t.slot, c, :], same_run[:, bass.ds(t.times(P), P)],
                            turned_bank[t.half][:, c, :], start, ALU.mult, ALU.add)
                    last.then_inc(summed.sem, 1)

                def low(t):
                    dve.wait_ge(high_done.sem, high_done.upto(t))
                    if t.has(UNROLL):
                        dve.wait_ge(product_done.sem, product_done.upto(t, UNROLL))
                    nc.vector.tensor_tensor(lo[:, t.slot], sums[:, t.slot], hi[:, t.slot].bitcast(F32),
                                            ALU.subtract).then_inc(low_done.sem, 1)

                def rows_out(t):
                    dve.wait_ge(product_done.sem, product_done.upto(t))
                    if t.has(UNROLL):
                        dve.wait_ge(rows_stored.sem(t), rows_stored.landed(t, 1))
                    if not t.has(1):
                        dve.wait_ge(consts_made.sem, consts_made.all(1))
                    factor = invdeg_at[:, bass.ds(t.times(1), 1)] if by_degree else 1.0
                    nc.vector.scalar_tensor_tensor(rows[:, t.slot, :], product_bank[t.half][:], factor, bias[:],
                                                   ALU.mult, ALU.add).then_inc(rows_done.sem, 1)

                def residual(t):
                    dve.wait_ge(product_done.sem, product_done.upto(t))
                    dve.wait_ge(gathered2.sem(t), gathered2.landed(t))
                    if t.has(UNROLL):
                        dve.wait_ge(norm_outer.applied.sem, norm_outer.applied.upto(t, UNROLL))
                    nc.vector.scalar_tensor_tensor(
                        y[:, t.slot, :], product_bank[t.half][:], 1.0, own[:, t.slot, :], ALU.mult, ALU.add,
                        accum_out=stats[:, t.slot, SUM:SUM + 1]).then_inc(y_done.sem, 1)

                def pick_own(t):
                    if t.has(UNROLL):
                        dve.wait_ge(gathered2.sem(t), gathered2.landed(t, 1))
                    pick_index(dve, t, own_picked, cur_own, src_idx)

                if to_nodes:
                    in_steps(dve, ET, [(0, pick_own), (6, lambda t: pick_last(dve, t)),
                                       (7, norm("rstd", dve)), (5, residual), (7, norm("shift", dve)),
                                       (2, low), (5, norm("mean", dve)), (1, run_sums),
                                       (7, weights.early(weights.low_chunk, dve))])
                else:
                    in_steps(dve, ET, [(1, run_sums), (2, low), (4, rows_out),
                                       (7, weights.early(weights.low_chunk, dve))])
                if late_jobs:
                    late_weights.low(dve)

            def tensor(pe):
                def turn(t):
                    if by_weight:
                        pe.wait_ge(scaled.sem, scaled.upto(t))
                    else:
                        pe.wait_ge(gathered.sem(t), gathered.landed(t))
                    if t.has(2):
                        pe.wait_ge(summed.sem, summed.upto(t, 2))
                    for c in range(DC):
                        last = nc.tensor.transpose(turned_bank[t.half][:, c, :], e[:, t.slot, c * P:(c + 1) * P],
                                                   ident[:])
                    last.then_inc(turned.sem, 1)

                def product(t):
                    pe.wait_ge(low_done.sem, low_done.upto(t))
                    if t.has(2):
                        reader = y_done if to_nodes else rows_done
                        pe.wait_ge(reader.sem, reader.upto(t, 2))
                    split_product(product_bank[t.half][:], hi[:, t.slot], lo[:, t.slot], slot)\
                        .then_inc(product_done.sem, 1)

                in_steps(pe, ET, [(0, turn), (3, product)])

            def close():
                for count in (index_picked, turned, summed, high_done, low_done, product_done):
                    count.close(ET)
                for ring in (gathered, rows_scattered if to_nodes else rows_stored):
                    ring.close(ET)
                if by_weight:
                    scaled.close(ET)
                if biases:
                    consts_in.close(len(biases))
                    consts_made.close(1)
                    fill_stored.close(1)
                if to_nodes:
                    for count in (own_picked, y_done, last_picked):
                        count.close(ET)
                    gathered2.close(ET)
                    norm_outer.close(ET)
                else:
                    rows_done.close(ET)

            return sync, gpsimd, scalar, vector, tensor, close

        def node_programs(ph, layer, x_dram, y_drams, slot, jobs):
            inner = layer == 0
            nested = not inner
            xs = sb(f"x{layer}", [P, UNROLL, D], F32, ph)
            g = sb(f"g{layer}", [P, UNROLL, D], F32, ph)
            cur = sb(f"cur_n{layer}", [P, UNROLL], I32, ph)
            hi = sb(f"x_hi{layer}", [P, 2, DC, P], F32R, ph)
            lo = sb(f"x_lo{layer}", [P, 2, DC, P], F32R, ph)
            y = sb(f"y{layer}", [P, UNROLL, D], F32, ph)
            done = [sb(f"done{layer}{k}", [P, UNROLL, D], F32, ph) for k in range(len(y_drams))]
            junk = sb(f"junk_n{layer}", [P, 2, D], F32, ph)
            stats = sb(f"stats{layer}", [P, UNROLL, STATS], F32, ph)
            gamma_beta = sb(f"gamma_beta{layer}", [P, 2, D], F32, ph)
            turned_bank = [pb(f"pt_n{layer}{k}", [P, DC, P], F32, ph) for k in range(2)]
            product_bank = [pb(f"pp_n{layer}{k}", [P, D], F32, ph) for k in range(2)]
            if inner:
                xb = sb("xb", [P, UNROLL, D], F32, ph)
                y2 = sb("y_outer", [P, UNROLL, D], F32, ph)
                stats2 = sb("stats_outer", [P, UNROLL, STATS], F32, ph)
                centered = sb("centered", [P, 2, D], F32, ph)
            weights = WeightSplit(ph, jobs)
            rows_in = [gamma, beta] if inner else []
            stores = [node_stored, stored_twice][:len(y_drams)]

            def done_free(act, t):
                if t.has(UNROLL):
                    act.wait_ge(node_stored.sem(t), node_stored.landed(t, 1))

            if inner:
                norm1 = norm_steps(norm_inner, y, y_done, stats, junk, None, None)
                norm2 = norm_steps(norm_outer, y2, y2_done, stats2, junk, lambda t: done[0][:, t.slot, :], done_free)
            else:
                norm1 = norm_steps(norm_outer, y, y_done, stats, junk, lambda t: done[0][:, t.slot, :], done_free,
                                   width=3)

            def load(sp, t):
                if t.has(UNROLL):
                    sp.wait_ge(y_done.sem, y_done.upto(t, UNROLL))
                    if inner:
                        sp.wait_ge(x_plus_beta.sem, x_plus_beta.upto(t, UNROLL))
                n = NREST if isinstance(t.loop, int) and t.offset == NT - 1 else P
                sp.dma_start(xs[0:n, t.slot, :], x_dram[bass.ds(t.times(P), n), :])\
                    .then_inc(x_landed.sem(t), 16)

            def load_first(sp):
                for k, b in enumerate(rows_in):
                    sp.dma_start(gamma_beta[:, k, :], b.partition_broadcast(P)).then_inc(node_consts_in.sem, 16)
                for n in range(UNROLL):
                    load(sp, Tile(0, n))

            def sync(sp):
                def load_next(t):
                    if t.has(UNROLL):
                        load(sp, t)

                def store(t):
                    n = NREST if isinstance(t.loop, int) and t.offset == NT - 1 else P
                    for k, y_dram in enumerate(y_drams):
                        applied = (norm_outer.applied, applied_twice)[k]
                        sp.wait_ge(applied.sem, applied.upto(t))
                        sp.dma_start(y_dram[bass.ds(t.times(P), n), :], done[k][0:n, t.slot, :])\
                            .then_inc(stores[k].sem(t), 16)

                def load_weights(t):
                    if isinstance(t.loop, int) and t.offset == 0:
                        weights.load(sp)

                in_steps(sp, NT, [(0, load_next), (3, load_weights), (11 if inner else 7, store)])
                for ring in stores:
                    for s, v in ring.used(NT):
                        sp.wait_ge(s, v)

            def gpsimd(pool):
                for s, v in rows_stored.used(ET):
                    pool.wait_ge(s, v)
                pool.wait_ge(fill_stored.sem, fill_stored.all(1))

                def fetch(t):
                    if t.has(UNROLL):
                        pool.wait_ge(preact_done.sem, preact_done.upto(t, UNROLL))
                    pick_index(pool, t, node_index_picked, cur, node_idx)
                    index_ready(pool, t, node_index_picked)
                    gather_rows(g, neigh_rows, cur, t, node_gathered)

                def add_beta(t):
                    pool.wait_ge(x_landed.sem(t), x_landed.landed(t))
                    if t.has(UNROLL):
                        pool.wait_ge(y2_done.sem, y2_done.upto(t, UNROLL))
                    nc.gpsimd.tensor_tensor(xb[:, t.slot, :], xs[:, t.slot, :], gamma_beta[:, 1, :], ALU.add)\
                        .then_inc(x_plus_beta.sem, 1)

                def apply_twice(t):
                    pool.wait_ge(norm_outer.scale.sem, norm_outer.scale.upto(t))
                    if t.has(UNROLL):
                        pool.wait_ge(stored_twice.sem(t), stored_twice.landed(t, 1))
                    pool.sem_inc(pool_steps, 1)
                    nc.gpsimd.tensor_scalar(done[1][:, t.slot, :], y[:, t.slot, :],
                                            stats[:, t.slot, RSTD + 1:RSTD + 2], stats[:, t.slot, SHIFT + 1:SHIFT + 2],
                                            ALU.mult, ALU.add).then_inc(applied_twice.sem, 1)

                if inner:
                    in_steps(pool, NT, [(0, fetch), (2, add_beta), (3, norm1("mean", pool)),
                                        (6, norm2("mean", pool)), (8, norm2("shift", pool))])
                else:
                    in_steps(pool, NT, [(0, fetch), (5, apply_twice)])

            def scalar(act):
                def high(t):
                    act.wait_ge(node_turned.sem, node_turned.upto(t))
                    if t.has(2):
                        act.wait_ge(node_product_done.sem, node_product_done.upto(t, 2))
                    nc.scalar.activation(hi[:, t.half], turned_bank[t.half][:], ACT.Copy)\
                        .then_inc(node_high_done.sem, 1)

                if inner:
                    stages = [(9, norm2("apply", act)), (0, high), (4, norm1("squares", act)),
                              (7, norm2("squares", act)), (4, norm1("std", act)), (7, norm2("std", act))]
                else:
                    stages = [(5, norm1("apply", act)), (0, high), (3, norm1("squares", act)),
                              (3, norm1("std", act))]
                def split_weights(t):
                    if isinstance(t.loop, int) and t.offset == 0:
                        act.wait_ge(product_done.sem, product_done.all(ET))
                    weights.early(weights.high_chunk, act)(t)

                in_steps(act, NT, stages + [(5, split_weights)])

            def vector(dve):
                if inner:
                    dve.wait_ge(node_consts_in.sem, node_consts_in.all(len(rows_in)))

                def low(t):
                    dve.wait_ge(node_high_done.sem, node_high_done.upto(t))
                    if t.has(2):
                        dve.wait_ge(node_product_done.sem, node_product_done.upto(t, 2))
                    nc.vector.tensor_tensor(lo[:, t.half], turned_bank[t.half][:], hi[:, t.half].bitcast(F32),
                                            ALU.subtract).then_inc(node_low_done.sem, 1)

                def preact(t):
                    dve.wait_ge(node_product_done.sem, node_product_done.upto(t))
                    dve.wait_ge(node_gathered.sem(t), node_gathered.landed(t))
                    nc.vector.tensor_tensor(product_bank[t.half][:], product_bank[t.half][:], g[:, t.slot, :],
                                            ALU.add).then_inc(preact_done.sem, 1)

                def residual(t):
                    dve.wait_ge(preact_done.sem, preact_done.upto(t))
                    if t.has(UNROLL):
                        if inner:
                            dve.wait_ge(norm_inner.squares.sem, norm_inner.squares.upto(t, UNROLL))
                            dve.wait_ge(scaled_gamma.sem, scaled_gamma.upto(t, UNROLL))
                        else:
                            for applied in (norm_outer.applied, applied_twice):
                                dve.wait_ge(applied.sem, applied.upto(t, UNROLL))
                    nc.vector.scalar_tensor_tensor(
                        y[:, t.slot, :], product_bank[t.half][:], 0.0, xs[:, t.slot, :], ALU.max, ALU.add,
                        accum_out=stats[:, t.slot, SUM:SUM + 1]).then_inc(y_done.sem, 1)

                def center(t):
                    dve.wait_ge(norm_inner.mean.sem, norm_inner.mean.upto(t))
                    if t.has(2):
                        dve.wait_ge(y2_done.sem, y2_done.upto(t, 2))
                    nc.vector.scalar_tensor_tensor(centered[:, t.half, :], y[:, t.slot, :],
                                                   stats[:, t.slot, NEG_MEAN:NEG_MEAN + 1], gamma_beta[:, 0, :],
                                                   ALU.add, ALU.mult).then_inc(scaled_gamma.sem, 1)

                def outer(t):
                    dve.wait_ge(norm_inner.rstd.sem, norm_inner.rstd.upto(t))
                    dve.wait_ge(scaled_gamma.sem, scaled_gamma.upto(t))
                    dve.wait_ge(x_plus_beta.sem, x_plus_beta.upto(t))
                    if t.has(UNROLL):
                        dve.wait_ge(norm_outer.applied.sem, norm_outer.applied.upto(t, UNROLL))
                    nc.vector.scalar_tensor_tensor(
                        y2[:, t.slot, :], centered[:, t.half, :], stats[:, t.slot, RSTD:RSTD + 1],
                        xb[:, t.slot, :], ALU.mult, ALU.add,
                        accum_out=stats2[:, t.slot, SUM:SUM + 1]).then_inc(y2_done.sem, 1)

                def ratio(t):
                    dve.wait_ge(norm_outer.rstd.sem, norm_outer.rstd.upto(t))
                    nc.vector.tensor_tensor(last_scale[:, bass.ds(t.times(1), 1)],
                                            stats[:, t.slot, STD + 1:STD + 2], stats[:, t.slot, RSTD + 2:RSTD + 3],
                                            ALU.mult).then_inc(ratio_done.sem, 1)

                if inner:
                    stages = [(2, preact), (8, norm2("rstd", dve)), (0, low), (5, norm1("rstd", dve)),
                              (2, residual), (4, center), (5, outer)]
                else:
                    stages = [(4, norm1("rstd", dve)), (2, preact), (4, norm1("shift", dve)), (2, residual),
                              (0, low), (4, ratio), (2, norm1("mean", dve))]
                in_steps(dve, NT, stages + [(6, weights.early(weights.low_chunk, dve))])

            def tensor(pe):
                def turn(t):
                    pe.wait_ge(x_landed.sem(t), x_landed.landed(t))
                    if t.has(2):
                        pe.wait_ge(node_low_done.sem, node_low_done.upto(t, 2))
                    for c in range(DC):
                        last = nc.tensor.transpose(turned_bank[t.half][:, c, :], xs[:, t.slot, c * P:(c + 1) * P],
                                                   ident[:])
                    last.then_inc(node_turned.sem, 1)

                def product(t):
                    pe.wait_ge(node_low_done.sem, node_low_done.upto(t))
                    if t.has(2):
                        pe.wait_ge(y_done.sem, y_done.upto(t, 2))
                    split_product(product_bank[t.half][:], hi[:, t.half], lo[:, t.half], slot)\
                        .then_inc(node_product_done.sem, 1)

                in_steps(pe, NT, [(0, turn), (1, product)])

            def close():
                for count in (node_index_picked, node_turned, node_high_done, node_low_done, node_product_done,
                              preact_done, y_done):
                    count.close(NT)
                for ring in [node_gathered, x_landed] + stores:
                    ring.close(NT)
                node_consts_in.close(len(rows_in))
                norm_outer.close(NT)
                if nested:
                    for count in (applied_twice, ratio_done):
                        count.close(NT)
                if inner:
                    for count in (norm_inner.mean, norm_inner.squares, norm_inner.std, norm_inner.rstd):
                        count.close(NT)
                    for count in (x_plus_beta, scaled_gamma, y2_done):
                        count.close(NT)

            return load_first, sync, gpsimd, scalar, vector, tensor, close

        def run_block(ph, *phases):
            block = ph.enter_context(nc.Block())

            @block.sync
            def _(sp):
                for sync, *_ in phases:
                    sync(sp)

            @block.gpsimd
            def _(pool):
                for _, gpsimd, *_ in phases:
                    gpsimd(pool)

            @block.scalar
            def _(act):
                for _, _, scalar, *_ in phases:
                    scalar(act)

            @block.vector
            def _(dve):
                for _, _, _, vector, *_ in phases:
                    vector(dve)

            @block.tensor
            def _(pe):
                for *_, tensor, _ in phases:
                    tensor(pe)

        def message_layer(layer, x_dram, edge_slot, biases, edge_jobs, y_drams, node_slot, node_jobs):
            with ExitStack() as ph:
                edge_phase = edge_programs(ph, layer, x_dram, edge_slot, biases, edge_jobs,
                                           load_first=lambda sp: load_first(sp))
                load_first, *node_phase = node_programs(ph, layer, x_dram, y_drams, node_slot, node_jobs)
                run_block(ph, edge_phase, node_phase)
            edge_phase[-1]()
            node_phase[-1]()

        def attention(x_dram, y_dram):
            with ExitStack() as keep:
                neighbours = sb("neighbours", [P, ET, DC, P], F32, keep)
                scores = sb("scores", [P, ET * HEADS], F32, keep)
                exps = sb("exps", [P, ET * HEADS], F32, keep)
                inverse = sb("inverse", [P, ET * HEADS], F32, keep)
                score_edges(x_dram, y_dram, neighbours, scores)
                softmax_terms(scores, exps, inverse)
                weighted_sums(neighbours, exps, inverse, x_dram, y_dram)

        def score_edges(x_dram, y_dram, neighbours, scores):
            with ExitStack() as ph:
                e = [sb(f"e_{side}", [P, UNROLL, D], F32, ph) for side in ("src", "dst")]
                cur = [sb(f"cur_{side}", [P, UNROLL], I32, ph) for side in ("src", "dst")]
                hi = [sb(f"hi_{side}", [P, 2, DC, P], F32R, ph) for side in ("src", "dst")]
                lo = [sb(f"lo_{side}", [P, 2, DC, P], F32R, ph) for side in ("src", "dst")]
                pair = sb("pair", [P, UNROLL, 2, D], F32, ph)
                q = sb("q", [P, 2, D], F32, ph)
                qk = sb("qk", [P, 2, D], F32, ph)
                turned_bank = [[pb(f"pt_{side}{k}", [P, DC, P], F32, ph) for k in range(2)] for side in ("src", "dst")]
                banks = {n: [pb(f"p{n}{k}", [P, D], F32, ph) for k in range(2)] for n in "qk"}
                landed = [gathered, gathered2]
                indices = [src_idx, dst_idx]
                kept = Count(sem("neighbours_kept"))
                q_copied = Count(sem("q_copied"))
                qk_done = Count(sem("qk_done"))
                scored = Count(sem("scored"))
                q_product_done = Count(sem("q_product_done"))
                block = ph.enter_context(nc.Block())

                @block.sync
                def _(sp):
                    def rows_of(dram, t):
                        if isinstance(t.loop, int) and t.offset == PAIRS:
                            return dram[PAIRS * 2 * P:N, :], pair[0:PAIR_REST, t.slot, 0, :]
                        return (dram[bass.ds(t.times(2 * P), 2 * P), :].rearrange("(k p) d -> p k d", p=P),
                                pair[:, t.slot])

                    def load(t):
                        if t.has(UNROLL):
                            sp.wait_ge(out_stored.sem(t), out_stored.landed(t, 1))
                        rows, place = rows_of(x_dram, t)
                        sp.dma_start(place, rows).then_inc(x_landed.sem(t), 16)

                    def store(t):
                        sp.wait_ge(out_scaled.sem, out_scaled.upto(t))
                        rows, place = rows_of(y_dram, t)
                        sp.dma_start(rows, place).then_inc(out_stored.sem(t), 16)

                    in_steps(sp, ET, [(1, load), (3, store)])
                    for s, v in out_stored.used(ET):
                        sp.wait_ge(s, v)

                @block.gpsimd
                def _(pool):
                    def gather(t):
                        if t.has(UNROLL):
                            pool.wait_ge(turned.sem, turned.upto(t, UNROLL))
                        pick_index(pool, t, both_picked, cur[0], src_idx)
                        pick_index(pool, t, both_picked, cur[1], dst_idx)
                        index_ready(pool, t, both_picked)
                        for side in range(2):
                            gather_rows(e[side], x_dram, cur[side], t, landed[side])

                    in_steps(pool, ET, [(0, gather)])

                @block.scalar
                def _(act):
                    def high(t):
                        act.wait_ge(turned.sem, turned.upto(t))
                        if t.has(2):
                            act.wait_ge(product_done.sem, product_done.upto(t, 2))
                        for side in range(2):
                            last = nc.scalar.activation(hi[side][:, t.half], turned_bank[side][t.half][:], ACT.Copy)
                        last.then_inc(high_done.sem, 1)

                    def copy_q(t):
                        act.wait_ge(q_product_done.sem, q_product_done.upto(t))
                        if t.has(2):
                            act.wait_ge(qk_done.sem, qk_done.upto(t, 2))
                        nc.scalar.activation(q[:, t.half, :], banks["q"][t.half][:], ACT.Copy,
                                             scale=float(FH) ** -0.5).then_inc(q_copied.sem, 1)

                    def keep(t):
                        act.wait_ge(turned.sem, turned.upto(t))
                        nc.scalar.activation(neighbours[:, bass.ds(t.times(1), 1), :, :]
                                             .rearrange("p o c e -> p (o c) e"), turned_bank[1][t.half][:], ACT.Copy)\
                            .then_inc(kept.sem, 1)

                    in_steps(act, ET, [(0, keep), (0, high), (2, copy_q)])

                @block.vector
                def _(dve):
                    def low(t):
                        dve.wait_ge(high_done.sem, high_done.upto(t))
                        if t.has(2):
                            dve.wait_ge(product_done.sem, product_done.upto(t, 2))
                        for side in range(2):
                            last = nc.vector.tensor_tensor(lo[side][:, t.half], turned_bank[side][t.half][:],
                                                           hi[side][:, t.half].bitcast(F32), ALU.subtract)
                        last.then_inc(low_done.sem, 1)

                    def score(t):
                        dve.wait_ge(product_done.sem, product_done.upto(t))
                        dve.wait_ge(q_copied.sem, q_copied.upto(t))
                        if t.has(2):
                            dve.wait_ge(scored.sem, scored.upto(t, 2))
                        nc.vector.tensor_tensor(qk[:, t.half, :], banks["k"][t.half][:], q[:, t.half, :], ALU.mult)\
                            .then_inc(qk_done.sem, 1)
                        dve.wait_ge(qk_done.sem, qk_done.upto(t))
                        nc.vector.tensor_reduce(scores[:, bass.ds(t.times(HEADS), HEADS)],
                                                qk[:, t.half, :].rearrange("p (h f) -> p h f", h=HEADS),
                                                AX_X, ALU.add).then_inc(scored.sem, 1)

                    def last_norm(t):
                        dve.wait_ge(x_landed.sem(t), x_landed.landed(t))
                        for k in range(2):
                            if isinstance(t.loop, int) and t.offset == PAIRS and k == 1:
                                dve.sem_inc(out_scaled.sem, 1)
                                continue
                            nc.vector.tensor_scalar(pair[:, t.slot, k, :], pair[:, t.slot, k, :],
                                                    last_scale[:, bass.ds(t.times(2, k), 1)], None,
                                                    ALU.mult).then_inc(out_scaled.sem, 1)

                    in_steps(dve, ET, [(0, low), (2, last_norm), (2, score)])

                @block.tensor
                def _(pe):
                    def turn(t):
                        for side in range(2):
                            pe.wait_ge(landed[side].sem(t), landed[side].landed(t))
                        if t.has(2):
                            pe.wait_ge(low_done.sem, low_done.upto(t, 2))
                            pe.wait_ge(kept.sem, kept.upto(t, 2))
                        for side in range(2):
                            for c in range(DC):
                                last = nc.tensor.transpose(turned_bank[side][t.half][:, c, :],
                                                           e[side][:, t.slot, c * P:(c + 1) * P], ident[:])
                        last.then_inc(turned.sem, 1)

                    def product(t):
                        pe.wait_ge(low_done.sem, low_done.upto(t))
                        if t.has(2):
                            pe.wait_ge(q_copied.sem, q_copied.upto(t, 2))
                            pe.wait_ge(qk_done.sem, qk_done.upto(t, 2))
                        split_product(banks["q"][t.half][:], hi[0][:, t.half], lo[0][:, t.half], Q_SLOT)\
                            .then_inc(q_product_done.sem, 1)
                        split_product(banks["k"][t.half][:], hi[1][:, t.half], lo[1][:, t.half], K_SLOT)\
                            .then_inc(product_done.sem, 1)

                    in_steps(pe, ET, [(0, turn), (1, product)])

            for count in (both_picked, turned, high_done, low_done, product_done):
                count.close(ET)
            for ring in (gathered, gathered2, x_landed, out_stored):
                ring.close(ET)
            out_scaled.close(ET)

        def softmax_terms(scores, exps, inverse):
            with ExitStack() as ph:
                by_head = sb("by_head", [HEADS, EP], F32, ph)
                penalty = sb("penalty", [HEADS, EP + 1], F32, ph)
                most = sb("most", [HEADS, EP], F32, ph)
                PER = 4
                GROUPS = ET // PER
                assert GROUPS * PER == ET
                head_bank = [pb(f"ph{k}", [HEADS, PER * P], F32, ph) for k in range(2)]
                exp_bank = pb("p_exp", [P, ET * HEADS], F32, ph)
                den_bank = pb("p_den", [P, ET * HEADS], F32, ph)
                heads_turned = sem("heads_turned")
                heads_copied = sem("heads_copied")
                penalty_made = sem("penalty_made")
                most_ahead = sem("most_ahead")
                most_of_run = sem("most_of_run")
                shifted = sem("shifted")
                exp_done = sem("exp_done")
                exps_summed = sem("exps_summed")
                terms_turned = sem("terms_turned")
                terms_copied = sem("terms_copied")
                block = ph.enter_context(nc.Block())

                def columns(n):
                    return slice(n * PER * P, (n + 1) * PER * P)

                @block.tensor
                def _(pe):
                    for done, n in enumerate(reversed(range(GROUPS))):
                        if done >= 2:
                            pe.wait_ge(heads_copied, done - 1)
                        for k in range(PER):
                            t = n * PER + k
                            last = nc.tensor.transpose(head_bank[n % 2][:, k * P:(k + 1) * P],
                                                       scores[:, t * HEADS:(t + 1) * HEADS], ident[:])
                        last.then_inc(heads_turned, 1)
                    for n in range(GROUPS):
                        pe.wait_ge(exps_summed, n + 1)
                        for bank, terms in ((exp_bank, by_head), (den_bank, most)):
                            for t in range(n * PER, (n + 1) * PER):
                                last = nc.tensor.transpose(bank[:, t * HEADS:(t + 1) * HEADS],
                                                           terms[:, t * P:(t + 1) * P], ident[0:HEADS, 0:HEADS])
                    last.then_inc(terms_turned, 1)

                @block.scalar
                def _(act):
                    for done, n in enumerate(reversed(range(GROUPS))):
                        act.wait_ge(heads_turned, done + 1)
                        nc.scalar.activation(by_head[:, columns(n)], head_bank[n % 2][:], ACT.Copy)\
                            .then_inc(heads_copied, 1)
                    for n in range(GROUPS):
                        act.wait_ge(shifted, n + 1)
                        nc.scalar.activation(by_head[:, columns(n)], by_head[:, columns(n)], ACT.Exp)\
                            .then_inc(exp_done, 1)

                @block.vector
                def _(dve):
                    nc.vector.memset(penalty[:, EP:EP + 1], -BIG)
                    nc.vector.tensor_scalar(penalty[:, 0:EP], same_run[0:HEADS, :], BIG, -BIG, ALU.mult, ALU.add)\
                        .then_inc(penalty_made, 1)
                    dve.wait_ge(penalty_made, 1)
                    for done, n in enumerate(reversed(range(GROUPS))):
                        dve.wait_ge(heads_copied, done + 1)
                        if done:
                            dve.wait_ge(most_ahead, done)
                        at = columns(n)
                        nc.vector.tensor_tensor_scan(most[:, at][:, ::-1], penalty[:, at.start + 1:at.stop + 1][:, ::-1],
                                                     by_head[:, at][:, ::-1],
                                                     most[:, at.stop:at.stop + 1] if done else 0.0,
                                                     ALU.add, ALU.max).then_inc(most_ahead, 1)
                    dve.wait_ge(most_ahead, GROUPS)

                    def whole_maximum(n):
                        at = columns(n)
                        if n:
                            dve.wait_ge(most_of_run, n)
                        nc.vector.tensor_tensor_scan(most[:, at], penalty[:, at], most[:, at],
                                                     most[:, at.start - 1:at.start] if n else 0.0,
                                                     ALU.add, ALU.max).then_inc(most_of_run, 1)

                    def shift(n):
                        at = columns(n)
                        dve.wait_ge(most_of_run, n + 1)
                        nc.vector.tensor_tensor(by_head[:, at], by_head[:, at], most[:, at], ALU.subtract)\
                            .then_inc(shifted, 1)

                    def sum_exps(n):
                        at = columns(n)
                        dve.wait_ge(exp_done, n + 1)
                        if n:
                            dve.wait_ge(exps_summed, n)
                        nc.vector.tensor_tensor_scan(most[:, at], same_run[0:HEADS, at], by_head[:, at],
                                                     most[:, at.start - 1:at.start] if n else 0.0,
                                                     ALU.mult, ALU.add).then_inc(exps_summed, 1)

                    for n in range(GROUPS + 2):
                        if n < GROUPS:
                            whole_maximum(n)
                        if n >= 2:
                            sum_exps(n - 2)
                        if n < GROUPS:
                            shift(n)
                    dve.wait_ge(terms_turned, 1)
                    nc.vector.tensor_copy(exps[:], exp_bank[:])
                    nc.vector.tensor_scalar(inverse[:], den_bank[:], 0.5, None, ALU.max).then_inc(terms_copied, 1)
                    dve.wait_ge(terms_copied, 1)
                    nc.vector.reciprocal(inverse[:], inverse[:]).then_inc(terms_copied, 1)

        def weighted_sums(neighbours, exps, inverse, x_dram, y_dram):
            with ExitStack() as ph:
                node_row = sb("node_row", [P, UNROLL, P + 1], F32, ph)
                same = sb("same", [P, UNROLL, P], F32R, ph)
                carry = sb("carry", [P, UNROLL, P], F32, ph)
                ev = sb("ev", [P, 2, D], F32, ph)
                ev_hi = sb("ev_hi", [P, 2, D], F32R, ph)
                ev_lo = sb("ev_lo", [P, 2, D], F32R, ph)
                sums = sb("sums", [P, UNROLL, D], F32, ph)
                own_rows = sb("own_rows", [P, UNROLL, D], F32, ph)
                cur_own = sb("cur_own3", [P, UNROLL], I32, ph)
                cur_last = sb("cur_last3", [P, UNROLL], I32, ph)
                hi = sb("neighbour_hi", [P, 2, DC, P], F32R, ph)
                lo = sb("neighbour_lo", [P, 2, DC, P], F32R, ph)
                y = sb("y3", [P, UNROLL, D], F32, ph)
                rows = sb("rows3", [P, UNROLL, D], F32, ph)
                junk = sb("junk3", [P, 2, D], F32, ph)
                stats = sb("stats3", [P, UNROLL, STATS], F32, ph)
                value_bank = [pb(f"p_value{k}", [P, D], F32, ph) for k in range(2)]
                sum_bank = [pb(f"p_sum{k}", [P, D], F32, ph) for k in range(2)]
                node_row_in = slots("node_row_in")
                matched = Count(sem("matched"))
                weighed = Count(sem("weighed"))
                ev_high_done = Count(sem("ev_high_done"))
                ev_low_done = Count(sem("ev_low_done"))
                own_done = Count(sem("own_done"))
                totals_done = Count(sem("totals_done"))
                totals_copied = Count(sem("totals_copied"))
                divided = Count(sem("divided"))

                def rows_free(act, t):
                    if t.has(UNROLL):
                        act.wait_ge(rows_scattered.sem(t), rows_scattered.landed(t, 1))

                def neighbour(t):
                    return neighbours[:, bass.ds(t.times(1), 1), :, :].rearrange("p o c e -> p (o c) e")

                norm = norm_steps(norm_outer, y, y_done, stats, junk, lambda t: rows[:, t.slot, :], rows_free)
                pick_last, scatter = scatter_steps(norm_outer, cur_last, rows, y_dram)
                block = ph.enter_context(nc.Block())

                @block.sync
                def _(sp):
                    def load_nodes(t):
                        if t.has(UNROLL):
                            sp.wait_ge(matched.sem, matched.upto(t, UNROLL))
                        sp.dma_start(node_row[:, t.slot, :], sorted_src_row[0, bass.ds(t.times(P), P + 1)]
                                     .partition_broadcast(P)).then_inc(node_row_in.sem(t), 16)

                    in_steps(sp, ET, [(0, load_nodes)])
                    for s, v in rows_scattered.used(ET):
                        sp.wait_ge(s, v)

                @block.gpsimd
                def _(pool):
                    def pick_own(t):
                        if t.has(UNROLL):
                            pool.wait_ge(y_done.sem, y_done.upto(t, UNROLL))
                        pick_index(pool, t, index_picked, cur_own, src_idx)

                    def gather_own(t):
                        index_ready(pool, t, index_picked)
                        gather_rows(own_rows, x_dram, cur_own, t, gathered)

                    def ev_low(t):
                        if t.has(2):
                            pool.wait_ge(own_done.sem, own_done.upto(t, 2))
                        pool.wait_ge(ev_high_done.sem, ev_high_done.upto(t))
                        nc.gpsimd.tensor_tensor(ev_lo[:, t.half, :], ev[:, t.half, :], ev_hi[:, t.half, :].bitcast(F32),
                                                ALU.subtract).then_inc(ev_low_done.sem, 1)

                    in_steps(pool, ET, [(1, ev_low), (0, pick_own), (8, lambda t: pick_last(pool, t)),
                                        (0, gather_own), (8, scatter)])

                @block.vector
                def _(dve):
                    def match(t):
                        if t.has(UNROLL):
                            dve.wait_ge(totals_done.sem, totals_done.upto(t, UNROLL))
                        dve.wait_ge(node_row_in.sem(t), node_row_in.landed(t))
                        mine = node_row[:, t.slot, 1:P + 1]
                        nc.vector.tensor_scalar(same[:, t.slot, :], mine, src_at[:, bass.ds(t.times(1), 1)], None,
                                                ALU.is_equal)
                        nc.vector.tensor_scalar(carry[:, t.slot, :], mine, node_row[:, t.slot, 0:1],
                                                ident[:, P - 1:P], ALU.is_equal, ALU.mult).then_inc(matched.sem, 1)

                    def low(t):
                        dve.wait_ge(high_done.sem, high_done.upto(t))
                        if t.has(2):
                            dve.wait_ge(product_done.sem, product_done.upto(t, 2))
                        nc.vector.tensor_tensor(lo[:, t.half], neighbour(t), hi[:, t.half].bitcast(F32),
                                                ALU.subtract).then_inc(low_done.sem, 1)

                    def weigh(t):
                        dve.wait_ge(product_done.sem, product_done.upto(t))
                        if t.has(2):
                            dve.wait_ge(ev_low_done.sem, ev_low_done.upto(t, 2))
                        terms = exps[:, bass.ds(t.times(HEADS), HEADS)].unsqueeze(2).to_broadcast([P, HEADS, FH])
                        nc.vector.tensor_tensor(ev[:, t.half, :].rearrange("p (h f) -> p h f", h=HEADS),
                                                value_bank[t.half][:].rearrange("p (h f) -> p h f", h=HEADS),
                                                terms, ALU.mult).then_inc(weighed.sem, 1)

                    def divide(t):
                        dve.wait_ge(totals_copied.sem, totals_copied.upto(t))
                        if t.has(UNROLL):
                            dve.wait_ge(norm_outer.applied.sem, norm_outer.applied.upto(t, UNROLL))
                        nc.vector.tensor_tensor(y[:, t.slot, :].rearrange("p (h f) -> p h f", h=HEADS),
                                                sums[:, t.slot, :].rearrange("p (h f) -> p h f", h=HEADS),
                                                inverse[:, bass.ds(t.times(HEADS), HEADS)].unsqueeze(2)
                                                .to_broadcast([P, HEADS, FH]), ALU.mult)\
                            .then_inc(divided.sem, 1)

                    def residual(t):
                        dve.wait_ge(divided.sem, divided.upto(t))
                        dve.wait_ge(gathered.sem(t), gathered.landed(t))
                        nc.vector.scalar_tensor_tensor(
                            y[:, t.slot, :], y[:, t.slot, :], 1.0, own_rows[:, t.slot, :], ALU.mult, ALU.add,
                            accum_out=stats[:, t.slot, SUM:SUM + 1]).then_inc(y_done.sem, 1)

                    in_steps(dve, ET, [(2, weigh), (2, match), (0, low), (6, divide), (8, norm("rstd", dve)),
                                       (6, residual), (8, norm("shift", dve)), (6, norm("mean", dve))])

                @block.tensor
                def _(pe):
                    def value(t):
                        pe.wait_ge(low_done.sem, low_done.upto(t))
                        if t.has(2):
                            pe.wait_ge(weighed.sem, weighed.upto(t, 2))
                        split_product(value_bank[t.half][:], hi[:, t.half], lo[:, t.half], V_SLOT)\
                            .then_inc(product_done.sem, 1)

                    def own(t):
                        pe.wait_ge(matched.sem, matched.upto(t))
                        pe.wait_ge(ev_low_done.sem, ev_low_done.upto(t))
                        if t.has(2):
                            pe.wait_ge(totals_copied.sem, totals_copied.upto(t, 2))
                        alone = not t.has(1)
                        nc.tensor.matmul(sum_bank[t.half][:], same[:, t.slot, :], ev_hi[:, t.half, :],
                                         start=True, stop=False)
                        nc.tensor.matmul(sum_bank[t.half][:], same[:, t.slot, :], ev_lo[:, t.half, :],
                                         start=False, stop=alone).then_inc(own_done.sem, 1)

                    def carried(t):
                        if not t.has(1):
                            pe.sem_inc(totals_done.sem, 1)
                            return
                        before = (t.slot - 1) % UNROLL
                        pe.wait_ge(totals_copied.sem, totals_copied.upto(t, 1))
                        nc.tensor.matmul(sum_bank[t.half][:], carry[:, t.slot, :], sums[:, before, :],
                                         start=False, stop=True).then_inc(totals_done.sem, 1)

                    in_steps(pe, ET, [(5, carried), (1, value), (4, own)])

                @block.scalar
                def _(act):
                    def copy_sums(t):
                        act.wait_ge(own_done.sem, own_done.upto(t))
                        act.wait_ge(totals_done.sem, totals_done.upto(t))
                        if t.has(UNROLL):
                            act.wait_ge(divided.sem, divided.upto(t, UNROLL))
                        nc.scalar.activation(sums[:, t.slot, :], sum_bank[t.half][:], ACT.Copy)\
                            .then_inc(totals_copied.sem, 1)

                    def high(t):
                        if t.has(2):
                            act.wait_ge(product_done.sem, product_done.upto(t, 2))
                        nc.scalar.activation(hi[:, t.half], neighbour(t), ACT.Copy).then_inc(high_done.sem, 1)

                    def ev_high(t):
                        act.wait_ge(weighed.sem, weighed.upto(t))
                        if t.has(2):
                            act.wait_ge(own_done.sem, own_done.upto(t, 2))
                        nc.scalar.activation(ev_hi[:, t.half, :], ev[:, t.half, :], ACT.Copy)\
                            .then_inc(ev_high_done.sem, 1)

                    in_steps(act, ET, [(0, high), (3, ev_high), (7, norm("squares", act)), (9, norm("apply", act)),
                                       (7, norm("std", act)), (5, copy_sums)])

            for count in (high_done, low_done, product_done, index_picked, y_done, last_picked):
                count.close(ET)
            gathered.close(ET)
            rows_scattered.close(ET)
            norm_outer.close(ET)

        message_layer(0, x, 0, (b_self0, b_neigh0), [(w_neigh1, 2)], [values[0]], 1, [(w_self1, 0)])
        Q_SLOT, K_SLOT, V_SLOT = 2, 0, 1
        message_layer(1, values[0], 2, (b_self1, b_neigh1), [(w_neigh2, 1)],
                      [values[1], values[2]], 0, [(w_qkv[:, 0:D], Q_SLOT)])
        with ExitStack() as ph:
            weighted_layer = edge_programs(ph, 2, values[1], 1, (), [(w_qkv[:, D:2 * D], K_SLOT)],
                                           [(w_qkv[:, 2 * D:3 * D], V_SLOT)], y_dram=values[2])
            run_block(ph, weighted_layer)
        weighted_layer[-1]()
        attention(values[2], out)


_INS = ["x", "src", "dst", "edge_weight", "L0_gnn_W_self", "L0_gnn_b_self", "L0_gnn_W_neigh", "L0_gnn_b_neigh",
        "L0_gnn_ln_gamma", "L0_gnn_ln_beta", "L1_gnn_self_w", "L1_gnn_self_b", "L1_gnn_neigh_w", "L1_gnn_neigh_b",
        "L2_gnn_weight", "L3_gnn_W"]
_TURNED = {"L0_gnn_W_self", "L0_gnn_W_neigh", "L1_gnn_self_w", "L1_gnn_neigh_w", "L2_gnn_weight"}


def kernel(**inputs):
    import numpy as np
    import concourse.bacc as bacc
    from concourse.bass_utils import run_bass_kernel_spmd

    nc = bacc.Bacc("TRN2", target_bir_lowering=False, num_devices=1)
    arrays, args = {}, []
    for name in _INS:
        a = np.asarray(inputs[name])
        a = np.ascontiguousarray(a.T if name in _TURNED else a)
        arrays[f"in_{name}"] = a
        args.append(nc.dram_tensor(f"in_{name}", a.shape, mybir.dt.from_np(a.dtype), kind="ExternalInput").ap())
    n, d = inputs["x"].shape
    out = nc.dram_tensor("out_x", [n, d], F32, kind="ExternalOutput").ap()
    build(nc, *args, out)
    result = run_bass_kernel_spmd(nc, [arrays], core_ids=[0])
    return result.results[0]["out_x"]
```
